# Optimizing a Trainium2 kernel written in Bass

```python
import numpy as np
import jax
import jax.numpy as jnp

def _softmax(x, axis=-1):
    return jax.nn.softmax(x, axis=axis)

def _gelu(x):
    return jax.nn.gelu(x, approximate=True)

def _silu(x):
    return jax.nn.silu(x)

def _sigmoid(x):
    return jax.nn.sigmoid(x)

def _layernorm(x, axis=-1, eps=1e-05):
    m = jnp.mean(x, axis=axis, keepdims=True)
    v = jnp.var(x, axis=axis, keepdims=True)
    return (x - m) / jnp.sqrt(v + eps)

def _scatter_add(tgt, idx, src, axis=0):
    return tgt.at[idx].add(src)

def _segment_sum(src, seg, n):
    return jax.ops.segment_sum(src, seg, n)
kernel_name = 'mk_gps_d1_gnn_r8_d19ee9'

def setup_inputs(seed: int=0):
    np.random.seed(seed)
    _w = jnp.asarray

    def _rec_inputs():
        import jax
        import jax.numpy as jnp
        _gk = jax.random.key(seed)
        x = -8.776e-05 + 1 * jax.random.normal(jax.random.fold_in(_gk, 1), (2500, 256), jnp.float32)
        src = jax.random.randint(jax.random.fold_in(_gk, 2), (80000,), 0, 2500, jnp.int32)
        dst = jax.random.randint(jax.random.fold_in(_gk, 3), (80000,), 0, 2500, jnp.int32)
        _o = jnp.argsort(dst, stable=True)
        src = src[_o]
        dst = dst[_o]
        edge_type_8 = jax.random.randint(jax.random.fold_in(_gk, 12), (80000,), 0, 8, jnp.int32)
        return (x, src, dst, edge_type_8)
    x, src, dst, edge_type_8 = _rec_inputs()

    def _L0_gnn_setup():
        import jax, jax.numpy as jnp
        import numpy as np
        N_NODES = 2500
        N_EDGES = 37500
        D = 256
        NUM_RELS = 8
        NUM_BASES = 4
        key = jax.random.key(seed)
        ks = jax.random.split(key, 8)
        x = jax.random.normal(ks[0], (N_NODES, D), dtype=jnp.float32)
        src = jax.random.randint(ks[1], (N_EDGES,), 0, N_NODES, dtype=jnp.int32)
        dst = jax.random.randint(ks[2], (N_EDGES,), 0, N_NODES, dtype=jnp.int32)
        etypes = jax.random.randint(ks[3], (N_EDGES,), 0, NUM_RELS, dtype=jnp.int32)
        scale = 1.0 / np.sqrt(D)
        basis = jax.random.normal(ks[4], (NUM_BASES, D, D), dtype=jnp.float32) * scale
        comp = jax.random.normal(ks[5], (NUM_RELS, NUM_BASES), dtype=jnp.float32)
        loop_weight = jax.random.normal(ks[6], (D, D), dtype=jnp.float32) * scale
        bias_param = jnp.zeros((D,), dtype=jnp.float32)
        return {'x': x, 'src': src, 'dst': dst, 'etypes': etypes, 'basis': basis, 'comp': comp, 'loop_weight': loop_weight, 'bias_param': bias_param}
    _L0_gnn_all = _L0_gnn_setup()
    _L0_gnn_in = {k: v for k, v in _L0_gnn_all.items() if k in ('basis', 'comp', 'loop_weight', 'bias_param')}
    del _L0_gnn_all

    def _L0_mix_setup():
        import jax, jax.numpy as jnp
        import numpy as np
        NUM_HEADS = 8
        key = jax.random.key(seed)
        ks = jax.random.split(key, 5)
        B, N, C = (8, 2048, 256)
        x = jax.random.normal(ks[0], (B, N, C), dtype=jnp.float32)
        Wq = jax.random.normal(ks[1], (C, C), dtype=jnp.float32) * 0.02
        Wkv = jax.random.normal(ks[2], (2 * C, C), dtype=jnp.float32) * 0.02
        Wproj = jax.random.normal(ks[3], (C, C), dtype=jnp.float32) * 0.02
        bproj = jnp.zeros((C,), dtype=jnp.float32)
        return {'x': x, 'Wq': Wq, 'Wkv': Wkv, 'Wproj': Wproj, 'bproj': bproj}
    _L0_mix_all = _L0_mix_setup()
    _L0_mix_in = {k: v for k, v in _L0_mix_all.items() if k in ('Wq', 'Wkv', 'Wproj', 'bproj')}
    del _L0_mix_all

    def _L0_ffn_setup():
        import jax, jax.numpy as jnp
        import numpy as np
        B, T, C = (64, 384, 256)
        NH, NKV = (4, 2)
        HD = C // NH
        NREP = NH // NKV
        NE, TOPK = (8, 2)
        HID = int(8 / 3 * C)
        EPS_RMS = 1e-06

        def _rope_tables(t_len):
            inv_freq = 1.0 / 10000.0 ** (np.arange(0, HD, 2, dtype=np.float32) / HD)
            t = np.arange(t_len, dtype=np.float32)
            freqs = np.outer(t, inv_freq)
            emb = np.concatenate([freqs, freqs], axis=-1)
            return (jnp.asarray(np.cos(emb)), jnp.asarray(np.sin(emb)))

        def _rotate_half(x):
            h = x.shape[-1] // 2
            return jnp.concatenate([-x[..., h:], x[..., :h]], axis=-1)

        def _rmsnorm(v, w):
            return v * jax.lax.rsqrt(jnp.mean(v * v, axis=-1, keepdims=True) + EPS_RMS) * w
        key = jax.random.key(seed)
        ks = jax.random.split(key, 10)
        s = lambda k, shape: jax.random.normal(k, shape, jnp.float32) * 0.02
        return {'x': jax.random.normal(ks[0], (B, T, C), jnp.float32), 'ln1_w': jnp.ones((C,), jnp.float32), 'ln2_w': jnp.ones((C,), jnp.float32), 'wq': s(ks[1], (NH * HD, C)), 'wk': s(ks[2], (NKV * HD, C)), 'wv': s(ks[3], (NKV * HD, C)), 'wo': s(ks[4], (C, C)), 'router_w': s(ks[5], (NE, C)), 'w1': s(ks[6], (NE, HID, C)), 'w2': s(ks[7], (NE, C, HID)), 'w3': s(ks[8], (NE, HID, C))}
    _L0_ffn_all = _L0_ffn_setup()
    _L0_ffn_in = {k: v for k, v in _L0_ffn_all.items() if k in ('ln1_w', 'ln2_w', 'wq', 'wk', 'wv', 'wo', 'router_w', 'w1', 'w2', 'w3')}
    del _L0_ffn_all
    return {'x': x, 'src': src, 'dst': dst, 'edge_type_8': edge_type_8, 'L0_gnn_basis': _L0_gnn_in['basis'], 'L0_gnn_comp': _L0_gnn_in['comp'], 'L0_gnn_loop_weight': _L0_gnn_in['loop_weight'], 'L0_gnn_bias_param': _L0_gnn_in['bias_param'], 'L0_mix_Wq': _L0_mix_in['Wq'], 'L0_mix_Wkv': _L0_mix_in['Wkv'], 'L0_mix_Wproj': _L0_mix_in['Wproj'], 'L0_mix_bproj': _L0_mix_in['bproj'], 'L0_ffn_ln1_w': _L0_ffn_in['ln1_w'], 'L0_ffn_ln2_w': _L0_ffn_in['ln2_w'], 'L0_ffn_wq': _L0_ffn_in['wq'], 'L0_ffn_wk': _L0_ffn_in['wk'], 'L0_ffn_wv': _L0_ffn_in['wv'], 'L0_ffn_wo': _L0_ffn_in['wo'], 'L0_ffn_router_w': _L0_ffn_in['router_w'], 'L0_ffn_w1': _L0_ffn_in['w1'], 'L0_ffn_w2': _L0_ffn_in['w2'], 'L0_ffn_w3': _L0_ffn_in['w3']}

def reference(x, src, dst, edge_type_8, L0_gnn_basis, L0_gnn_comp, L0_gnn_loop_weight, L0_gnn_bias_param, L0_mix_Wq, L0_mix_Wkv, L0_mix_Wproj, L0_mix_bproj, L0_ffn_ln1_w, L0_ffn_ln2_w, L0_ffn_wq, L0_ffn_wk, L0_ffn_wv, L0_ffn_wo, L0_ffn_router_w, L0_ffn_w1, L0_ffn_w2, L0_ffn_w3):
    import jax
    import jax.numpy as jnp

    def _L0_gnn_ref(x, src, dst, etypes, basis, comp, loop_weight, bias_param):
        import jax, jax.numpy as jnp
        import numpy as np
        N_NODES = 2500
        N_EDGES = 37500
        D = 256
        NUM_RELS = 8
        NUM_BASES = 4
        W = jnp.einsum('rb,bio->rio', comp, basis)
        H = jnp.einsum('ni,rio->nro', x, W)
        msg = H[src, etypes]
        agg = jax.ops.segment_sum(msg, dst, num_segments=N_NODES)
        out = agg + x @ loop_weight + bias_param
        return out

    def _L0_mix_ref(x, Wq, Wkv, Wproj, bproj):
        import jax, jax.numpy as jnp
        import numpy as np
        NUM_HEADS = 8
        B, N, C = x.shape
        h = NUM_HEADS
        d = C // h
        q = jnp.einsum('bnc,oc->bno', x, Wq).reshape(B, N, h, d).transpose(0, 2, 1, 3)
        kv = jnp.einsum('bnc,oc->bno', x, Wkv).reshape(B, N, 2, h, d)
        k = kv[:, :, 0].transpose(0, 2, 1, 3)
        v = kv[:, :, 1].transpose(0, 2, 1, 3)
        q = jax.nn.elu(q) + 1.0
        k = jax.nn.elu(k) + 1.0
        k_sum = k.sum(axis=2)
        D_inv = 1.0 / jnp.maximum(jnp.einsum('bhnd,bhd->bhn', q, k_sum), 1e-06)
        context = jnp.einsum('bhnd,bhne->bhde', k, v)
        attn = jnp.einsum('bhnd,bhde->bhne', q, context) * D_inv[..., None]
        out = attn.transpose(0, 2, 1, 3).reshape(B, N, C)
        out = jnp.einsum('bnc,oc->bno', out, Wproj) + bproj
        return out

    def _L0_ffn_ref(x, ln1_w, ln2_w, wq, wk, wv, wo, router_w, w1, w2, w3):
        import jax, jax.numpy as jnp
        import numpy as np
        B, T, C = (64, 384, 256)
        NH, NKV = (4, 2)
        HD = C // NH
        NREP = NH // NKV
        NE, TOPK = (8, 2)
        HID = int(8 / 3 * C)
        EPS_RMS = 1e-06

        def _rope_tables(t_len):
            inv_freq = 1.0 / 10000.0 ** (np.arange(0, HD, 2, dtype=np.float32) / HD)
            t = np.arange(t_len, dtype=np.float32)
            freqs = np.outer(t, inv_freq)
            emb = np.concatenate([freqs, freqs], axis=-1)
            return (jnp.asarray(np.cos(emb)), jnp.asarray(np.sin(emb)))

        def _rotate_half(x):
            h = x.shape[-1] // 2
            return jnp.concatenate([-x[..., h:], x[..., :h]], axis=-1)

        def _rmsnorm(v, w):
            return v * jax.lax.rsqrt(jnp.mean(v * v, axis=-1, keepdims=True) + EPS_RMS) * w
        Bx, Tx, Cx = x.shape
        h = _rmsnorm(x, ln1_w)
        q = (h @ wq.T).reshape(Bx, Tx, NH, HD).transpose(0, 2, 1, 3)
        k = (h @ wk.T).reshape(Bx, Tx, NKV, HD).transpose(0, 2, 1, 3)
        v = (h @ wv.T).reshape(Bx, Tx, NKV, HD).transpose(0, 2, 1, 3)
        cos, sin = _rope_tables(Tx)
        cos, sin = (cos[None, None], sin[None, None])
        q = q * cos + _rotate_half(q) * sin
        k = k * cos + _rotate_half(k) * sin
        k = jnp.repeat(k, NREP, axis=1)
        v = jnp.repeat(v, NREP, axis=1)
        scores = jnp.einsum('bhtd,bhsd->bhts', q, k) / jnp.sqrt(jnp.float32(HD))
        causal = jnp.tril(jnp.ones((Tx, Tx), dtype=bool))
        scores = jnp.where(causal[None, None], scores, jnp.float32(-1e+30))
        att = jax.nn.softmax(scores, axis=-1)
        y = jnp.einsum('bhts,bhsd->bhtd', att, v).transpose(0, 2, 1, 3).reshape(Bx, Tx, Cx)
        x = x + y @ wo.T
        flat = _rmsnorm(x, ln2_w).reshape(-1, Cx)
        probs = jax.nn.softmax(flat @ router_w.T, axis=-1)
        tp, ti = jax.lax.top_k(probs, TOPK)
        tp = tp / (jnp.sum(tp, axis=-1, keepdims=True) + 1e-09)
        weights = jnp.sum(tp[..., None] * jax.nn.one_hot(ti, NE, dtype=flat.dtype), axis=1)
        out = jnp.zeros_like(flat)
        for e in range(NE):
            hh = jax.nn.silu(flat @ w1[e].T) * (flat @ w3[e].T)
            out = out + weights[:, e:e + 1] * (hh @ w2[e].T)
        return x + out.reshape(Bx, Tx, Cx)
    xn = _layernorm(x, axis=-1)
    x = x + _L0_gnn_ref(xn, src, dst, edge_type_8, L0_gnn_basis, L0_gnn_comp, L0_gnn_loop_weight, L0_gnn_bias_param) + _L0_mix_ref(xn[None], L0_mix_Wq, L0_mix_Wkv, L0_mix_Wproj, L0_mix_bproj)[0]
    x = x + _L0_ffn_ref(_layernorm(x, axis=-1)[None], L0_ffn_ln1_w, L0_ffn_ln2_w, L0_ffn_wq, L0_ffn_wk, L0_ffn_wv, L0_ffn_wo, L0_ffn_router_w, L0_ffn_w1, L0_ffn_w2, L0_ffn_w3)[0]
    return x

_drawn_inputs = setup_inputs


def setup_inputs(seed=0):
    import zlib

    import numpy as np

    out = dict(_drawn_inputs(seed))
    spreads = {'L0_gnn_bias_param': (0.0, 0.8),
     'L0_mix_bproj': (0.0, 0.8),
     'L0_ffn_ln1_w': (1.0, 0.6),
     'L0_ffn_ln2_w': (1.0, 0.6)}
    factors = {'L0_mix_Wq': 8.0,
     'L0_mix_Wkv': 8.0,
     'L0_mix_Wproj': 8.0,
     'L0_ffn_wq': 8.0,
     'L0_ffn_wk': 8.0,
     'L0_ffn_wv': 8.0,
     'L0_ffn_wo': 8.0,
     'L0_ffn_router_w': 8.0,
     'L0_ffn_w1': 8.0,
     'L0_ffn_w2': 8.0,
     'L0_ffn_w3': 8.0}
    for name, (base, spread) in spreads.items():
        noise = np.random.default_rng([zlib.crc32(name.encode()), seed]).standard_normal(out[name].shape)
        drawn = base * np.exp(spread * noise) if base else spread * noise
        out[name] = jnp.asarray(drawn.astype(out[name].dtype))
    for name, factor in factors.items():
        out[name] = (out[name] * factor).astype(out[name].dtype)
    return out
```

```python
import math

import concourse.bass as bass
import numpy as np
from concourse import mybir
from contextlib import ExitStack

F32, F32R, I32, U32 = mybir.dt.float32, mybir.dt.float32r, mybir.dt.int32, mybir.dt.uint32
ALU, ACT, AX = mybir.AluOpType, mybir.ActivationFunctionType, mybir.AxisListType

P = 128
NODES, C, EDGES = 2500, 256, 80000
K2 = C // P
TILES = math.ceil(NODES / P)
LAST = NODES - (TILES - 1) * P
PADDED = TILES * P
RELS, BASES = 8, 4
H_COLS = RELS * C
BANK = 512
EPS_LN, EPS_RMS = 1e-5, 1e-6

COLUMNS = EDGES // P
GROUP = 5
GROUPS = COLUMNS // GROUP
RING = 5
WINDOW = 64
GENERAL_WINDOWS = PADDED // BANK

NH, NKV, HD = 4, 2, 64
NE, HID = 8, 682
"""Columns of the table of constants."""
IDENT, BLOCKS, HEADS, ROW0, DUP, MASK, MASK_T = 0, 128, 256, 260, 388, 516, 644
CONSTANTS = 772


def constants():
    t = np.zeros((P, CONSTANTS), np.float32)
    i = np.arange(P)
    t[:, IDENT:IDENT + P] = np.eye(P)
    t[:, BLOCKS:BLOCKS + P] = i[:, None] // 32 == i[None] // 32
    t[:, HEADS:HEADS + 4] = i[:, None] // 32 == np.arange(4)[None]
    t[0, ROW0:ROW0 + P] = 1
    t[:, DUP:DUP + P] = i[:, None] % HD == i[None] % HD
    t[:, MASK:MASK + P] = np.where(i[None] > i[:, None], -1e30, 0)
    t[:, MASK_T:MASK_T + P] = np.where(i[:, None] > i[None], -1e30, 0)
    return t


def rope_table():
    inv = 1.0 / 10000.0 ** (np.arange(0, HD, 2, dtype=np.float32) / HD)
    f = np.outer(np.arange(PADDED, dtype=np.float32), inv)
    emb = np.concatenate([f, f], axis=-1).T
    sign = np.where(np.arange(HD) < HD // 2, -1, 1)[:, None]
    return np.concatenate([np.cos(emb), np.sin(emb) * sign]).astype(np.float32)


class Memory:

    def __init__(self, nc, ctx, stage):
        self.nc, self.ctx, self.stage = nc, ctx, stage

    def sb(self, name, shape, dt=F32):
        return self.ctx.enter_context(self.nc.sbuf_tensor(f"{self.stage}_{name}", shape, dt))

    def ps(self, name, shape=(P, BANK)):
        return self.ctx.enter_context(self.nc.psum_tensor(f"{self.stage}_psum_{name}", list(shape), F32))

    def sem(self, name):
        return self.ctx.enter_context(self.nc.semaphore(f"{self.stage}_{name}"))


def split_product(nc, out, w_hi, w_lo, x_hi, x_lo, first, last):
    n = len(w_hi)
    for k in range(n):
        for j, (w, x) in enumerate(((w_hi[k], x_hi[k]), (w_hi[k], x_lo[k]), (w_lo[k], x_hi[k]))):
            ins = nc.tensor.matmul(out, w, x, start=first and k == 0 and j == 0, stop=last and k == n - 1 and j == 2)
    return ins


def inverse_root(nc, dve, done, count, value, root, inverse, work):
    for out, op in ((inverse, lambda o: nc.vector.reciprocal(o, root)),
                    (work, lambda o: nc.vector.tensor_tensor(o, value, inverse, ALU.mult)),
                    (work, lambda o: nc.vector.tensor_tensor(o, work, inverse, ALU.mult)),
                    (work, lambda o: nc.vector.tensor_scalar(o, work, -0.5, 1.5, ALU.mult, ALU.add)),
                    (inverse, lambda o: nc.vector.tensor_tensor(o, inverse, work, ALU.mult))):
        op(out).then_inc(done, 1)
        count += 1
        dve.wait_ge(done, count)
    return count


def stage_projections(nc, t, keep):
    with ExitStack() as ctx:
        m = Memory(nc, ctx, "proj")
        residual, q_all, context, const = keep["residual"], keep["q_all"], keep["context"], keep["const"]
        WIDE = H_COLS + 4 * C
        w_hi, w_lo = m.sb("w_hi", [P, K2, WIDE], F32R), m.sb("w_lo", [P, K2, WIDE], F32R)
        dense = m.sb("dense", [P, K2, 4 * C])
        basis = m.sb("basis", [P, K2, BASES, C])
        comp = m.sb("comp", [P, RELS * BASES])
        rel = m.sb("rel", [P, 2, K2, C])
        stats, mv = m.sb("stats", [P, TILES, 6]), m.sb("mv", [P, TILES, 2])
        std, rstd = m.sb("std", [P, TILES]), m.sb("rstd", [P, TILES])
        var_eps, work = m.sb("var_eps", [P, TILES]), m.sb("work", [P, TILES])
        xn = m.sb("xn", [P, 2, C])
        x_hi = [m.sb(f"x_hi{s}", [P, K2, P], F32R) for s in range(2)]
        x_lo = [m.sb(f"x_lo{s}", [P, K2, P], F32R) for s in range(2)]
        h_out = m.sb("h_out", [P, 2, 4, BANK])
        k_exp, q_exp = m.sb("k_exp", [P, 2, C]), m.sb("q_exp", [P, 2, C])
        k_row, v_row = m.sb("k_row", [P, 2, C]), m.sb("v_row", [P, 2, K2, P + 1])
        psum_t = [m.ps(f"t{s}") for s in range(2)]
        banks = [m.ps(f"bank{s}") for s in range(4)]
        psum_c = [m.ps(f"context{k}") for k in range(K2)]

        const_loaded, pad_zero, x_loaded = m.sem("const_loaded"), m.sem("pad_zero"), m.sem("x_loaded")
        basis_loaded, dense_loaded = m.sem("basis_loaded"), m.sem("dense_loaded")
        stats_step, std_ready = m.sem("stats_step"), m.sem("std_ready")
        mix_step, rel_split, w_hi_ready, w_lo_ready = m.sem("mix_step"), m.sem("rel_split"), m.sem("w_hi_ready"), m.sem("w_lo_ready")
        ones_ready = m.sem("ones_ready")
        xn_ready, transposed, hi_ready, lo_ready = (m.sem(n) for n in ("xn_ready", "transposed", "hi_ready", "lo_ready"))
        chunk_done, h_by_act, h_by_dve = m.sem("chunk_done"), m.sem("h_by_act"), m.sem("h_by_dve")
        h_stored = [m.sem(f"h_stored{s}") for s in range(2)]
        relu_done, k_exp_ready, q_exp_ready = m.sem("relu_done"), m.sem("k_exp_ready"), m.sem("q_exp_ready")
        kv_ready, qb_ready, context_done, context_kept = (m.sem(n) for n in ("kv_ready", "qb_ready", "context_done", "context_kept"))

        block = ctx.enter_context(nc.Block())
        PAIRS = (TILES - 2) // 2
        CHUNKS = 6

        def over_tiles(eng, tile):
            tile(0, 0, 0)
            with eng.Fori(0, PAIRS) as i:
                tile(i * 2 + 1, 1, i)
                tile(i * 2 + 2, 0, i + 1)
            tile(TILES - 1, 1, PAIRS)

        @block.sync
        def _(sp):
            sp.dma_start(residual[:, 0:TILES - 1, :], t["x"][0:(TILES - 1) * P, :].rearrange("(t p) c -> p t c", p=P)).then_inc(x_loaded, 16)
            sp.wait_ge(pad_zero, 1)
            sp.dma_start(residual[0:LAST, TILES - 1, :], t["x"][(TILES - 1) * P:NODES, :]).then_inc(x_loaded, 16)
            sp.dma_start(const[:, :], t["constants"]).then_inc(const_loaded, 16)

            def tile(n, s, use):
                sp.wait_ge(h_by_act, n * 2 + 2)
                sp.wait_ge(h_by_dve, n * 2 + 2)
                sp.dma_start(keep["h_rows"][bass.ds(n * P, P), :], h_out[:, s, :, :].rearrange("p a b -> p (a b)")).then_inc(h_stored[s], 16)

            over_tiles(sp, tile)
            for s in range(2):
                sp.wait_ge(h_stored[s], 16 * (TILES // 2))

        @block.gpsimd
        def _(pool):
            nc.gpsimd.memset(v_row[:, :, :, P:P + 1], 1.0).then_inc(ones_ready, 1)

        @block.scalar
        def _(act):
            for b in range(BASES):
                act.dma_start(basis[:, :, b, :], t["basis"][b].rearrange("(k p) o -> p k o", p=P)).then_inc(basis_loaded, 16)
            act.dma_start(comp[:, :], t["comp"].rearrange("r b -> (r b)").partition_broadcast(P)).then_inc(basis_loaded, 16)
            act.dma_start(dense[:, :, :], t["dense_T"].rearrange("(k p) o -> p k o", p=P)).then_inc(dense_loaded, 16)
            act.wait_ge(stats_step, 2 * TILES + 1)
            nc.scalar.activation(std[:, :], var_eps[:, :], ACT.Sqrt).then_inc(std_ready, 1)
            act.wait_ge(dense_loaded, 16)
            nc.scalar.activation(w_hi[:, :, H_COLS:WIDE], dense[:, :, :], ACT.Copy).then_inc(w_hi_ready, 1)
            for r in range(RELS):
                act.wait_ge(mix_step, BASES * (r + 1))
                nc.scalar.activation(w_hi[:, :, r * C:(r + 1) * C], rel[:, r % 2, :, :], ACT.Copy).then_inc(w_hi_ready, 1)

            def hi(n, s):
                act.wait_ge(transposed, n + 1)
                nc.scalar.activation(x_hi[s][:, :, :], psum_t[s][:, 0:C].rearrange("p (k c) -> p k c", k=K2), ACT.Copy).then_inc(hi_ready, 1)

            def elu_exp(bank, out, n, which, ready):
                nc.scalar.activation(out, bank, ACT.Relu, scale=-1.0).then_inc(relu_done, 1)
                act.wait_ge(relu_done, n * 2 + which)
                nc.scalar.activation(out, out, ACT.Exp, scale=-1.0).then_inc(ready, 1)

            def tile(n, s, use):
                first = isinstance(n, int) and n == 0
                last = isinstance(n, int) and n == TILES - 1
                at = 2 * s
                for j, c in enumerate((0, 2)):
                    act.wait_ge(chunk_done, n * CHUNKS + c + 1)
                    if c == 0 and not first:
                        act.wait_ge(h_stored[s], use * 16)
                    nc.scalar.activation(h_out[:, s, c, :], banks[(at + c) % 4][:, :], ACT.Copy).then_inc(h_by_act, 1)
                if not last:
                    hi(n + 1, 1 - s)
                act.wait_ge(chunk_done, n * CHUNKS + 5)
                if not first:
                    act.wait_ge(kv_ready, n - 1)
                elu_exp(banks[(at + 4) % 4][:, 0:C], k_exp[:, s, :], n, 1, k_exp_ready)
                act.wait_ge(chunk_done, n * CHUNKS + 6)
                if not first:
                    act.wait_ge(qb_ready, n - 1)
                elu_exp(banks[(at + 5) % 4][:, 0:C], q_exp[:, s, :], n, 2, q_exp_ready)

            hi(0, 0)
            over_tiles(act, tile)

        @block.tensor
        def _(pe):
            pe.wait_ge(const_loaded, 16)
            ident = const[:, IDENT:IDENT + P]

            def transposes(n, s):
                pe.wait_ge(xn_ready, n + 1)
                for k in range(K2):
                    ins = nc.tensor.transpose(psum_t[s][:, k * P:(k + 1) * P], xn[:, s, k * P:(k + 1) * P], ident)
                ins.then_inc(transposed, 1)

            def context_products(n, s, first, last):
                pe.wait_ge(kv_ready, n + 1)
                rows = LAST if last else P
                for k in range(K2):
                    ins = nc.tensor.matmul(psum_c[k][:, 0:P + 1], k_row[0:rows, s, k * P:(k + 1) * P], v_row[0:rows, s, k, :], start=first, stop=last)
                ins.then_inc(context_done, 1)

            def chunk(n, s, c):
                if not (isinstance(n, int) and n == 0 and c < 4):
                    if c in (0, 4):
                        pe.wait_ge(h_by_act, n * 2 + (c == 4))
                    elif c in (1, 5):
                        pe.wait_ge(h_by_dve, n * 2 + (c == 5))
                    else:
                        pe.wait_ge(kv_ready if c == 2 else qb_ready, n)
                cols = slice(c * BANK, (c + 1) * BANK)
                split_product(nc, banks[(2 * s + c) % 4][:, :], [x_hi[s][:, k, :] for k in range(K2)], [x_lo[s][:, k, :] for k in range(K2)],
                              [w_hi[:, k, cols] for k in range(K2)], [w_lo[:, k, cols] for k in range(K2)], True, True).then_inc(chunk_done, 1)

            def tile(n, s, use):
                first = isinstance(n, int) and n == 0
                last = isinstance(n, int) and n == TILES - 1
                pe.wait_ge(lo_ready, n + 1)
                for c in range(3):
                    chunk(n, s, c)
                if not last:
                    transposes(n + 1, 1 - s)
                if not first:
                    context_products(n - 1, 1 - s, tile.unstarted, False)
                    tile.unstarted = False
                for c in range(3, CHUNKS):
                    chunk(n, s, c)

            tile.unstarted = True
            transposes(0, 0)
            pe.wait_ge(w_hi_ready, RELS + 1)
            pe.wait_ge(w_lo_ready, RELS + 1)
            pe.wait_ge(ones_ready, 1)
            tile(0, 0, 0)
            tile(1, 1, 0)
            with pe.Fori(1, PAIRS) as i:
                tile(i * 2, 0, i)
                tile(i * 2 + 1, 1, i)
            tile(TILES - 2, 0, PAIRS)
            tile(TILES - 1, 1, PAIRS)
            context_products(TILES - 1, (TILES - 1) % 2, False, True)

        @block.vector
        def _(dve):
            nc.vector.memset(residual[:, TILES - 1, :], 0.0).then_inc(pad_zero, 1)
            dve.wait_ge(x_loaded, 32)
            for n in range(TILES):
                nc.vector.bn_stats(stats[:, n, :], residual[:, n, :]).then_inc(stats_step, 1)
            dve.wait_ge(stats_step, TILES)
            for n in range(TILES):
                nc.vector.bn_aggr(mv[:, n, :], stats[:, n, :]).then_inc(stats_step, 1)
            dve.wait_ge(stats_step, 2 * TILES)
            nc.vector.tensor_scalar(var_eps[:, :], mv[:, :, 1], EPS_LN, None, ALU.add).then_inc(stats_step, 1)
            dve.wait_ge(std_ready, 1)
            inverse_root(nc, dve, stats_step, 2 * TILES + 1, var_eps[:, :], std[:, :], rstd[:, :], work[:, :])

            def normalise(n, s):
                nc.vector.tensor_scalar(xn[:, s, :], residual[:, bass.ds(n, 1), :].rearrange("p a c -> p (a c)"), mv[:, bass.ds(n, 1), 0],
                                        rstd[:, bass.ds(n, 1)], ALU.subtract, ALU.mult).then_inc(xn_ready, 1)

            def lo(n, s):
                dve.wait_ge(hi_ready, n + 1)
                nc.vector.tensor_tensor(x_lo[s][:, :, :], psum_t[s][:, 0:C].rearrange("p (k c) -> p k c", k=K2), x_hi[s][:, :, :].bitcast(F32),
                                        ALU.subtract).then_inc(lo_ready, 1)

            normalise(0, 0)
            dve.wait_ge(w_hi_ready, 1)
            nc.vector.tensor_tensor(w_lo[:, :, H_COLS:WIDE], dense[:, :, :], w_hi[:, :, H_COLS:WIDE].bitcast(F32), ALU.subtract).then_inc(w_lo_ready, 1)
            dve.wait_ge(basis_loaded, 16 * (BASES + 1))
            for r in range(RELS):
                if r >= 2:
                    dve.wait_ge(w_lo_ready, r)
                nc.vector.tensor_scalar(rel[:, r % 2, :, :], basis[:, :, 0, :], comp[:, r * BASES:r * BASES + 1], None, ALU.mult).then_inc(mix_step, 1)
                for b in range(1, BASES):
                    dve.wait_ge(mix_step, BASES * r + b)
                    nc.vector.scalar_tensor_tensor(rel[:, r % 2, :, :], basis[:, :, b, :], comp[:, r * BASES + b:r * BASES + b + 1], rel[:, r % 2, :, :],
                                                   ALU.mult, ALU.add).then_inc(mix_step, 1)
                dve.wait_ge(mix_step, BASES * (r + 1))
                dve.wait_ge(w_hi_ready, r + 2)
                nc.vector.tensor_tensor(w_lo[:, :, r * C:(r + 1) * C], rel[:, r % 2, :, :], w_hi[:, :, r * C:(r + 1) * C].bitcast(F32),
                                        ALU.subtract).then_inc(w_lo_ready, 1)

            def tile(n, s, use):
                first = isinstance(n, int) and n == 0
                last = isinstance(n, int) and n == TILES - 1
                at = 2 * s
                if not last:
                    dve.wait_ge(transposed, n)
                    normalise(n + 1, 1 - s)
                dve.wait_ge(chunk_done, n * CHUNKS + 2)
                if not first:
                    dve.wait_ge(h_stored[s], use * 16)
                nc.vector.tensor_copy(h_out[:, s, 1, :], banks[(at + 1) % 4][:, :]).then_inc(h_by_dve, 1)
                if not last:
                    lo(n + 1, 1 - s)
                dve.wait_ge(chunk_done, n * CHUNKS + 4)
                nc.vector.tensor_copy(h_out[:, s, 3, :], banks[(at + 3) % 4][:, :]).then_inc(h_by_dve, 1)
                kv, ql = banks[(at + 4) % 4], banks[(at + 5) % 4]
                dve.wait_ge(k_exp_ready, n + 1)
                if not first:
                    dve.wait_ge(context_done, n - 1)
                nc.vector.scalar_tensor_tensor(k_row[:, s, :], kv[:, 0:C], 0.0, k_exp[:, s, :], ALU.max, ALU.add)
                nc.vector.tensor_copy(v_row[:, s, :, 0:P], kv[:, C:2 * C].rearrange("p (k c) -> p k c", k=K2)).then_inc(kv_ready, 1)
                dve.wait_ge(q_exp_ready, n + 1)
                nc.vector.scalar_tensor_tensor(q_all[:, bass.ds(n, 1), :].rearrange("p a c -> p (a c)"), ql[:, 0:C], 0.0, q_exp[:, s, :], ALU.max, ALU.add)
                row = residual[:, bass.ds(n, 1), :].rearrange("p a c -> p (a c)")
                nc.vector.tensor_tensor(row, row, ql[:, C:2 * C], ALU.add).then_inc(qb_ready, 1)

            dve.wait_ge(ones_ready, 1)
            lo(0, 0)
            over_tiles(dve, tile)
            dve.wait_ge(context_done, TILES)
            for k in range(K2):
                nc.vector.tensor_tensor(context[:, k, 0:P], psum_c[k][:, 0:P], const[:, BLOCKS:BLOCKS + P], ALU.mult)
                nc.vector.tensor_scalar(context[:, k, P:P + 4], const[:, HEADS:HEADS + 4], psum_c[k][:, P:P + 1], None, ALU.mult).then_inc(context_kept, 1)


def stage_graph(nc, t, keep):
    with ExitStack() as ctx:
        m = Memory(nc, ctx, "graph")
        residual, q_all, context, const, agg_T = keep["residual"], keep["q_all"], keep["context"], keep["const"], keep["agg_T"]
        src, dst, typ = m.sb("src", [P, COLUMNS], I32), m.sb("dst", [P, COLUMNS], I32), m.sb("typ", [P, COLUMNS], I32)
        row_index = m.sb("row_index", [P, COLUMNS], I32)
        dst_f, in_window = m.sb("dst_f", [P, COLUMNS]), m.sb("in_window", [P, COLUMNS])
        base_f = m.sb("base_f", [P, GROUPS])
        extremes, worst = m.sb("extremes", [P, 2]), m.sb("worst", [P, 2])
        outside, flag = m.sb("outside", [P, 2]), m.sb("flag", [P, 1], I32)
        iota_i, iota = m.sb("iota_i", [P, PADDED], I32), m.sb("iota", [P, PADDED])
        slots = [m.sb(f"slot{s}", [P, GROUP], I32) for s in range(RING)]
        rows = m.sb("rows", [P, RING, GROUP, C])
        hot = m.sb("hot", [P, RING, GROUP, WINDOW])
        wide_hot = m.sb("wide_hot", [P, 2, BANK])
        proj = m.sb("proj", [P, K2, C])
        q_row, q_T, den, attn, attn_T = m.sb("q_row", [P, C]), m.sb("q_T", [P, K2, P]), m.sb("den", [P, 2, 8]), m.sb("attn", [P, C]), m.sb("attn_T", [P, K2, P])
        psum = [m.ps(f"sum{s}") for s in range(RING)]
        pq, pa, pm = m.ps("q"), m.ps("attn"), m.ps("mix")

        edges_loaded, types_loaded, proj_loaded, iota_made, prep = (m.sem(n) for n in ("edges_loaded", "types_loaded", "proj_loaded", "iota_made", "prep"))
        index_ready, bases_spread, worst_found = m.sem("index_ready"), m.sem("bases_spread"), m.sem("worst_found")
        flag_ready = m.sem("flag_ready")
        slot_filled = [m.sem(f"slot_filled{s}") for s in range(RING)]
        gathered = [m.sem(f"gathered{s}") for s in range(RING)]
        gather_turns, group_used = m.sem("gather_turns"), m.sem("group_used")
        hot_ready, summed, added = m.sem("hot_ready"), m.sem("summed"), m.sem("added")
        wide_ready, wide_used, wide_summed, wide_added = (m.sem(n) for n in ("wide_ready", "wide_used", "wide_summed", "wide_added"))
        q_copied, q_turned, q_T_ready, attended, den_step, attn_ready, attn_turned, attn_T_ready, mixed, mix_added = (
            m.sem(n) for n in ("q_copied", "q_turned", "q_T_ready", "attended", "den_step", "attn_ready", "attn_turned", "attn_T_ready", "mixed", "mix_added"))

        block = ctx.enter_context(nc.Block())
        ident = const[:, IDENT:IDENT + P]

        @block.sync
        def _(sp):
            sp.dma_start(src[:, :], t["src_T"]).then_inc(edges_loaded, 16)
            sp.dma_start(typ[:, :], t["type_T"]).then_inc(edges_loaded, 16)
            sp.dma_start(dst[:, :], t["dst_T"]).then_inc(types_loaded, 16)
            sp.dma_start(proj[:, :, :], t["proj_T"].rearrange("(k p) o -> p k o", p=P)).then_inc(proj_loaded, 16)
            sp.wait_ge(index_ready, 1)

            def fill(s, group):
                sp.dma_start(slots[s][:, :], row_index[:, bass.ds(group * GROUP, GROUP)]).then_inc(slot_filled[s], 16)

            for s in range(RING):
                fill(s, s)
            with sp.Fori(1, GROUPS // RING) as i:
                for s in range(RING):
                    sp.wait_ge(gathered[s], i * (16 * GROUP))
                    fill(s, i * RING + s)

        @block.gpsimd
        def _(pool):
            nc.gpsimd.iota(iota_i[:, :], pattern=[[1, PADDED]], base=0, channel_multiplier=0).then_inc(iota_made, 1)

            def gather(s):
                for e in range(GROUP):
                    pool.indirect_dma_start(out=rows[:, s, e, :], out_offset=None, in_=keep["h_table"],
                                            in_offset=bass.IndirectOffsetOnAxis(ap=slots[s][:, e:e + 1], axis=0),
                                            bounds_check=last_row, oob_is_err=True).then_inc(gathered[s], 16)

            last_row = pool.to_reg(PADDED * RELS - 1)
            for s in range(RING):
                pool.wait_ge(slot_filled[s], 16)
                gather(s)
            pool.wait_ge(worst_found, 1)
            nc.gpsimd.partition_all_reduce(worst[:, :], extremes[:, :], P, bass.bass_isa.ReduceOp.max).then_inc(worst_found, 1)
            with pool.Fori(1, GROUPS // RING) as i:
                for s in range(RING):
                    pool.wait_ge(slot_filled[s], i * 16 + 16)
                    pool.wait_ge(group_used, i * RING + (s - RING + 1))
                    pool.sem_inc(gather_turns, 1)
                    gather(s)

        @block.scalar
        def _(act):
            def tile(n):
                act.wait_ge(q_turned, n)
                nc.scalar.activation(q_row[:, :], q_all[:, bass.ds(n, 1), :].rearrange("p a c -> p (a c)"), ACT.Copy).then_inc(q_copied, 1)
                act.wait_ge(q_turned, n + 1)
                nc.scalar.activation(q_T[:, :, :], pq[:, 0:C].rearrange("p (k c) -> p k c", k=K2), ACT.Copy).then_inc(q_T_ready, 1)
                act.wait_ge(attn_turned, n + 1)
                nc.scalar.activation(attn_T[:, :, :], pq[:, C:2 * C].rearrange("p (k c) -> p k c", k=K2), ACT.Copy).then_inc(attn_T_ready, 1)

            with act.Fori(0, TILES) as n:
                tile(n)

        @block.tensor
        def _(pe):
            pe.wait_ge(prep, 2)
            nc.tensor.matmul(psum[0][:, 0:GROUPS], const[:, ROW0:ROW0 + P], dst_f[:, :].rearrange("p (g e) -> p g e", e=GROUP)[:, :, 0],
                             start=True, stop=True).then_inc(bases_spread, 1)
            pe.wait_ge(proj_loaded, 16)
            with pe.Fori(0, TILES) as n:
                pe.wait_ge(q_copied, n + 1)
                for k in range(K2):
                    ins = nc.tensor.transpose(pq[:, k * P:(k + 1) * P], q_row[:, k * P:(k + 1) * P], ident)
                ins.then_inc(q_turned, 1)
                pe.wait_ge(q_T_ready, n + 1)
                pe.wait_ge(attn_ready, n)
                for k in range(K2):
                    ins = nc.tensor.matmul(pa[:, k * (P + 4):(k + 1) * (P + 4)], q_T[:, k, :], context[:, k, :], start=True, stop=True)
                ins.then_inc(attended, 1)
                pe.wait_ge(attn_ready, n + 1)
                for k in range(K2):
                    ins = nc.tensor.transpose(pq[:, C + k * P:C + (k + 1) * P], attn[:, k * P:(k + 1) * P], ident)
                ins.then_inc(attn_turned, 1)
                pe.wait_ge(attn_T_ready, n + 1)
                pe.wait_ge(mix_added, n)
                for k in range(K2):
                    ins = nc.tensor.matmul(pm[:, 0:C], attn_T[:, k, :], proj[:, k, :], start=k == 0, stop=k == K2 - 1)
                ins.then_inc(mixed, 1)

            pe.wait_ge(flag_ready, 1)
            scattered = pe.value_load(flag[0:1, 0:1], min_val=0, max_val=2)
            with pe.If(scattered < 1):
                with pe.Fori(0, GROUPS // RING) as i:
                    for s in range(RING):
                        pe.wait_ge(gathered[s], i * (16 * GROUP) + 16 * GROUP)
                        pe.wait_ge(hot_ready, i * RING + (s + 1))
                        for k in range(K2):
                            for e in range(GROUP):
                                ins = nc.tensor.matmul(psum[s][:, k * WINDOW:(k + 1) * WINDOW], rows[:, s, e, k * P:(k + 1) * P], hot[:, s, e, :],
                                                       start=e == 0, stop=e == GROUP - 1)
                        ins.then_inc(summed, 1)
                        pe.wait_ge(summed, i * RING + (s + 1))
                        pe.sem_inc(group_used, 1)
            with pe.Else():
                with pe.Fori(0, GROUPS // RING) as i:
                    for s in range(RING):
                        with pe.Fori(0, GENERAL_WINDOWS) as w:
                            for e in range(GROUP):
                                step = i * (RING * GENERAL_WINDOWS * GROUP) + w * GROUP + (s * GENERAL_WINDOWS * GROUP + e)
                                pe.wait_ge(wide_ready, step + 1)
                                if e == 0:
                                    pe.wait_ge(gathered[s], i * (16 * GROUP) + 16 * GROUP)
                                    pe.wait_ge(wide_added, i * (RING * GENERAL_WINDOWS) + w + s * GENERAL_WINDOWS)
                                for k in range(K2):
                                    ins = nc.tensor.matmul(psum[k][:, :], rows[:, s, e, k * P:(k + 1) * P], wide_hot[:, 0, :],
                                                           start=e == 0, stop=e == GROUP - 1)
                                ins.then_inc(wide_used, 1)
                        pe.wait_ge(wide_used, i * (RING * GENERAL_WINDOWS * GROUP) + (s + 1) * GENERAL_WINDOWS * GROUP)
                        pe.sem_inc(group_used, 1)

        @block.vector
        def _(dve):
            nc.vector.memset(agg_T[:, :, :], 0.0).then_inc(prep, 1)
            dve.wait_ge(edges_loaded, 32)
            nc.vector.scalar_tensor_tensor(row_index[:, :], src[:, :], float(RELS), typ[:, :], ALU.mult, ALU.add).then_inc(index_ready, 1)
            dve.wait_ge(types_loaded, 16)
            nc.vector.tensor_copy(dst_f[:, :], dst[:, :]).then_inc(prep, 1)
            dve.wait_ge(iota_made, 1)
            nc.vector.tensor_copy(iota[:, :], iota_i[:, :]).then_inc(prep, 1)
            dve.wait_ge(bases_spread, 1)
            nc.vector.tensor_copy(base_f[:, :], psum[0][:, 0:GROUPS]).then_inc(prep, 1)
            dve.wait_ge(prep, 4)
            nc.vector.tensor_tensor(in_window[:, :].rearrange("p (g e) -> p g e", e=GROUP), dst_f[:, :].rearrange("p (g e) -> p g e", e=GROUP),
                                    base_f[:, :].unsqueeze(2).to_broadcast([P, GROUPS, GROUP]), ALU.subtract).then_inc(prep, 1)
            dve.wait_ge(prep, 5)
            nc.vector.tensor_reduce(extremes[:, 0:1], in_window[:, :], AX.X, ALU.max)
            nc.vector.tensor_reduce(extremes[:, 1:2], in_window[:, :], AX.X, ALU.min, negate=True).then_inc(worst_found, 1)
            dve.wait_ge(worst_found, 2)
            nc.vector.tensor_scalar(outside[:, 0:1], worst[:, 0:1], float(WINDOW), None, ALU.is_ge)
            nc.vector.tensor_scalar(outside[:, 1:2], worst[:, 1:2], 0.0, None, ALU.is_gt).then_inc(prep, 1)
            dve.wait_ge(prep, 6)
            nc.vector.tensor_tensor(flag[:, :], outside[:, 0:1], outside[:, 1:2], ALU.add).then_inc(flag_ready, 1)

            with dve.Fori(0, TILES) as n:
                dve.wait_ge(attended, n + 1)
                both = pa[:, 0:2 * (P + 4)].rearrange("p (k c) -> p k c", k=K2)
                nc.vector.tensor_scalar(den[:, 0, :].rearrange("p (k c) -> p k c", k=K2), both[:, :, P:P + 4], 1e-6, None, ALU.max).then_inc(den_step, 1)
                dve.wait_ge(den_step, n * 2 + 1)
                nc.vector.reciprocal(den[:, 1, :], den[:, 0, :]).then_inc(den_step, 1)
                dve.wait_ge(den_step, n * 2 + 2)
                for k in range(K2):
                    ins = nc.vector.tensor_tensor(attn[:, k * P:(k + 1) * P].rearrange("p (h e) -> p h e", h=4), both[:, k, 0:P].rearrange("p (h e) -> p h e", h=4),
                                                  den[:, 1, 4 * k:4 * k + 4].unsqueeze(2).to_broadcast([P, 4, 32]), ALU.mult)
                ins.then_inc(attn_ready, 1)
                dve.wait_ge(mixed, n + 1)
                row = residual[:, bass.ds(n, 1), :].rearrange("p a c -> p (a c)")
                nc.vector.tensor_tensor(row, row, pm[:, 0:C], ALU.add).then_inc(mix_added, 1)

            dve.wait_ge(flag_ready, 1)
            scattered = dve.value_load(flag[0:1, 0:1], min_val=0, max_val=2)
            with dve.If(scattered < 1):
                with dve.Fori(0, GROUPS // RING) as i:
                    for s in range(RING):
                        g = i * RING + s
                        nc.vector.tensor_tensor(hot[:, s, :, :], iota[:, 0:WINDOW].unsqueeze(1).to_broadcast([P, GROUP, WINDOW]),
                                                in_window[:, bass.ds(g * GROUP, GROUP)].unsqueeze(2).to_broadcast([P, GROUP, WINDOW]),
                                                ALU.is_equal).then_inc(hot_ready, 1)
                        base = dve.value_load(dst[0:1, bass.ds(g * GROUP, 1)], min_val=0, max_val=NODES - 1)
                        dve.wait_ge(summed, g + 1)
                        dve.wait_ge(added, g)
                        place = agg_T[:, :, bass.ds(base, WINDOW)]
                        nc.vector.tensor_tensor(place, place, psum[s][:, 0:K2 * WINDOW].rearrange("p (k w) -> p k w", k=K2), ALU.add).then_inc(added, 1)
            with dve.Else():
                with dve.Fori(0, GROUPS // RING) as i:
                    for s in range(RING):
                        with dve.Fori(0, GENERAL_WINDOWS) as w:
                            for e in range(GROUP):
                                step = i * (RING * GENERAL_WINDOWS * GROUP) + w * GROUP + (s * GENERAL_WINDOWS * GROUP + e)
                                dve.wait_ge(wide_used, step)
                                nc.vector.tensor_scalar(wide_hot[:, 0, :], iota[:, bass.ds(w * BANK, BANK)],
                                                        dst_f[:, bass.ds(i * (RING * GROUP) + (s * GROUP + e), 1)], None, ALU.is_equal).then_inc(wide_ready, 1)
                            turn = i * (RING * GENERAL_WINDOWS) + w + s * GENERAL_WINDOWS
                            dve.wait_ge(wide_used, i * (RING * GENERAL_WINDOWS * GROUP) + w * GROUP + ((s * GENERAL_WINDOWS + 1) * GROUP))
                            dve.wait_ge(wide_added, turn)
                            for k in range(K2):
                                place = agg_T[:, k, bass.ds(w * BANK, BANK)]
                                ins = nc.vector.tensor_tensor(place, place, psum[k][:, :], ALU.add)
                            ins.then_inc(wide_added, 1)


def over_pairs(eng, tile, tiles=TILES):
    tile(0, 0, True)
    tile(1, 1, True)
    with eng.Fori(1, tiles // 2) as i:
        tile(i * 2, 0, False)
        tile(i * 2 + 1, 1, False)


def row_of(tensor, n):
    return tensor[:, bass.ds(n, 1), :].rearrange("p a c -> p (a c)")


def stage_sum(nc, t, keep):
    with ExitStack() as ctx:
        m = Memory(nc, ctx, "sum")
        residual, const, agg_T, mv = keep["residual"], keep["const"], keep["agg_T"], keep["mv"]
        both, bias = m.sb("biases", [P, 2, C]), m.sb("bias", [P, C])
        stats = m.sb("stats", [P, TILES, 6])
        part = [m.sb(f"part{s}", [P, K2, P]) for s in range(2)]
        psum = [m.ps(f"turned{s}") for s in range(2)]
        biases_loaded, bias_ready, part_ready, turned, agg_added, bias_added, stats_ready, mv_ready = (
            m.sem(n) for n in ("biases_loaded", "bias_ready", "part_ready", "turned", "agg_added", "bias_added", "stats_ready", "mv_ready"))
        block = ctx.enter_context(nc.Block())

        @block.sync
        def _(sp):
            sp.dma_start(both[:, :, :], t["biases"].partition_broadcast(P)).then_inc(biases_loaded, 16)

        @block.scalar
        def _(act):
            def tile(n, s, first):
                if not first:
                    act.wait_ge(turned, n - 1)
                nc.scalar.activation(part[s][:, :, :], agg_T[:, :, bass.ds(n * P, P)], ACT.Copy).then_inc(part_ready, 1)

            over_pairs(act, tile)

        @block.tensor
        def _(pe):
            def tile(n, s, first):
                pe.wait_ge(part_ready, n + 1)
                if not first:
                    pe.wait_ge(agg_added, n - 1)
                for k in range(K2):
                    ins = nc.tensor.transpose(psum[s][:, k * P:(k + 1) * P], part[s][:, k, :], const[:, IDENT:IDENT + P])
                ins.then_inc(turned, 1)

            over_pairs(pe, tile)

        @block.vector
        def _(dve):
            dve.wait_ge(biases_loaded, 16)
            nc.vector.tensor_tensor(bias[:, :], both[:, 0, :], both[:, 1, :], ALU.add).then_inc(bias_ready, 1)
            dve.wait_ge(bias_ready, 1)

            def tile(n, s, first):
                row = row_of(residual, n)
                dve.wait_ge(turned, n + 1)
                nc.vector.tensor_tensor(row, row, psum[s][:, 0:C], ALU.add).then_inc(agg_added, 1)
                dve.wait_ge(agg_added, n + 1)
                nc.vector.tensor_tensor(row, row, bias[:, :], ALU.add).then_inc(bias_added, 1)
                dve.wait_ge(bias_added, n + 1)
                nc.vector.bn_stats(row_of(stats, n), row).then_inc(stats_ready, 1)

            over_pairs(dve, tile)
            dve.wait_ge(stats_ready, TILES)
            for n in range(TILES):
                nc.vector.bn_aggr(mv[:, n, :], stats[:, n, :]).then_inc(mv_ready, 1)
            dve.wait_ge(mv_ready, TILES)


def stage_turn(nc, t, keep, router):
    with ExitStack() as ctx:
        m = Memory(nc, ctx, "route" if router else "values")
        residual, const, mv, z, h_hi, h_lo = (keep[n] for n in ("residual", "const", "mv", "z", "h_hi", "h_lo"))
        OUT = NE if router else NKV * HD
        raw_w = m.sb("raw_w", [P, K2, OUT])
        w_hi, w_lo = m.sb("w_hi", [P, K2, OUT], F32R), m.sb("w_lo", [P, K2, OUT], F32R)
        norm_w = m.sb("norm_w", [P, K2])
        std, rstd, var_eps, work = (m.sb(n, [P, TILES]) for n in ("std", "rstd", "var_eps", "work"))
        squares, mean_sq, rinv = m.sb("squares", [P, 2, C]), m.sb("mean_sq", [P, TILES]), m.sb("rinv", [P, TILES])
        h = [m.sb(f"h{s}", [P, C]) for s in range(2)]
        t_hi = [m.sb(f"t_hi{s}", [P, K2, P], F32R) for s in range(2)]
        t_lo = [m.sb(f"t_lo{s}", [P, K2, P], F32R) for s in range(2)]
        psum_t = [m.ps(f"turned{s}") for s in range(2)]
        psum_o = [m.ps(f"out{s}") for s in range(2)]
        loaded, w_hi_ready, w_lo_ready, eps_added, std_ready, rstd_ready, z_ready, squared = (
            m.sem(n) for n in ("loaded", "w_hi_ready", "w_lo_ready", "eps_added", "std_ready", "rstd_ready", "z_ready", "squared"))
        h_ready, turned, hi_ready, lo_ready, copied, product_done, product_read = (
            m.sem(n) for n in ("h_ready", "turned", "hi_ready", "lo_ready", "copied", "product_done", "product_read"))
        if router:
            logits, top, index_u = m.sb("logits", [P, TILES, NE]), m.sb("top", [P, TILES, NE]), m.sb("index_u", [P, TILES, NE], U32)
            peak, total, scale = m.sb("peak", [P, TILES]), m.sb("total", [P, TILES]), m.sb("scale", [P, TILES])
            probs, index, pair = m.sb("probs", [P, TILES, NE]), m.sb("index", [P, TILES, NE]), m.sb("pair", [P, TILES, 2])
            hit, gates = m.sb("hit", [P, 2, TILES, NE]), m.sb("gates", [P, TILES, NE])
            iota_i, iota = m.sb("iota_i", [P, NE], I32), m.sb("iota", [P, NE])
            gates_T = m.sb("gates_T", [NE, PADDED])
            psum_g = [m.ps(f"gates{s}") for s in range(4)]
            iota_made, step, exps_ready, gates_turned, gates_copied, gates_stored = (
                m.sem(n) for n in ("iota_made", "step", "exps_ready", "gates_turned", "gates_copied", "gates_stored"))
        block = ctx.enter_context(nc.Block())

        @block.sync
        def _(sp):
            sp.dma_start(raw_w[:, :, :], t["router_T" if router else "wv_T"].rearrange("(k p) o -> p k o", p=P)).then_inc(loaded, 16)
            sp.dma_start(norm_w[:, :], t["ln2_w" if router else "ln1_w"]).then_inc(loaded, 16)
            if router:
                sp.wait_ge(gates_copied, TILES // 4)
                sp.dma_start(keep["gate_rows"], gates_T[:, :]).then_inc(gates_stored, 16)
                sp.wait_ge(gates_stored, 16)

        @block.gpsimd
        def _(pool):
            if router:
                nc.gpsimd.iota(iota_i[:, :], pattern=[[1, NE]], base=0, channel_multiplier=0).then_inc(iota_made, 1)

            def tile(n, s, first):
                pool.wait_ge(lo_ready, n + 1)
                nc.gpsimd.tensor_copy(h_hi[:, :, bass.ds(n * P, P)], t_hi[s][:, :, :])
                nc.gpsimd.tensor_copy(h_lo[:, :, bass.ds(n * P, P)], t_lo[s][:, :, :]).then_inc(copied, 1)

            over_pairs(pool, tile)

        @block.scalar
        def _(act):
            act.wait_ge(loaded, 32)
            nc.scalar.activation(w_hi[:, :, :], raw_w[:, :, :], ACT.Copy).then_inc(w_hi_ready, 1)
            if not router:
                act.wait_ge(eps_added, 1)
                nc.scalar.activation(std[:, :], var_eps[:, :], ACT.Sqrt).then_inc(std_ready, 1)

            def square(n, s, first):
                if not router:
                    act.wait_ge(z_ready, n + 1)
                if not first:
                    act.wait_ge(squared, n - 1)
                nc.scalar.activation(squares[:, s, :], row_of(z, n), ACT.Square, accum_out=mean_sq[:, bass.ds(n, 1)]).then_inc(squared, 1)

            over_pairs(act, square)
            act.wait_ge(eps_added, 1 if router else 2)
            nc.scalar.activation(std[:, :], mean_sq[:, :], ACT.Sqrt).then_inc(std_ready, 1)

            def tile(n, s, first):
                act.wait_ge(turned, n + 1)
                if not first:
                    act.wait_ge(copied, n - 1)
                    act.wait_ge(product_done, n - 1)
                for k in range(K2):
                    ins = nc.scalar.activation(t_hi[s][:, k, :], psum_t[s][:, k * P:(k + 1) * P], ACT.Copy, scale=norm_w[:, k:k + 1])
                ins.then_inc(hi_ready, 1)
                if not router:
                    act.wait_ge(product_done, n + 1)
                    nc.scalar.activation(keep["v"][:, :, bass.ds(n, 1), 0:HD].rearrange("p a b c -> p a (b c)"),
                                         psum_o[s][:, 0:OUT].rearrange("p (a c) -> p a c", a=NKV), ACT.Copy).then_inc(product_read, 1)

            over_pairs(act, tile)
            if router:
                act.wait_ge(step, 2)
                nc.scalar.activation(probs[:, :, :], logits[:, :, :], ACT.Exp).then_inc(exps_ready, 1)
                for q in range(TILES // 4):
                    act.wait_ge(gates_turned, q + 1)
                    nc.scalar.activation(gates_T[:, q * BANK:(q + 1) * BANK], psum_g[q % 4][0:NE, :], ACT.Copy).then_inc(gates_copied, 1)

        @block.tensor
        def _(pe):
            ident = const[:, IDENT:IDENT + P]
            pe.wait_ge(w_lo_ready, 1)

            def tile(n, s, first):
                pe.wait_ge(h_ready, n + 1)
                if not first:
                    pe.wait_ge(lo_ready, n - 1)
                for k in range(K2):
                    ins = nc.tensor.transpose(psum_t[s][:, k * P:(k + 1) * P], h[s][:, k * P:(k + 1) * P], ident)
                ins.then_inc(turned, 1)
                pe.wait_ge(lo_ready, n + 1)
                if not first:
                    pe.wait_ge(product_read, n - 1)
                split_product(nc, psum_o[s][:, 0:OUT], [t_hi[s][:, k, :] for k in range(K2)], [t_lo[s][:, k, :] for k in range(K2)],
                              [w_hi[:, k, :] for k in range(K2)], [w_lo[:, k, :] for k in range(K2)], True, True).then_inc(product_done, 1)

            over_pairs(pe, tile)
            if router:
                pe.wait_ge(step, 15)
                for n in range(TILES):
                    if n >= 16 and n % 4 == 0:
                        pe.wait_ge(gates_copied, n // 4 - 3)
                    ins = nc.tensor.transpose(psum_g[n // 4 % 4][0:NE, n % 4 * P:(n % 4 + 1) * P], gates[:, n, :], ident)
                    if n % 4 == 3:
                        ins.then_inc(gates_turned, 1)

        @block.vector
        def _(dve):
            dve.wait_ge(w_hi_ready, 1)
            nc.vector.tensor_tensor(w_lo[:, :, :], raw_w[:, :, :], w_hi[:, :, :].bitcast(F32), ALU.subtract).then_inc(w_lo_ready, 1)
            if not router:
                nc.vector.memset(keep["v"][:, :, :, HD:HD + 1], 1.0)
                nc.vector.tensor_scalar(var_eps[:, :], mv[:, :, 1], EPS_LN, None, ALU.add).then_inc(eps_added, 1)
                dve.wait_ge(std_ready, 1)
                steps = inverse_root(nc, dve, rstd_ready, 0, var_eps[:, :], std[:, :], rstd[:, :], work[:, :])
                with dve.Fori(0, TILES) as n:
                    nc.vector.tensor_scalar(row_of(z, n), row_of(residual, n), mv[:, bass.ds(n, 1), 0], rstd[:, bass.ds(n, 1)],
                                            ALU.subtract, ALU.mult).then_inc(z_ready, 1)
            else:
                nc.vector.tensor_tensor(residual[:, :, :], residual[:, :, :], z[:, :, :], ALU.add).then_inc(z_ready, 1)
            dve.wait_ge(squared, TILES)
            nc.vector.tensor_scalar(mean_sq[:, :], mean_sq[:, :], 1.0 / C, EPS_RMS, ALU.mult, ALU.add).then_inc(eps_added, 1)
            dve.wait_ge(std_ready, 1 if router else 2)
            inverse_root(nc, dve, rstd_ready, 0 if router else steps, mean_sq[:, :], std[:, :], rinv[:, :], work[:, :])

            def tile(n, s, first):
                if not first:
                    dve.wait_ge(turned, n - 1)
                nc.vector.tensor_scalar(h[s][:, :], row_of(z, n), rinv[:, bass.ds(n, 1)], None, ALU.mult).then_inc(h_ready, 1)
                dve.wait_ge(hi_ready, n + 1)
                for k in range(K2):
                    ins = nc.vector.scalar_tensor_tensor(t_lo[s][:, k, :], psum_t[s][:, k * P:(k + 1) * P], norm_w[:, k:k + 1], t_hi[s][:, k, :].bitcast(F32),
                                                         ALU.mult, ALU.subtract)
                ins.then_inc(lo_ready, 1)
                if router:
                    dve.wait_ge(product_done, n + 1)
                    nc.vector.tensor_copy(row_of(logits, n), psum_o[s][:, 0:NE]).then_inc(product_read, 1)

            over_pairs(dve, tile)
            if router:
                done = [0]

                def then(ins):
                    done[0] += 1
                    ins.then_inc(step, 1)
                    dve.wait_ge(step, done[0])

                def spread(rows):
                    return rows.unsqueeze(2).to_broadcast([P, TILES, NE])

                dve.wait_ge(product_read, TILES)
                then(nc.vector.tensor_reduce(peak[:, :], logits[:, :, :], AX.X, ALU.max))
                then(nc.vector.tensor_tensor(logits[:, :, :], logits[:, :, :], spread(peak[:, :]), ALU.subtract))
                dve.wait_ge(exps_ready, 1)
                then(nc.vector.tensor_reduce(total[:, :], probs[:, :, :], AX.X, ALU.add))
                then(nc.vector.reciprocal(scale[:, :], total[:, :]))
                then(nc.vector.tensor_tensor(probs[:, :, :], probs[:, :, :], spread(scale[:, :]), ALU.mult))
                for n in range(TILES):
                    ins = nc.vector.max(top[:, n, :], probs[:, n, :])
                then(ins)
                for n in range(TILES):
                    ins = nc.vector.max_index(index_u[:, n, :], top[:, n, :], probs[:, n, :])
                then(ins)
                dve.wait_ge(iota_made, 1)
                nc.vector.tensor_copy(iota[:, :], iota_i[:, :])
                nc.vector.tensor_copy(index[:, :, :], index_u[:, :, :])
                then(nc.vector.tensor_tensor(total[:, :], top[:, :, 0], top[:, :, 1], ALU.add))
                then(nc.vector.tensor_scalar(total[:, :], total[:, :], 1e-9, None, ALU.add))
                then(nc.vector.reciprocal(scale[:, :], total[:, :]))
                then(nc.vector.tensor_tensor(pair[:, :, :], top[:, :, 0:2], scale[:, :].unsqueeze(2).to_broadcast([P, TILES, 2]), ALU.mult))
                for j in range(2):
                    ins = nc.vector.tensor_tensor(hit[:, j, :, :], spread(index[:, :, j]), iota[:, :].unsqueeze(1).to_broadcast([P, TILES, NE]), ALU.is_equal)
                then(ins)
                then(nc.vector.tensor_tensor(hit[:, 0, :, :], hit[:, 0, :, :], spread(pair[:, :, 0]), ALU.mult))
                then(nc.vector.tensor_tensor(hit[:, 1, :, :], hit[:, 1, :, :], spread(pair[:, :, 1]), ALU.mult))
                then(nc.vector.tensor_tensor(gates[:, :, :], hit[:, 0, :, :], hit[:, 1, :, :], ALU.add))
                assert done[0] == 15


SPAN = BANK // P
SPANS = TILES // SPAN


def attention_order():
    def maxima(j):
        return [("maxima", j, r, c) for r in range(SPAN) for c in range(j + 1)]

    order = maxima(0) + [("turn", 0)]
    before = None
    b = 0
    for j in range(SPANS):
        steps = SPAN * (j + 1)
        ahead = maxima(j + 1) if j + 1 < SPANS else []
        taken = 0
        for i in range(steps):
            order.append(("scores", b, j, i))
            if before:
                order.append(("values",) + before)
            if i == 0 and j:
                order.append(("keep", j - 1))
            if i == 1 and j:
                order.append(("out", j - 1))
            share = min(len(ahead), -(-len(ahead) * (i + 1) // max(1, steps - 2)))
            order += ahead[taken:share]
            taken = share
            if i == steps - 2 and ahead:
                order.append(("turn", j + 1))
            before = (b, j, i)
            b += 1
    return order + [("values",) + before, ("keep", SPANS - 1), ("out", SPANS - 1)]


def stage_attention(nc, t, keep):
    with ExitStack() as ctx:
        m = Memory(nc, ctx, "att")
        const, z, h_hi, h_lo = (keep[n] for n in ("const", "z", "h_hi", "h_lo"))
        rope = m.sb("rope", [P, PADDED])
        raw_w = m.sb("raw_w", [P, K2, P])
        w_hi, w_lo = m.sb("w_hi", [P, K2, P], F32R), m.sb("w_lo", [P, K2, P], F32R)
        rotated = m.sb("rotated", [P, 2, BANK])
        q_both, k_hi = m.sb("q_both", [P, PADDED], F32R), m.sb("k_hi", [P, PADDED], F32R)
        q_max, k_lo = m.sb("q_max", [HD + 2, PADDED], F32R), m.sb("k_lo", [HD + 2, PADDED], F32R)
        v = m.sb("v", [P, TILES, HD + 1])
        wo = m.sb("wo", [HD + 1, C + 1])
        probs = m.sb("probs", [P, 3, BANK])
        y_T = m.sb("y_T", [HD + 1, BANK])
        neg = m.sb("neg", [P, 2, SPAN, SPANS])
        neg_max, neg_hi = m.sb("neg_max", [P, SPAN]), m.sb("neg_hi", [P, SPAN], F32R)
        columns = m.sb("columns", [P, SPAN, P])
        inverse = m.sb("inverse", [P, 2])
        ident_r, mask, mask_T = m.sb("ident_r", [P, P], F32R), m.sb("mask", [P, P], F32R), m.sb("mask_T", [P, P], F32R)
        p_max = [m.ps(f"max{s}") for s in range(2)]
        p_score = [m.ps(f"score{s}") for s in range(2)]
        p_y, p_out = m.ps("y"), m.ps("o")
        p_a, p_b = m.ps("a"), m.ps("b")
        outs = (p_out, p_a)

        rope_loaded, raw_loaded, v_loaded, wo_loaded, ready, cleared = (
            m.sem(n) for n in ("rope_loaded", "raw_loaded", "v_loaded", "wo_loaded", "ready", "cleared"))
        w_hi_ready, w_lo_ready, projected, rotated_ready, doubled, part_hi, part_lo = (
            m.sem(n) for n in ("w_hi_ready", "w_lo_ready", "projected", "rotated_ready", "doubled", "part_hi", "part_lo"))
        max_done, max_free, max_step, turned, maxima_ready = (m.sem(n) for n in ("max_done", "max_free", "max_step", "turned", "maxima_ready"))
        score_done, score_free, probs_free, y_ready, out_done, out_step, out_free = (
            m.sem(n) for n in ("score_done", "score_free", "probs_free", "y_ready", "out_done", "out_step", "out_free"))
        block = ctx.enter_context(nc.Block())
        ORDER = attention_order()
        STEPS = sum(o[0] == "scores" for o in ORDER)
        PER_KV = NH // NKV
        PROJECTIONS = 1 + PER_KV
        COMBINE = 4

        def first_step(j):
            return SPAN * j * (j + 1) // 2

        def over_heads(eng, key, head):
            with eng.Fori(0, NKV) as kv:
                key(kv, kv * PROJECTIONS)
                with eng.Fori(0, PER_KV) as r:
                    head(kv * PER_KV + r, kv, kv * PROJECTIONS + r + 1)

        @block.sync
        def _(sp):
            sp.dma_start(rope[:, :], t["rope"]).then_inc(rope_loaded, 16)
            sp.wait_ge(cleared, 3)

            def load(number):
                sp.wait_ge(w_lo_ready, number)
                sp.dma_start(raw_w[:, :, :], t["wqk_T"][bass.ds(number, 1)].rearrange("g (k p) n -> p (g k) n", p=P)).then_inc(raw_loaded, 16)

            def key(kv, number):
                load(number)
                sp.wait_ge(probs_free, kv * (PER_KV * STEPS) + 3)
                sp.dma_start(v[:, :, :], keep["v"][:, bass.ds(kv, 1)].rearrange("p a b c -> p (a b) c")).then_inc(v_loaded, 16)

            def head(h, kv, number):
                load(number)
                sp.wait_ge(out_done, h * TILES)
                sp.dma_start(wo[0:HD, 0:C], t["wo_T"][bass.ds(h, 1)].rearrange("g d c -> (g d) c")).then_inc(wo_loaded, 16)

            over_heads(sp, key, head)

        @block.scalar
        def _(act):
            act.sem_inc(score_free, 2)
            act.wait_ge(rope_loaded, 16)
            nc.scalar.activation(mask[:, :], const[:, MASK:MASK + P], ACT.Copy)
            nc.scalar.activation(mask_T[:, :], const[:, MASK_T:MASK_T + P], ACT.Copy)
            nc.scalar.activation(ident_r[:, :], const[:, IDENT:IDENT + P], ACT.Copy).then_inc(ready, 1)

            def projection(number, scale, outputs):
                act.wait_ge(raw_loaded, number * 16 + 16)
                act.wait_ge(projected, number * SPANS)
                nc.scalar.activation(w_hi[:, :, :], raw_w[:, :, :], ACT.Copy).then_inc(w_hi_ready, 1)
                for j in range(SPANS):
                    act.wait_ge(doubled, number * SPANS + (j + 1))
                    for out in outputs:
                        rows = out.shape[0] if out.shape[0] == P else HD
                        ins = nc.scalar.activation(out[0:rows, j * BANK:(j + 1) * BANK], p_b[0:rows, :], ACT.Copy, scale=scale)
                    ins.then_inc(part_hi, 1)

            def key(kv, number):
                projection(number, 1.0, [k_hi])

            def head(h, kv, number):
                projection(number, HD ** -0.5, [q_both, q_max])
                for what, *at in ORDER:
                    if what == "scores":
                        b, j, i = at
                        start = max(0, i - SPAN * j) * P
                        act.wait_ge(score_done, h * STEPS + (b + 1))
                        act.wait_ge(probs_free, h * STEPS + (b + 1))
                        nc.scalar.activation(probs[:, b % 3, start:BANK], p_score[b % 2][:, start:BANK], ACT.Exp).then_inc(score_free, 1)
                    elif what == "turn":
                        j, = at
                        act.wait_ge(turned, h * SPANS + (j + 1))
                        nc.scalar.activation(q_max[HD:HD + 2, j * BANK:(j + 1) * BANK], p_b[HD:HD + 2, :], ACT.Copy).then_inc(maxima_ready, 1)
                    elif what == "keep":
                        j, = at
                        act.wait_ge(probs_free, h * STEPS + (first_step(j + 1) + 3))
                        act.wait_ge(out_done, h * TILES + SPAN * j)
                        nc.scalar.activation(y_T[:, :], p_y[0:HD + 1, :], ACT.Copy).then_inc(y_ready, 1)

            over_heads(act, key, head)

        @block.tensor
        def _(pe):
            pe.sem_inc(probs_free, 3)
            pe.wait_ge(ready, 1)
            pe.wait_ge(cleared, 3)

            def project(number, j):
                pe.wait_ge(rotated_ready, number * SPANS + j)
                x = slice(j * BANK, (j + 1) * BANK)
                split_product(nc, p_a[:, :], [w_hi[:, k, :] for k in range(K2)], [w_lo[:, k, :] for k in range(K2)],
                              [h_hi[:, k, x] for k in range(K2)], [h_lo[:, k, x] for k in range(K2)], True, True).then_inc(projected, 1)

            def projection(number):
                pe.wait_ge(w_lo_ready, number + 1)
                project(number, 0)
                for j in range(SPANS):
                    if j + 1 < SPANS:
                        project(number, j + 1)
                    pe.wait_ge(rotated_ready, number * SPANS + (j + 1))
                    pe.wait_ge(part_lo, number * SPANS + j)
                    nc.tensor.matmul(p_b[:, :], const[:, DUP:DUP + P], rotated[:, j % 2, :], start=True, stop=True).then_inc(doubled, 1)

            def key(kv, number):
                pe.wait_ge(out_free, kv * (PER_KV * TILES) + 2)
                projection(number)

            def head(h, kv, number):
                pe.wait_ge(out_free, h * TILES + 2)
                projection(number)
                pe.wait_ge(part_lo, number * SPANS + SPANS)
                pe.wait_ge(wo_loaded, h * 16 + 16)
                pe.wait_ge(v_loaded, kv * 16 + 16)
                a = 0
                for what, *at in ORDER:
                    if what == "maxima":
                        j, r, c = at
                        width = BANK if c < j else (r + 1) * P
                        pe.wait_ge(max_free, h * STEPS + (a + 1))
                        tile = slice((SPAN * j + r) * P, (SPAN * j + r + 1) * P)
                        ins = nc.tensor.matmul(p_max[a % 2][:, 0:width], q_both[:, tile], k_hi[:, c * BANK:c * BANK + width], start=True, stop=c < j, skip_group_check=True)
                        if c == j:
                            ins = nc.tensor.matmul(p_max[a % 2][:, width - P:width], ident_r[:, :], mask[:, :], start=False, stop=True, skip_group_check=True)
                        ins.then_inc(max_done, 1)
                        a += 1
                    elif what == "turn":
                        j, = at
                        pe.wait_ge(max_step, h * (SPANS * COMBINE) + (j + 1) * COMBINE)
                        pe.wait_ge(maxima_ready, h * SPANS + j)
                        for r in range(SPAN):
                            ins = nc.tensor.transpose(p_b[:, r * P:(r + 1) * P], columns[:, r, :], const[:, IDENT:IDENT + P])
                        ins.then_inc(turned, 1)
                    elif what == "scores":
                        b, j, i = at
                        start = max(0, i - SPAN * j) * P
                        if i == 0:
                            pe.wait_ge(maxima_ready, h * SPANS + (j + 1))
                        pe.wait_ge(score_free, h * STEPS + (b + 1))
                        out, keys, queries = p_score[b % 2][:, start:BANK], slice(i * P, (i + 1) * P), slice(j * BANK + start, (j + 1) * BANK)
                        diagonal = i >= SPAN * j
                        nc.tensor.matmul(out, k_hi[:, keys], q_both[:, queries], start=True, stop=False, skip_group_check=True)
                        ins = nc.tensor.matmul(out, k_lo[:, keys], q_max[:, queries], start=False, stop=not diagonal, skip_group_check=True)
                        if diagonal:
                            ins = nc.tensor.matmul(p_score[b % 2][:, start:start + P], ident_r[:, :], mask_T[:, :], start=False, stop=True, skip_group_check=True)
                        ins.then_inc(score_done, 1)
                    elif what == "values":
                        b, j, i = at
                        start = max(0, i - SPAN * j) * P
                        pe.wait_ge(score_free, h * STEPS + (b + 3))
                        if i == 0:
                            pe.wait_ge(y_ready, h * SPANS + j)
                        nc.tensor.matmul(p_y[0:HD + 1, start:BANK], v[:, i, :], probs[:, b % 3, start:BANK], start=i == 0,
                                         stop=i == SPAN * (j + 1) - 1).then_inc(probs_free, 1)
                    elif what == "out":
                        j, = at
                        pe.wait_ge(y_ready, h * SPANS + (j + 1))
                        for r in range(SPAN):
                            n = SPAN * j + r
                            pe.wait_ge(out_free, h * TILES + (n + 1))
                            nc.tensor.matmul(outs[r % 2][:, 0:C + 1], y_T[:, r * P:(r + 1) * P], wo[:, :], start=True, stop=True).then_inc(out_done, 1)

            over_heads(pe, key, head)

        @block.vector
        def _(dve):
            dve.sem_inc(max_free, 2)
            dve.sem_inc(out_free, 2)
            nc.vector.memset(columns[:, :, :], 0.0).then_inc(cleared, 1)
            nc.vector.memset(wo[:, :], 0.0)
            nc.vector.memset(k_lo[HD:HD + 2, :].bitcast(F32), 1.0).then_inc(cleared, 1)
            dve.wait_ge(cleared, 2)
            nc.vector.memset(wo[HD:HD + 1, C:C + 1], 1.0).then_inc(cleared, 1)
            dve.wait_ge(rope_loaded, 16)

            def projection(number, scale):
                dve.wait_ge(w_hi_ready, number + 1)
                nc.vector.tensor_tensor(w_lo[:, :, :], raw_w[:, :, :], w_hi[:, :, :].bitcast(F32), ALU.subtract).then_inc(w_lo_ready, 1)

                def rotate(j):
                    dve.wait_ge(projected, number * SPANS + (j + 1))
                    if j >= 2:
                        dve.wait_ge(doubled, number * SPANS + (j - 1))
                    nc.vector.tensor_tensor(rotated[:, j % 2, :], p_a[:, :], rope[:, j * BANK:(j + 1) * BANK], ALU.mult).then_inc(rotated_ready, 1)

                rotate(0)
                for j in range(SPANS):
                    if j + 1 < SPANS:
                        rotate(j + 1)
                    x = slice(j * BANK, (j + 1) * BANK)
                    dve.wait_ge(part_hi, number * SPANS + (j + 1))
                    if scale is None:
                        ins = nc.vector.tensor_tensor(k_lo[0:HD, x], p_b[0:HD, :], k_hi[0:HD, x].bitcast(F32), ALU.subtract)
                    else:
                        ins = nc.vector.scalar_tensor_tensor(q_both[HD:P, x], p_b[HD:P, :], scale, q_both[HD:P, x].bitcast(F32), ALU.mult, ALU.subtract)
                    ins.then_inc(part_lo, 1)

            def head(h, kv, number):
                projection(number, HD ** -0.5)
                a = 0
                for what, *at in ORDER:
                    if what == "maxima":
                        j, r, c = at
                        width = BANK if c < j else (r + 1) * P
                        dve.wait_ge(max_done, h * STEPS + (a + 1))
                        nc.vector.tensor_reduce(neg[:, j % 2, r, c:c + 1], p_max[a % 2][:, 0:width], AX.X, ALU.max, negate=True).then_inc(max_free, 1)
                        a += 1
                    elif what == "turn":
                        j, = at
                        done = h * (SPANS * COMBINE) + j * COMBINE
                        dve.wait_ge(max_free, h * STEPS + (a + 2))
                        nc.vector.tensor_reduce(neg_max[:, :], neg[:, j % 2, :, 0:j + 1], AX.X, ALU.min).then_inc(max_step, 1)
                        dve.wait_ge(max_step, done + 1)
                        nc.vector.tensor_copy(neg_hi[:, :], neg_max[:, :]).then_inc(max_step, 1)
                        dve.wait_ge(max_step, done + 2)
                        dve.wait_ge(turned, h * SPANS + j)
                        nc.vector.tensor_copy(columns[:, :, HD], neg_hi[:, :].bitcast(F32)).then_inc(max_step, 1)
                        nc.vector.tensor_tensor(columns[:, :, HD + 1], neg_max[:, :], neg_hi[:, :].bitcast(F32), ALU.subtract).then_inc(max_step, 1)
                    elif what == "out":
                        j, = at
                        for r in range(SPAN):
                            n = SPAN * j + r
                            dve.wait_ge(out_done, h * TILES + (n + 1))
                            nc.vector.reciprocal(inverse[:, r % 2:r % 2 + 1], outs[r % 2][:, C:C + 1]).then_inc(out_step, 1)
                            dve.wait_ge(out_step, h * TILES + (n + 1))
                            nc.vector.scalar_tensor_tensor(z[:, n, :], outs[r % 2][:, 0:C], inverse[:, r % 2:r % 2 + 1], z[:, n, :], ALU.mult, ALU.add).then_inc(out_free, 1)

            over_heads(dve, lambda kv, number: projection(number, None), head)


CHUNKS = HID // P
REST = HID - CHUNKS * P
REST_SHARE = P // REST
REST_GROUPS = math.ceil(NE / REST_SHARE)
TOKENS = 500
ROUNDS = NODES // TOKENS
GROUP_STEPS = ROUNDS * CHUNKS


def stage_experts(nc, t, keep):
    with ExitStack() as ctx:
        m = Memory(nc, ctx, "experts")
        h_hi, h_lo, acc_T = keep["h_hi"], keep["h_lo"], keep["acc_T"]
        raw_up, raw_down = m.sb("raw_up", [P, 2, K2, CHUNKS * P]), m.sb("raw_down", [P, CHUNKS, C])
        up_hi, up_lo = ([m.sb(f"up_{x}{s}", [P, 2, K2, CHUNKS * P], F32R) for s in range(2)] for x in ("hi", "lo"))
        down_hi, down_lo = ([m.sb(f"down_{x}{s}", [P, CHUNKS, C], F32R) for s in range(2)] for x in ("hi", "lo"))
        gate = m.sb("gate", [P, 2, NODES])
        hidden = m.sb("hidden", [P, 3, TOKENS])
        hid_hi, hid_lo = m.sb("hid_hi", [P, CHUNKS, TOKENS], F32R), m.sb("hid_lo", [P, CHUNKS, TOKENS], F32R)
        psum_1, psum_3 = [m.ps(f"one{s}") for s in range(3)], [m.ps(f"three{s}") for s in range(3)]
        psum_o = [m.ps(f"out{k}") for k in range(K2)]
        raw_loaded, split_turns, split_hi, weights_ready, acc_zero = (m.sem(n) for n in ("raw_loaded", "split_turns", "split_hi", "weights_ready", "acc_zero"))
        gates_loaded = [m.sem(f"gates_loaded{s}") for s in range(2)]
        one_done, three_done, silu_done, multiplied, gated, hi_done, lo_done, down_done, round_done, acc_added = (
            m.sem(n) for n in ("one_done", "three_done", "silu_done", "multiplied", "gated", "hi_done", "lo_done", "down_done", "round_done", "acc_added"))
        block = ctx.enter_context(nc.Block())
        TAIL = REST_GROUPS * ROUNDS
        MAIN = NE * GROUP_STEPS

        def over_groups(eng, group, tail):
            group(0, 0, 0)
            with eng.Fori(0, (NE - 2) // 2) as i:
                group(i * 2 + 1, 1, i)
                group(i * 2 + 2, 0, i + 1)
            group(NE - 1, 1, NE // 2 - 1)
            tail()

        def over_rounds(eng, g, round_):
            round_(g, g * GROUP_STEPS, 0, 0)
            with eng.Fori(1, ROUNDS) as r:
                round_(g, g * GROUP_STEPS + r * CHUNKS, r * TOKENS, r)

        def steps_of_tail():
            for n in range(TAIL):
                yield n, MAIN + n, n % CHUNKS, (n // ROUNDS) % 2, n % ROUNDS * TOKENS

        @block.sync
        def _(sp):
            def load(g, s, uses):
                if not (isinstance(g, int) and g == 0):
                    sp.wait_ge(weights_ready, g)
                for w in range(2):
                    sp.dma_start(raw_up[:, w, :, :], t["up_T"][bass.ds(g, 1), w].rearrange("g (k p) n -> p (g k) n", p=P)).then_inc(raw_loaded, 16)
                sp.dma_start(raw_down[:, :, :], t["down_T"][bass.ds(g, 1)].rearrange("g (k p) n -> p (g k) n", p=P)).then_inc(raw_loaded, 16)
                if not (isinstance(g, int) and g <= 1):
                    sp.wait_ge(gated, (g - 1) * GROUP_STEPS)
                sp.dma_start(gate[:, s, :], keep["gate_rows"][bass.ds(g, 1), 0:NODES].rearrange("a n -> (a n)").partition_broadcast(P)).then_inc(gates_loaded[s], 16)

            def tail():
                for j in range(REST_GROUPS):
                    g, s = NE + j, j % 2
                    sp.wait_ge(weights_ready, g)
                    for w in range(2):
                        sp.dma_start(raw_up[:, w, :, 0:P], t["rest_up_T"][j, w].rearrange("(k p) n -> p k n", p=P)).then_inc(raw_loaded, 16)
                    sp.dma_start(raw_down[:, 0, :], t["rest_down_T"][j]).then_inc(raw_loaded, 16)
                    sp.wait_ge(gated, (NE - 1) * GROUP_STEPS if j == 0 else MAIN + (j - 1) * ROUNDS)
                    for e in range(REST_SHARE):
                        top = P if e == REST_SHARE - 1 else (e + 1) * REST
                        expert = min(j * REST_SHARE + e, NE - 1)
                        sp.dma_start(gate[e * REST:top, s, :], keep["gate_rows"][expert, 0:NODES].partition_broadcast(top - e * REST)).then_inc(gates_loaded[s], 16)

            over_groups(sp, load, tail)

        @block.gpsimd
        def _(pool):
            def split(g, s, chunks):
                pool.wait_ge(raw_loaded, g * 48 + 48)
                if not (isinstance(g, int) and g <= 1):
                    pool.wait_ge(down_done, (g - 1) * GROUP_STEPS if not isinstance(g, int) or g <= NE else MAIN + (g - NE - 1) * ROUNDS)
                pool.sem_inc(split_turns, 1)
                cols = slice(0, chunks * P)
                nc.gpsimd.tensor_copy(up_hi[s][:, :, :, cols], raw_up[:, :, :, cols])
                nc.gpsimd.tensor_copy(down_hi[s][:, 0:chunks, :], raw_down[:, 0:chunks, :]).then_inc(split_hi, 1)
                pool.wait_ge(split_hi, g + 1)
                for w in range(2):
                    nc.gpsimd.tensor_tensor(up_lo[s][:, w, :, cols], raw_up[:, w, :, cols], up_hi[s][:, w, :, cols].bitcast(F32), ALU.subtract)
                nc.gpsimd.tensor_tensor(down_lo[s][:, 0:chunks, :], raw_down[:, 0:chunks, :], down_hi[s][:, 0:chunks, :].bitcast(F32),
                                        ALU.subtract).then_inc(weights_ready, 1)

            def tail():
                for j in range(REST_GROUPS):
                    split(NE + j, j % 2, 1)

            over_groups(pool, lambda g, s, uses: split(g, s, CHUNKS), tail)

        @block.scalar
        def _(act):
            def silu(n, q):
                act.wait_ge(one_done, n + 1)
                if not (isinstance(n, int) and n < 2):
                    act.wait_ge(lo_done, n - 1)
                nc.scalar.activation(hidden[:, q % 3, :], psum_1[q % 3][:, 0:TOKENS], ACT.Silu).then_inc(silu_done, 1)

            def hi(n, q):
                act.wait_ge(gated, n + 1)
                if not (isinstance(n, int) and n < CHUNKS):
                    act.wait_ge(down_done, n - (CHUNKS - 1))
                nc.scalar.activation(hid_hi[:, q, :], hidden[:, q % 3, :], ACT.Copy).then_inc(hi_done, 1)

            def step(n, q):
                silu(n, q)
                if not (isinstance(n, int) and n == 0):
                    hi(n - 1, (q - 1) % CHUNKS)

            def tail():
                for _, n, q, _, _ in steps_of_tail():
                    step(n, q)
                hi(MAIN + TAIL - 1, CHUNKS - 1)

            def group(g, s, uses):
                over_rounds(act, g, lambda g, n, col, r: [step(n + c, c) for c in range(CHUNKS)])

            over_groups(act, group, tail)

        @block.tensor
        def _(pe):
            def up(n, q, s, c, col):
                if not (isinstance(n, int) and n < 2):
                    pe.wait_ge(multiplied, n - 1)
                cols, x = slice(c * P, (c + 1) * P), bass.ds(col, TOKENS)
                for w, (bank, done) in enumerate(((psum_1, one_done), (psum_3, three_done))):
                    split_product(nc, bank[q % 3][:, 0:TOKENS], [up_hi[s][:, w, k, cols] for k in range(K2)], [up_lo[s][:, w, k, cols] for k in range(K2)],
                                  [h_hi[:, k, x] for k in range(K2)], [h_lo[:, k, x] for k in range(K2)], True, True).then_inc(done, 1)

            def down(n, q, s, c, first, last, rounds):
                pe.wait_ge(lo_done, n + 1)
                if first and not (isinstance(rounds, int) and rounds == 0):
                    pe.wait_ge(acc_added, rounds)
                for k in range(K2):
                    rows = slice(k * P, (k + 1) * P)
                    ins = split_product(nc, psum_o[k][:, 0:TOKENS], [down_hi[s][:, c, rows]], [down_lo[s][:, c, rows]],
                                        [hid_hi[:, q, :]], [hid_lo[:, q, :]], first, last)
                ins.then_inc(down_done, 1)
                if last:
                    pe.wait_ge(down_done, n + 1)
                    pe.sem_inc(round_done, 1)

            def group(g, s, uses):
                pe.wait_ge(weights_ready, g + 1)

                def round_(g, n, col, r):
                    for c in range(CHUNKS):
                        up(n + c, c, s, c, col)
                        if c >= 2:
                            down(n + (c - 2), c - 2, s, c - 2, c == 2, False, g * ROUNDS + r)
                        elif not (isinstance(n, int) and n == 0):
                            before = (1 - s) if isinstance(r, int) else s
                            down(n + (c - 2), CHUNKS - 2 + c, before, CHUNKS - 2 + c, False, c == 1, None)

                over_rounds(pe, g, round_)

            def tail():
                def tail_down(n):
                    if n < 0:
                        down(MAIN + n, CHUNKS + n, 1, CHUNKS + n, False, n == -1, None)
                    else:
                        down(MAIN + n, n % CHUNKS, (n // ROUNDS) % 2, 0, True, True, NE * ROUNDS + n)

                for i, n, q, s, col in steps_of_tail():
                    if i % ROUNDS == 0:
                        pe.wait_ge(weights_ready, NE + i // ROUNDS + 1)
                    up(n, q, s, 0, col)
                    tail_down(i - 2)
                tail_down(TAIL - 2)
                tail_down(TAIL - 1)

            over_groups(pe, group, tail)

        @block.vector
        def _(dve):
            def add(rounds, col):
                dve.wait_ge(round_done, rounds + 1)
                for k in range(K2):
                    place = acc_T[:, k, bass.ds(col, TOKENS)]
                    ins = nc.vector.tensor_tensor(place, place, psum_o[k][:, 0:TOKENS], ALU.add)
                ins.then_inc(acc_added, 1)

            def lo(n, q):
                dve.wait_ge(hi_done, n + 1)
                nc.vector.tensor_tensor(hid_lo[:, q, :], hidden[:, q % 3, :], hid_hi[:, q, :].bitcast(F32), ALU.subtract).then_inc(lo_done, 1)

            def step(n, q, s, col):
                here = hidden[:, q % 3, :]
                dve.wait_ge(silu_done, n + 1)
                dve.wait_ge(three_done, n + 1)
                nc.vector.tensor_tensor(here, here, psum_3[q % 3][:, 0:TOKENS], ALU.mult).then_inc(multiplied, 1)
                dve.wait_ge(multiplied, n + 1)
                nc.vector.tensor_tensor(here, here, gate[:, s, bass.ds(col, TOKENS)], ALU.mult).then_inc(gated, 1)
                if not (isinstance(n, int) and n == 0):
                    lo(n - 1, (q - 1) % CHUNKS)

            def group(g, s, uses):
                dve.wait_ge(gates_loaded[s], uses * 16 + 16)

                def round_(g, n, col, r):
                    for c in range(CHUNKS):
                        if c == 2 and not (isinstance(n, int) and n == 0):
                            if isinstance(r, int):
                                add(g * ROUNDS - 1, NODES - TOKENS)
                            else:
                                add(g * ROUNDS + r - 1, col - TOKENS)
                        step(n + c, c, s, col)

                over_rounds(dve, g, round_)

            def tail():
                for i, n, q, s, col in steps_of_tail():
                    if i % ROUNDS == 0:
                        dve.wait_ge(gates_loaded[s], 16 * (NE // 2) + 16 * REST_SHARE * (i // ROUNDS // 2 + 1))
                    if i == 2:
                        add(NE * ROUNDS - 1, NODES - TOKENS)
                    if i >= 3:
                        add(NE * ROUNDS + i - 3, (i - 3) % ROUNDS * TOKENS)
                    step(n, q, s, col)
                lo(MAIN + TAIL - 1, CHUNKS - 1)
                for i in range(TAIL - 3, TAIL):
                    add(NE * ROUNDS + i, i % ROUNDS * TOKENS)

            nc.vector.memset(acc_T[:, :, :], 0.0).then_inc(acc_zero, 1)
            dve.wait_ge(acc_zero, 1)
            over_groups(dve, group, tail)


def stage_output(nc, t, keep, out):
    with ExitStack() as ctx:
        m = Memory(nc, ctx, "output")
        residual, const, acc_T = keep["residual"], keep["const"], keep["acc_T"]
        part = [m.sb(f"part{s}", [P, K2, P]) for s in range(2)]
        rows = m.sb("rows", [P, 2, C])
        psum = [m.ps(f"turned{s}") for s in range(2)]
        part_ready, turned, rows_ready = m.sem("part_ready"), m.sem("turned"), m.sem("rows_ready")
        stored = [m.sem(f"stored{s}") for s in range(2)]
        block = ctx.enter_context(nc.Block())
        PAIRS = TILES // 2 - 1

        def over(eng, tile):
            tile(0, 0, 0, P)
            tile(1, 1, 0, P)
            with eng.Fori(1, PAIRS) as i:
                tile(i * 2, 0, i, P)
                tile(i * 2 + 1, 1, i, P)
            tile(TILES - 2, 0, PAIRS, P)
            tile(TILES - 1, 1, PAIRS, LAST)

        def opens(n):
            return isinstance(n, int) and n < 2

        @block.scalar
        def _(act):
            def tile(n, s, use, tall):
                if not opens(n):
                    act.wait_ge(turned, n - 1)
                nc.scalar.activation(part[s][:, :, 0:tall], acc_T[:, :, bass.ds(n * P, tall)], ACT.Copy).then_inc(part_ready, 1)

            over(act, tile)

        @block.tensor
        def _(pe):
            def tile(n, s, use, tall):
                pe.wait_ge(part_ready, n + 1)
                if not opens(n):
                    pe.wait_ge(rows_ready, n - 1)
                for k in range(K2):
                    ins = nc.tensor.transpose(psum[s][0:tall, k * P:(k + 1) * P], part[s][:, k, 0:tall], const[:, IDENT:IDENT + P])
                ins.then_inc(turned, 1)

            over(pe, tile)

        @block.vector
        def _(dve):
            def tile(n, s, use, tall):
                dve.wait_ge(turned, n + 1)
                if not opens(n):
                    dve.wait_ge(stored[s], use * 16)
                nc.vector.tensor_tensor(rows[0:tall, s, :], residual[0:tall, bass.ds(n, 1), :].rearrange("p a c -> p (a c)"), psum[s][0:tall, 0:C],
                                        ALU.add).then_inc(rows_ready, 1)

            over(dve, tile)

        @block.sync
        def _(sp):
            def tile(n, s, use, tall):
                sp.wait_ge(rows_ready, n + 1)
                sp.dma_start(out[bass.ds(n * P, tall), :], rows[0:tall, s, :]).then_inc(stored[s], 16)

            over(sp, tile)
            for s in range(2):
                sp.wait_ge(stored[s], 16 * (TILES // 2))


def program(nc, t, out):
    with ExitStack() as ctx:
        m = Memory(nc, ctx, "kept")
        keep = {"residual": m.sb("residual", [P, TILES, C]), "const": m.sb("const", [P, CONSTANTS]), "mv": m.sb("mv", [P, TILES, 2]),
                "h_rows": nc.dram_tensor("h_rows", (PADDED, H_COLS), F32, kind="Internal").ap(),
                "gate_rows": nc.dram_tensor("gate_rows", (NE, PADDED), F32, kind="Internal").ap()}
        keep["h_table"] = keep["h_rows"].rearrange("n (r c) -> (n r) c", r=RELS)
        with ExitStack() as nodes:
            m = Memory(nc, nodes, "nodes")
            keep.update(q_all=m.sb("q_all", [P, TILES, C]), context=m.sb("context", [P, K2, P + 4]), agg_T=m.sb("agg_T", [P, K2, PADDED + WINDOW]))
            stage_projections(nc, t, keep)
            stage_graph(nc, t, keep)
            stage_sum(nc, t, keep)
        m = Memory(nc, ctx, "tokens")
        keep.update(h_hi=m.sb("h_hi", [P, K2, PADDED], F32R), h_lo=m.sb("h_lo", [P, K2, PADDED], F32R))
        with ExitStack() as inner:
            m = Memory(nc, inner, "attention_io")
            keep.update(z=m.sb("z", [P, TILES, C]), v=m.sb("v", [P, NKV, TILES, HD + 1]))
            stage_turn(nc, t, keep, router=False)
            stage_attention(nc, t, keep)
            stage_turn(nc, t, keep, router=True)
        m = Memory(nc, ctx, "experts_sum")
        keep["acc_T"] = m.sb("acc_T", [P, K2, NODES])
        stage_experts(nc, t, keep)
        stage_output(nc, t, keep, out)


def attention_arrays(a):
    half = HD // 2
    wq, wk = a["L0_ffn_wq"].reshape(NH, HD, C), a["L0_ffn_wk"].reshape(NKV, HD, C)

    def with_rotated(w):
        return np.concatenate([w, w[:, half:], w[:, :half]], axis=1).transpose(0, 2, 1)

    w1, w3, w2 = (w.transpose(0, 2, 1) for w in (a["L0_ffn_w1"], a["L0_ffn_w3"], a["L0_ffn_w2"]))
    up = np.stack([w1, w3], axis=1)
    whole = CHUNKS * P
    rest_up = np.zeros((REST_GROUPS, 2, C, P), up.dtype)
    rest_down = np.zeros((REST_GROUPS, P, C), w2.dtype)
    for e in range(NE):
        j, at = e // REST_SHARE, e % REST_SHARE * REST
        rest_up[j, :, :, at:at + REST] = up[e, :, :, whole:]
        rest_down[j, at:at + REST] = w2[e, whole:]
    return {
        "up_T": up[..., :whole],
        "down_T": w2[:, :whole],
        "rest_up_T": rest_up,
        "rest_down_T": rest_down,
        "wv_T": a["L0_ffn_wv"].T,
        "wqk_T": np.concatenate([np.concatenate([with_rotated(wk[g:g + 1]), with_rotated(wq[g * NH // NKV:(g + 1) * NH // NKV])]) for g in range(NKV)]),
        "wo_T": a["L0_ffn_wo"].T.reshape(NH, HD, C),
        "router_T": a["L0_ffn_router_w"].T,
        "ln1_w": a["L0_ffn_ln1_w"].reshape(K2, P).T,
        "ln2_w": a["L0_ffn_ln2_w"].reshape(K2, P).T,
        "rope": rope_table(),
    }


def kernel(**inputs):
    import concourse.bacc as bacc
    from concourse.bass_utils import run_bass_kernel_spmd as run

    a = {name: np.asarray(v) for name, v in inputs.items()}
    arrays = {
        "x": a["x"],
        "src_T": a["src"].reshape(COLUMNS, P).T,
        "dst_T": a["dst"].reshape(COLUMNS, P).T,
        "type_T": a["edge_type_8"].reshape(COLUMNS, P).T,
        "basis": a["L0_gnn_basis"],
        "comp": a["L0_gnn_comp"],
        "dense_T": np.concatenate([a["L0_mix_Wkv"].T, a["L0_mix_Wq"].T, a["L0_gnn_loop_weight"]], axis=1),
        "biases": np.stack([a["L0_gnn_bias_param"], a["L0_mix_bproj"]]),
        "proj_T": a["L0_mix_Wproj"].T,
        "constants": constants(),
    }
    arrays.update(attention_arrays(a))
    arrays = {name: np.ascontiguousarray(v) for name, v in arrays.items()}
    nc = bacc.Bacc("TRN2", target_bir_lowering=False, num_devices=1)
    t = {name: nc.dram_tensor(name, v.shape, mybir.dt.from_np(v.dtype), kind="ExternalInput").ap() for name, v in arrays.items()}
    out = nc.dram_tensor("out", (NODES, C), F32, kind="ExternalOutput").ap()
    program(nc, t, out)
    return run(nc, [arrays], core_ids=[0]).results[0]["out"]
```

```python
import math

import concourse.bass as bass
import numpy as np
from concourse import mybir
from contextlib import ExitStack

F32, F32R, I32, U32 = mybir.dt.float32, mybir.dt.float32r, mybir.dt.int32, mybir.dt.uint32
ALU, ACT, AX = mybir.AluOpType, mybir.ActivationFunctionType, mybir.AxisListType

P = 128
NODES, C, EDGES = 2500, 256, 80000
K2 = C // P
TILES = math.ceil(NODES / P)
LAST = NODES - (TILES - 1) * P
PADDED = TILES * P
RELS, BASES = 8, 4
H_COLS = RELS * C
BANK = 512
EPS_LN, EPS_RMS = 1e-5, 1e-6

COLUMNS = EDGES // P
GROUP = 5
GROUPS = COLUMNS // GROUP
RING = 5
WINDOW = 64
GENERAL_WINDOWS = PADDED // BANK

NH, NKV, HD = 4, 2, 64
NE, HID = 8, 682
"""Columns of the table of constants."""
IDENT, BLOCKS, HEADS, ROW0, DUP, MASK, MASK_T = 0, 128, 256, 260, 388, 516, 644
CONSTANTS = 772


def constants():
    t = np.zeros((P, CONSTANTS), np.float32)
    i = np.arange(P)
    t[:, IDENT:IDENT + P] = np.eye(P)
    t[:, BLOCKS:BLOCKS + P] = i[:, None] // 32 == i[None] // 32
    t[:, HEADS:HEADS + 4] = i[:, None] // 32 == np.arange(4)[None]
    t[0, ROW0:ROW0 + P] = 1
    t[:, DUP:DUP + P] = i[:, None] % HD == i[None] % HD
    t[:, MASK:MASK + P] = np.where(i[None] > i[:, None], -1e30, 0)
    t[:, MASK_T:MASK_T + P] = np.where(i[:, None] > i[None], -1e30, 0)
    return t


def rope_table():
    inv = 1.0 / 10000.0 ** (np.arange(0, HD, 2, dtype=np.float32) / HD)
    f = np.outer(np.arange(PADDED, dtype=np.float32), inv)
    emb = np.concatenate([f, f], axis=-1).T
    sign = np.where(np.arange(HD) < HD // 2, -1, 1)[:, None]
    return np.concatenate([np.cos(emb), np.sin(emb) * sign]).astype(np.float32)


class Memory:

    def __init__(self, nc, ctx, stage):
        self.nc, self.ctx, self.stage = nc, ctx, stage

    def sb(self, name, shape, dt=F32):
        return self.ctx.enter_context(self.nc.sbuf_tensor(f"{self.stage}_{name}", shape, dt))

    def ps(self, name, shape=(P, BANK)):
        return self.ctx.enter_context(self.nc.psum_tensor(f"{self.stage}_psum_{name}", list(shape), F32))

    def sem(self, name):
        return self.ctx.enter_context(self.nc.semaphore(f"{self.stage}_{name}"))


def split_product(nc, out, w_hi, w_lo, x_hi, x_lo, first, last):
    n = len(w_hi)
    for k in range(n):
        for j, (w, x) in enumerate(((w_hi[k], x_hi[k]), (w_hi[k], x_lo[k]), (w_lo[k], x_hi[k]))):
            ins = nc.tensor.matmul(out, w, x, start=first and k == 0 and j == 0, stop=last and k == n - 1 and j == 2)
    return ins


def inverse_root(nc, dve, done, count, value, root, inverse, work):
    for out, op in ((inverse, lambda o: nc.vector.reciprocal(o, root)),
                    (work, lambda o: nc.vector.tensor_tensor(o, value, inverse, ALU.mult)),
                    (work, lambda o: nc.vector.tensor_tensor(o, work, inverse, ALU.mult)),
                    (work, lambda o: nc.vector.tensor_scalar(o, work, -0.5, 1.5, ALU.mult, ALU.add)),
                    (inverse, lambda o: nc.vector.tensor_tensor(o, inverse, work, ALU.mult))):
        op(out).then_inc(done, 1)
        count += 1
        dve.wait_ge(done, count)
    return count


def stage_projections(nc, t, keep):
    with ExitStack() as ctx:
        m = Memory(nc, ctx, "proj")
        residual, q_all, context, const = keep["residual"], keep["q_all"], keep["context"], keep["const"]
        WIDE = H_COLS + 4 * C
        w_hi, w_lo = m.sb("w_hi", [P, K2, WIDE], F32R), m.sb("w_lo", [P, K2, WIDE], F32R)
        dense = m.sb("dense", [P, K2, 4 * C])
        basis = m.sb("basis", [P, K2, BASES, C])
        comp = m.sb("comp", [P, RELS * BASES])
        rel = m.sb("rel", [P, 2, K2, C])
        stats, mv = m.sb("stats", [P, TILES, 6]), m.sb("mv", [P, TILES, 2])
        std, rstd = m.sb("std", [P, TILES]), m.sb("rstd", [P, TILES])
        var_eps, work = m.sb("var_eps", [P, TILES]), m.sb("work", [P, TILES])
        xn = m.sb("xn", [P, 2, C])
        x_hi = [m.sb(f"x_hi{s}", [P, K2, P], F32R) for s in range(2)]
        x_lo = [m.sb(f"x_lo{s}", [P, K2, P], F32R) for s in range(2)]
        h_out = m.sb("h_out", [P, 2, 4, BANK])
        k_exp, q_exp = m.sb("k_exp", [P, 2, C]), m.sb("q_exp", [P, 2, C])
        k_row, v_row = m.sb("k_row", [P, 2, C]), m.sb("v_row", [P, 2, K2, P + 1])
        psum_t = [m.ps(f"t{s}") for s in range(2)]
        banks = [m.ps(f"bank{s}") for s in range(4)]
        psum_c = [m.ps(f"context{k}") for k in range(K2)]

        const_loaded, pad_zero, x_loaded = m.sem("const_loaded"), m.sem("pad_zero"), m.sem("x_loaded")
        basis_loaded, dense_loaded = m.sem("basis_loaded"), m.sem("dense_loaded")
        stats_step, std_ready = m.sem("stats_step"), m.sem("std_ready")
        mix_step, rel_split, w_hi_ready, w_lo_ready = m.sem("mix_step"), m.sem("rel_split"), m.sem("w_hi_ready"), m.sem("w_lo_ready")
        ones_ready = m.sem("ones_ready")
        xn_ready, transposed, hi_ready, lo_ready = (m.sem(n) for n in ("xn_ready", "transposed", "hi_ready", "lo_ready"))
        chunk_done, h_by_act, h_by_dve = m.sem("chunk_done"), m.sem("h_by_act"), m.sem("h_by_dve")
        h_stored = [m.sem(f"h_stored{s}") for s in range(2)]
        relu_done, k_exp_ready, q_exp_ready = m.sem("relu_done"), m.sem("k_exp_ready"), m.sem("q_exp_ready")
        kv_ready, qb_ready, context_done, context_kept = (m.sem(n) for n in ("kv_ready", "qb_ready", "context_done", "context_kept"))

        block = ctx.enter_context(nc.Block())
        PAIRS = (TILES - 2) // 2
        CHUNKS = 6

        def over_tiles(eng, tile):
            tile(0, 0, 0)
            with eng.Fori(0, PAIRS) as i:
                tile(i * 2 + 1, 1, i)
                tile(i * 2 + 2, 0, i + 1)
            tile(TILES - 1, 1, PAIRS)

        @block.sync
        def _(sp):
            sp.dma_start(residual[:, 0:TILES - 1, :], t["x"][0:(TILES - 1) * P, :].rearrange("(t p) c -> p t c", p=P)).then_inc(x_loaded, 16)
            sp.wait_ge(pad_zero, 1)
            sp.dma_start(residual[0:LAST, TILES - 1, :], t["x"][(TILES - 1) * P:NODES, :]).then_inc(x_loaded, 16)
            sp.dma_start(const[:, :], t["constants"]).then_inc(const_loaded, 16)

            def tile(n, s, use):
                sp.wait_ge(h_by_act, n * 2 + 2)
                sp.wait_ge(h_by_dve, n * 2 + 2)
                sp.dma_start(keep["h_rows"][bass.ds(n * P, P), :], h_out[:, s, :, :].rearrange("p a b -> p (a b)")).then_inc(h_stored[s], 16)

            over_tiles(sp, tile)
            for s in range(2):
                sp.wait_ge(h_stored[s], 16 * (TILES // 2))

        @block.gpsimd
        def _(pool):
            nc.gpsimd.memset(v_row[:, :, :, P:P + 1], 1.0).then_inc(ones_ready, 1)

        @block.scalar
        def _(act):
            for b in range(BASES):
                act.dma_start(basis[:, :, b, :], t["basis"][b].rearrange("(k p) o -> p k o", p=P)).then_inc(basis_loaded, 16)
            act.dma_start(comp[:, :], t["comp"].rearrange("r b -> (r b)").partition_broadcast(P)).then_inc(basis_loaded, 16)
            act.dma_start(dense[:, :, :], t["dense_T"].rearrange("(k p) o -> p k o", p=P)).then_inc(dense_loaded, 16)
            act.wait_ge(stats_step, 2 * TILES + 1)
            nc.scalar.activation(std[:, :], var_eps[:, :], ACT.Sqrt).then_inc(std_ready, 1)
            act.wait_ge(dense_loaded, 16)
            nc.scalar.activation(w_hi[:, :, H_COLS:WIDE], dense[:, :, :], ACT.Copy).then_inc(w_hi_ready, 1)
            for r in range(RELS):
                act.wait_ge(mix_step, BASES * (r + 1))
                nc.scalar.activation(w_hi[:, :, r * C:(r + 1) * C], rel[:, r % 2, :, :], ACT.Copy).then_inc(w_hi_ready, 1)

            def hi(n, s):
                act.wait_ge(transposed, n + 1)
                nc.scalar.activation(x_hi[s][:, :, :], psum_t[s][:, 0:C].rearrange("p (k c) -> p k c", k=K2), ACT.Copy).then_inc(hi_ready, 1)

            def elu_exp(bank, out, n, which, ready):
                nc.scalar.activation(out, bank, ACT.Relu, scale=-1.0).then_inc(relu_done, 1)
                act.wait_ge(relu_done, n * 2 + which)
                nc.scalar.activation(out, out, ACT.Exp, scale=-1.0).then_inc(ready, 1)

            def tile(n, s, use):
                first = isinstance(n, int) and n == 0
                last = isinstance(n, int) and n == TILES - 1
                at = 2 * s
                for j, c in enumerate((0, 2)):
                    act.wait_ge(chunk_done, n * CHUNKS + c + 1)
                    if c == 0 and not first:
                        act.wait_ge(h_stored[s], use * 16)
                    nc.scalar.activation(h_out[:, s, c, :], banks[(at + c) % 4][:, :], ACT.Copy).then_inc(h_by_act, 1)
                if not last:
                    hi(n + 1, 1 - s)
                act.wait_ge(chunk_done, n * CHUNKS + 5)
                if not first:
                    act.wait_ge(kv_ready, n - 1)
                elu_exp(banks[(at + 4) % 4][:, 0:C], k_exp[:, s, :], n, 1, k_exp_ready)
                act.wait_ge(chunk_done, n * CHUNKS + 6)
                if not first:
                    act.wait_ge(qb_ready, n - 1)
                elu_exp(banks[(at + 5) % 4][:, 0:C], q_exp[:, s, :], n, 2, q_exp_ready)

            hi(0, 0)
            over_tiles(act, tile)

        @block.tensor
        def _(pe):
            pe.wait_ge(const_loaded, 16)
            ident = const[:, IDENT:IDENT + P]

            def transposes(n, s):
                pe.wait_ge(xn_ready, n + 1)
                for k in range(K2):
                    ins = nc.tensor.transpose(psum_t[s][:, k * P:(k + 1) * P], xn[:, s, k * P:(k + 1) * P], ident)
                ins.then_inc(transposed, 1)

            def context_products(n, s, first, last):
                pe.wait_ge(kv_ready, n + 1)
                rows = LAST if last else P
                for k in range(K2):
                    ins = nc.tensor.matmul(psum_c[k][:, 0:P + 1], k_row[0:rows, s, k * P:(k + 1) * P], v_row[0:rows, s, k, :], start=first, stop=last)
                ins.then_inc(context_done, 1)

            def chunk(n, s, c):
                if not (isinstance(n, int) and n == 0 and c < 4):
                    if c in (0, 4):
                        pe.wait_ge(h_by_act, n * 2 + (c == 4))
                    elif c in (1, 5):
                        pe.wait_ge(h_by_dve, n * 2 + (c == 5))
                    else:
                        pe.wait_ge(kv_ready if c == 2 else qb_ready, n)
                cols = slice(c * BANK, (c + 1) * BANK)
                split_product(nc, banks[(2 * s + c) % 4][:, :], [x_hi[s][:, k, :] for k in range(K2)], [x_lo[s][:, k, :] for k in range(K2)],
                              [w_hi[:, k, cols] for k in range(K2)], [w_lo[:, k, cols] for k in range(K2)], True, True).then_inc(chunk_done, 1)

            def tile(n, s, use):
                first = isinstance(n, int) and n == 0
                last = isinstance(n, int) and n == TILES - 1
                pe.wait_ge(lo_ready, n + 1)
                for c in range(3):
                    chunk(n, s, c)
                if not last:
                    transposes(n + 1, 1 - s)
                if not first:
                    context_products(n - 1, 1 - s, tile.unstarted, False)
                    tile.unstarted = False
                for c in range(3, CHUNKS):
                    chunk(n, s, c)

            tile.unstarted = True
            transposes(0, 0)
            pe.wait_ge(w_hi_ready, RELS + 1)
            pe.wait_ge(w_lo_ready, RELS + 1)
            pe.wait_ge(ones_ready, 1)
            tile(0, 0, 0)
            tile(1, 1, 0)
            with pe.Fori(1, PAIRS) as i:
                tile(i * 2, 0, i)
                tile(i * 2 + 1, 1, i)
            tile(TILES - 2, 0, PAIRS)
            tile(TILES - 1, 1, PAIRS)
            context_products(TILES - 1, (TILES - 1) % 2, False, True)

        @block.vector
        def _(dve):
            nc.vector.memset(residual[:, TILES - 1, :], 0.0).then_inc(pad_zero, 1)
            dve.wait_ge(x_loaded, 32)
            for n in range(TILES):
                nc.vector.bn_stats(stats[:, n, :], residual[:, n, :]).then_inc(stats_step, 1)
            dve.wait_ge(stats_step, TILES)
            for n in range(TILES):
                nc.vector.bn_aggr(mv[:, n, :], stats[:, n, :]).then_inc(stats_step, 1)
            dve.wait_ge(stats_step, 2 * TILES)
            nc.vector.tensor_scalar(var_eps[:, :], mv[:, :, 1], EPS_LN, None, ALU.add).then_inc(stats_step, 1)
            dve.wait_ge(std_ready, 1)
            inverse_root(nc, dve, stats_step, 2 * TILES + 1, var_eps[:, :], std[:, :], rstd[:, :], work[:, :])

            def normalise(n, s):
                nc.vector.tensor_scalar(xn[:, s, :], residual[:, bass.ds(n, 1), :].rearrange("p a c -> p (a c)"), mv[:, bass.ds(n, 1), 0],
                                        rstd[:, bass.ds(n, 1)], ALU.subtract, ALU.mult).then_inc(xn_ready, 1)

            def lo(n, s):
                dve.wait_ge(hi_ready, n + 1)
                nc.vector.tensor_tensor(x_lo[s][:, :, :], psum_t[s][:, 0:C].rearrange("p (k c) -> p k c", k=K2), x_hi[s][:, :, :].bitcast(F32),
                                        ALU.subtract).then_inc(lo_ready, 1)

            normalise(0, 0)
            dve.wait_ge(w_hi_ready, 1)
            nc.vector.tensor_tensor(w_lo[:, :, H_COLS:WIDE], dense[:, :, :], w_hi[:, :, H_COLS:WIDE].bitcast(F32), ALU.subtract).then_inc(w_lo_ready, 1)
            dve.wait_ge(basis_loaded, 16 * (BASES + 1))
            for r in range(RELS):
                if r >= 2:
                    dve.wait_ge(w_lo_ready, r)
                nc.vector.tensor_scalar(rel[:, r % 2, :, :], basis[:, :, 0, :], comp[:, r * BASES:r * BASES + 1], None, ALU.mult).then_inc(mix_step, 1)
                for b in range(1, BASES):
                    dve.wait_ge(mix_step, BASES * r + b)
                    nc.vector.scalar_tensor_tensor(rel[:, r % 2, :, :], basis[:, :, b, :], comp[:, r * BASES + b:r * BASES + b + 1], rel[:, r % 2, :, :],
                                                   ALU.mult, ALU.add).then_inc(mix_step, 1)
                dve.wait_ge(mix_step, BASES * (r + 1))
                dve.wait_ge(w_hi_ready, r + 2)
                nc.vector.tensor_tensor(w_lo[:, :, r * C:(r + 1) * C], rel[:, r % 2, :, :], w_hi[:, :, r * C:(r + 1) * C].bitcast(F32),
                                        ALU.subtract).then_inc(w_lo_ready, 1)

            def tile(n, s, use):
                first = isinstance(n, int) and n == 0
                last = isinstance(n, int) and n == TILES - 1
                at = 2 * s
                if not last:
                    dve.wait_ge(transposed, n)
                    normalise(n + 1, 1 - s)
                dve.wait_ge(chunk_done, n * CHUNKS + 2)
                if not first:
                    dve.wait_ge(h_stored[s], use * 16)
                nc.vector.tensor_copy(h_out[:, s, 1, :], banks[(at + 1) % 4][:, :]).then_inc(h_by_dve, 1)
                if not last:
                    lo(n + 1, 1 - s)
                dve.wait_ge(chunk_done, n * CHUNKS + 4)
                nc.vector.tensor_copy(h_out[:, s, 3, :], banks[(at + 3) % 4][:, :]).then_inc(h_by_dve, 1)
                kv, ql = banks[(at + 4) % 4], banks[(at + 5) % 4]
                dve.wait_ge(k_exp_ready, n + 1)
                if not first:
                    dve.wait_ge(context_done, n - 1)
                nc.vector.scalar_tensor_tensor(k_row[:, s, :], kv[:, 0:C], 0.0, k_exp[:, s, :], ALU.max, ALU.add)
                nc.vector.tensor_copy(v_row[:, s, :, 0:P], kv[:, C:2 * C].rearrange("p (k c) -> p k c", k=K2)).then_inc(kv_ready, 1)
                dve.wait_ge(q_exp_ready, n + 1)
                nc.vector.scalar_tensor_tensor(q_all[:, bass.ds(n, 1), :].rearrange("p a c -> p (a c)"), ql[:, 0:C], 0.0, q_exp[:, s, :], ALU.max, ALU.add)
                row = residual[:, bass.ds(n, 1), :].rearrange("p a c -> p (a c)")
                nc.vector.tensor_tensor(row, row, ql[:, C:2 * C], ALU.add).then_inc(qb_ready, 1)

            dve.wait_ge(ones_ready, 1)
            lo(0, 0)
            over_tiles(dve, tile)
            dve.wait_ge(context_done, TILES)
            for k in range(K2):
                nc.vector.tensor_tensor(context[:, k, 0:P], psum_c[k][:, 0:P], const[:, BLOCKS:BLOCKS + P], ALU.mult)
                nc.vector.tensor_scalar(context[:, k, P:P + 4], const[:, HEADS:HEADS + 4], psum_c[k][:, P:P + 1], None, ALU.mult).then_inc(context_kept, 1)


def row_of(tensor, n):
    return tensor[:, bass.ds(n, 1), :].rearrange("p a c -> p (a c)")


SPAN = BANK // P
SPANS = TILES // SPAN
GROUPS_BEFORE = [min(GROUPS, math.ceil(GROUPS * BANK * (j + 1) / NODES + 2)) for j in range(SPANS)]


def stage_edges(nc, t, keep):
    with ExitStack() as ctx:
        m = Memory(nc, ctx, "edges")
        const, agg_T, row_numbers, in_window, base, rows, slots, window_iota = (
            keep[n] for n in ("const", "agg_T", "row_numbers", "in_window", "base", "rows", "slots", "window_iota"))
        src, dst, typ = m.sb("src", [P, COLUMNS], I32), m.sb("dst", [P, COLUMNS], I32), m.sb("typ", [P, COLUMNS], I32)
        row_index = m.sb("row_index", [P, COLUMNS], I32)
        dst_f, base_f = m.sb("dst_f", [P, COLUMNS]), m.sb("base_f", [P, GROUPS])
        extremes, worst = m.sb("extremes", [P, 2]), m.sb("worst", [P, 2])
        CONDITIONS = 1 + SPANS
        earliest = m.sb("earliest", [P, SPANS - 1])
        outside, count = m.sb("outside", [P, CONDITIONS]), m.sb("count", [P, 1])
        push, flag = m.sb("push", [P, 2]), m.sb("flag", [P, 1], I32)
        iota_i, iota = m.sb("iota_i", [P, PADDED], I32), m.sb("iota", [P, PADDED])
        wide_hot = m.sb("wide_hot", [P, BANK])
        psum = [m.ps(f"sum{k}") for k in range(K2)]

        edges_loaded, targets_loaded, iota_made, prep, spread = (m.sem(n) for n in ("edges_loaded", "targets_loaded", "iota_made", "prep", "spread"))
        extremes_ready, worst_found, flag_ready, ready, numbers_stored = (m.sem(n) for n in ("extremes_ready", "worst_found", "flag_ready", "ready", "numbers_stored"))
        slot_filled, gathered, group_used = m.sem("slot_filled"), m.sem("gathered"), m.sem("group_used")
        gather_turns = m.sem("gather_turns")
        wide_ready, wide_used, wide_added = m.sem("wide_ready"), m.sem("wide_used"), m.sem("wide_added")
        block = ctx.enter_context(nc.Block())

        def scattered(eng):
            eng.wait_ge(flag_ready, 1)
            return eng.value_load(flag[0:1, 0:1], min_val=0, max_val=CONDITIONS)

        def over_groups(eng, group):
            with eng.Fori(0, GROUPS) as g:
                group(g)

        @block.sync
        def _(sp):
            sp.dma_start(dst[:, :], t["dst_T"]).then_inc(targets_loaded, 16)
            sp.dma_start(src[:, :], t["src_T"]).then_inc(edges_loaded, 16)
            sp.dma_start(typ[:, :], t["type_T"]).then_inc(edges_loaded, 16)
            sp.wait_ge(ready, 1)
            sp.dma_start(row_numbers, row_index[:, :]).then_inc(numbers_stored, 16)
            sp.wait_ge(numbers_stored, 16)

            def group(g):
                sp.wait_ge(gathered, g * (16 * GROUP))
                sp.dma_start(slots[0][:, :], row_numbers[:, bass.ds(g * GROUP, GROUP)]).then_inc(slot_filled, 16)

            with sp.If(scattered(sp) > 0):
                over_groups(sp, group)

        @block.gpsimd
        def _(pool):
            nc.gpsimd.iota(iota_i[:, :], pattern=[[1, PADDED]], base=0, channel_multiplier=0).then_inc(iota_made, 1)
            last_row = pool.to_reg(PADDED * RELS - 1)
            pool.wait_ge(extremes_ready, 1)
            nc.gpsimd.partition_all_reduce(worst[:, :], extremes[:, :], P, bass.bass_isa.ReduceOp.max).then_inc(worst_found, 1)

            def group(g):
                pool.wait_ge(slot_filled, g * 16 + 16)
                pool.wait_ge(group_used, g)
                pool.sem_inc(gather_turns, 1)
                for e in range(GROUP):
                    pool.indirect_dma_start(out=rows[:, 0, e, :], out_offset=None, in_=keep["h_table"],
                                            in_offset=bass.IndirectOffsetOnAxis(ap=slots[0][:, e:e + 1], axis=0),
                                            bounds_check=last_row, oob_is_err=True).then_inc(gathered, 16)

            with pool.If(scattered(pool) > 0):
                over_groups(pool, group)

        @block.tensor
        def _(pe):
            pe.wait_ge(prep, 2)
            nc.tensor.matmul(psum[0][:, 0:GROUPS], const[:, ROW0:ROW0 + P], dst_f[:, :].rearrange("p (g e) -> p g e", e=GROUP)[:, :, 0],
                             start=True, stop=True).then_inc(spread, 1)

            def group(g):
                with pe.Fori(0, GENERAL_WINDOWS) as w:
                    for e in range(GROUP):
                        pe.wait_ge(wide_ready, g * (GENERAL_WINDOWS * GROUP) + w * GROUP + (e + 1))
                        if e == 0:
                            pe.wait_ge(gathered, g * (16 * GROUP) + 16 * GROUP)
                            pe.wait_ge(wide_added, g * GENERAL_WINDOWS + w)
                        for k in range(K2):
                            ins = nc.tensor.matmul(psum[k][:, :], rows[:, 0, e, k * P:(k + 1) * P], wide_hot[:, :], start=e == 0, stop=e == GROUP - 1)
                        ins.then_inc(wide_used, 1)
                pe.wait_ge(wide_used, g * (GENERAL_WINDOWS * GROUP) + GENERAL_WINDOWS * GROUP)
                pe.sem_inc(group_used, 1)

            with pe.If(scattered(pe) > 0):
                over_groups(pe, group)

        @block.vector
        def _(dve):
            nc.vector.memset(agg_T[:, :, :], 0.0).then_inc(prep, 1)
            dve.wait_ge(targets_loaded, 16)
            nc.vector.tensor_copy(dst_f[:, :], dst[:, :]).then_inc(prep, 1)
            dve.wait_ge(edges_loaded, 32)
            nc.vector.scalar_tensor_tensor(row_index[:, :], src[:, :], float(RELS), typ[:, :], ALU.mult, ALU.add).then_inc(ready, 1)
            dve.wait_ge(spread, 1)
            nc.vector.tensor_copy(base_f[:, :], psum[0][:, 0:GROUPS]).then_inc(prep, 1)
            dve.wait_ge(prep, 3)
            nc.vector.tensor_tensor(in_window[:, :].rearrange("p (g e) -> p g e", e=GROUP), dst_f[:, :].rearrange("p (g e) -> p g e", e=GROUP),
                                    base_f[:, :].unsqueeze(2).to_broadcast([P, GROUPS, GROUP]), ALU.subtract).then_inc(prep, 1)
            for j in range(SPANS - 1):
                nc.vector.tensor_reduce(earliest[:, j:j + 1], base_f[:, GROUPS_BEFORE[j]:GROUPS], AX.X, ALU.min)
            dve.wait_ge(prep, 4)
            nc.vector.tensor_reduce(extremes[:, 0:1], in_window[:, :], AX.X, ALU.max)
            nc.vector.tensor_reduce(extremes[:, 1:2], in_window[:, :], AX.X, ALU.min, negate=True).then_inc(extremes_ready, 1)
            dve.wait_ge(iota_made, 1)
            nc.vector.tensor_copy(window_iota[:, :], iota_i[:, 0:WINDOW])
            dve.wait_ge(worst_found, 1)
            dve.wait_ge(extremes_ready, 1)
            nc.vector.tensor_scalar(outside[:, 0:1], worst[:, 0:1], float(WINDOW), None, ALU.is_ge)
            nc.vector.tensor_scalar(outside[:, 1:2], worst[:, 1:2], 0.0, None, ALU.is_gt)
            for j in range(SPANS - 1):
                ins = nc.vector.tensor_scalar(outside[:, 2 + j:3 + j], earliest[:, j:j + 1], float((j + 1) * BANK), None, ALU.is_lt)
            ins.then_inc(prep, 1)
            dve.wait_ge(prep, 5)
            nc.vector.tensor_reduce(count[:, :], outside[:, :], AX.X, ALU.add).then_inc(prep, 1)
            dve.wait_ge(prep, 6)
            nc.vector.tensor_copy(flag[:, :], count[:, :]).then_inc(flag_ready, 1)
            nc.vector.tensor_scalar(push[:, 0:1], count[:, :], -4.0 * PADDED, None, ALU.mult)
            nc.vector.tensor_scalar(push[:, 1:2], count[:, :], float(PADDED), None, ALU.mult).then_inc(prep, 1)
            dve.wait_ge(prep, 7)
            nc.vector.tensor_scalar(in_window[:, :], in_window[:, :], push[:, 0:1], None, ALU.add)
            nc.vector.tensor_scalar(base[:, :], base_f[:, :], push[:, 1:2], float(PADDED), ALU.add, ALU.min).then_inc(prep, 1)

            def group(g):
                with dve.Fori(0, GENERAL_WINDOWS) as w:
                    for e in range(GROUP):
                        dve.wait_ge(wide_used, g * (GENERAL_WINDOWS * GROUP) + w * GROUP + e)
                        nc.vector.tensor_scalar(wide_hot[:, :], iota[:, bass.ds(w * BANK, BANK)], dst_f[:, bass.ds(g * GROUP + e, 1)], None,
                                                ALU.is_equal).then_inc(wide_ready, 1)
                    dve.wait_ge(wide_used, g * (GENERAL_WINDOWS * GROUP) + w * GROUP + GROUP)
                    dve.wait_ge(wide_added, g * GENERAL_WINDOWS + w)
                    for k in range(K2):
                        place = agg_T[:, k, bass.ds(w * BANK, BANK)]
                        ins = nc.vector.tensor_tensor(place, place, psum[k][:, :], ALU.add)
                    ins.then_inc(wide_added, 1)

            with dve.If(scattered(dve) > 0):
                nc.vector.tensor_copy(iota[:, :], iota_i[:, :]).then_inc(prep, 1)
                dve.wait_ge(prep, 9)
                over_groups(dve, group)


SPAN_HEADS = NH * SPANS
MIX_ROUNDS = TILES // RING
LOOPED = GROUPS_BEFORE[0] // RING * RING


def span_steps(j):
    return SPAN * (j + 1)


def rows_items(j):
    chain = ("sums", "root_1", "normal", "squares", "value_2", "root_2", "h", "h_turn", "h_hi", "h_lo", "v", "v_keep")
    return ([("rope", j)] + [("key_weights", j, kv) for kv in range(NKV)] + [(name, j) for name in chain] +
            [(name, j, kv) for kv in range(NKV) for name in ("key_project", "key_double")])


def prepare_items(m):
    return ([("weights", m), ("project", m), ("double", m)] + [("maxima", m, n, c) for n in range(SPAN) for c in range(m // NH + 1)] + [("turn", m)])


def late_items(j):
    return [(name, j) for name in ("late_squares", "late_value", "late_root", "late_rows")], [
        (name, j) for name in ("late_turn", "late_hi", "late_lo", "late_logits", "late_exp", "late_pick", "late_gates")]


def shares(items, places):
    cost = [0.4 if what[0] == "maxima" else 0.1 if what[0].endswith("weights") else 1 for what in items]
    out, spent = [[] for _ in range(places)], 0
    for what, c in zip(items, cost):
        out[min(places - 1, int(spent * places / (sum(cost) + 1e-9)))].append(what)
        spent += c
    return out


def span_order():
    order = [("hot", LOOPED)]

    def add_group(g):
        order.append(("sum", g))
        if g + 1 < GROUPS:
            order.append(("hot", g + 1))

    for g in range(LOOPED, GROUPS_BEFORE[0]):
        add_group(g)
    order += rows_items(0) + prepare_items(0)
    before = None
    for m in range(SPAN_HEADS):
        j, turn = divmod(m, NH)
        ahead, groups = [], []
        if turn == NH - 1 and j + 1 < SPANS:
            ahead += rows_items(j + 1)
        if m + 1 < SPAN_HEADS:
            ahead += prepare_items(m + 1)
        if j and turn < 2:
            ahead += late_items(j - 1)[turn]
        if turn < NH - 1 and j + 1 < SPANS:
            start, count = GROUPS_BEFORE[j], GROUPS_BEFORE[j + 1] - GROUPS_BEFORE[j]
            groups = range(start + count * turn // (NH - 1), start + count * (turn + 1) // (NH - 1))
        steps = span_steps(j)
        ahead = shares(ahead, steps - 1)
        for i in range(steps):
            order.append(("scores", m, i))
            if before:
                order.append(("values",) + before)
            if m and i == 0:
                order.append(("keep", m - 1))
            if m and i == 1:
                order.append(("out", m - 1))
            if i:
                order += ahead[i - 1]
            for g in groups[len(groups) * i // steps:len(groups) * (i + 1) // steps]:
                add_group(g)
            before = (m, i)
    first, second = late_items(SPANS - 1)
    return order + [("values",) + before, ("keep", SPAN_HEADS - 1), ("out", SPAN_HEADS - 1)] + first + second


def stage_spans(nc, t, keep):
    with ExitStack() as ctx:
        m = Memory(nc, ctx, "spans")
        residual, const, agg_T, context, z = keep["residual"], keep["const"], keep["agg_T"], keep["context"], keep["q_all"]
        q_all = z
        row_numbers, in_window, base, rows, slots, window_iota = (keep[n] for n in ("row_numbers", "in_window", "base", "rows", "slots", "window_iota"))
        hot = m.sb("hot", [P, GROUP, WINDOW])
        late_h = m.sb("late_h", [P, SPAN, C])
        proj, biases = late_h[:, 0:2, :], late_h[:, 2:4, :]
        late_hi, late_lo = m.sb("late_hi", [P, K2, BANK], F32R), m.sb("late_lo", [P, K2, BANK], F32R)
        gates_T = late_h[:, :, :].rearrange("p a c -> p (a c)")[0:NE, 0:BANK]
        den = m.sb("den", [P, 2, 8])
        rope = m.sb("rope", [P, BANK])
        raw_w = m.sb("raw_w", [P, NKV + NH, K2, P])
        w_hi, w_lo = ([m.sb(f"w_{x}{s}", [P, K2, P], F32R) for s in range(2)] for x in ("hi", "lo"))
        wv_hi, wv_lo = m.sb("wv_hi", [P, K2, P], F32R), m.sb("wv_lo", [P, K2, P], F32R)
        norm_w, norm2_w = m.sb("norm_w", [P, K2]), m.sb("norm2_w", [P, K2])
        router = m.sb("router", [P, K2, NE])
        router_hi, router_lo = m.sb("router_hi", [P, K2, NE], F32R), m.sb("router_lo", [P, K2, NE], F32R)
        logits, top, probs_e, index_u = m.sb("logits", [P, SPAN, NE]), m.sb("top", [P, SPAN, NE]), m.sb("probs_e", [P, SPAN, NE]), m.sb("index_u", [P, SPAN, NE], U32)
        index, gates = logits, top
        hit = m.sb("hit", [P, 2, SPAN, NE])
        peak, total, scale, pair = m.sb("peak", [P, SPAN]), m.sb("total", [P, SPAN]), m.sb("scale", [P, SPAN]), m.sb("pair", [P, SPAN, 2])
        h_hi, h_lo = m.sb("h_hi", [P, K2, BANK], F32R), m.sb("h_lo", [P, K2, BANK], F32R)
        rotated = m.sb("rotated", [P, 2, BANK])
        q_both = [m.sb(f"q_both{s}", [P, BANK], F32R) for s in range(NKV)]
        q_max = [m.sb(f"q_max{s}", [HD + 2, BANK], F32R) for s in range(NKV)]
        k_hi = [m.sb(f"k_hi{s}", [P, PADDED], F32R) for s in range(NKV)]
        k_lo = [m.sb(f"k_lo{s}", [HD + 2, PADDED], F32R) for s in range(NKV)]
        v = m.sb("v", [P, NKV, TILES, HD + 1])
        wo = m.sb("wo", [HD + 1, NH, C + 1])
        probs = m.sb("probs", [P, 2, BANK])
        y_T = m.sb("y_T", [HD + 1, BANK])
        neg = m.sb("neg", [P, NKV, SPAN, SPANS])
        neg_max, neg_hi = m.sb("neg_max", [P, SPAN]), m.sb("neg_hi", [P, SPAN], F32R)
        columns = m.sb("columns", [P, SPAN, P])
        inverse = m.sb("inverse", [P, 2])
        stats, mv = m.sb("stats", [P, SPAN, 6]), m.sb("mv", [P, SPAN, 2])
        value, std, inv, work = (m.sb(n, [P, 3, SPAN]) for n in ("value", "std", "inv", "work"))
        mean_sq = m.sb("mean_sq", [P, 2, SPAN])
        ident_r, mask, mask_T = m.sb("ident_r", [P, P], F32R), m.sb("mask", [P, P], F32R), m.sb("mask_T", [P, P], F32R)
        h = rotated[:, :, :].rearrange("p a (b c) -> p (a b) c", c=C)
        q_row, attn = h[:, 0, :], h[:, 2, :]
        q_T, attn_T = (probs[:, s, 0:C].rearrange("p (k c) -> p k c", k=K2) for s in range(2))
        ident = const[:, IDENT:IDENT + P]

        p_sum = m.ps("sum")
        p_max = [m.ps(f"max{s}") for s in range(2)]
        p_score = [m.ps(f"score{s}") for s in range(2)]
        p_y, p_a, p_b = m.ps("y"), m.ps("a"), m.ps("b")
        outs = (p_a, p_b)
        pq, pa, pm = p_score[0], p_a, p_b

        slot_filled = [m.sem(f"slot_filled{s}") for s in range(RING)]
        gathered = [m.sem(f"gathered{s}") for s in range(RING)]
        gather_turns, hot_ready, summed, added = (m.sem(n) for n in ("gather_turns", "hot_ready", "summed", "added"))
        proj_loaded, v_weights_loaded, weights_loaded, wo_loaded = (
            m.sem(n) for n in ("proj_loaded", "v_weights_loaded", "weights_loaded", "wo_loaded"))
        rope_loaded = m.sem("rope_loaded")
        q_copied, q_turned, q_T_ready, attended, den_step, attn_ready, attn_turned, attn_T_ready, mixed, mix_added = (
            m.sem(n) for n in ("q_copied", "q_turned", "q_T_ready", "attended", "den_step", "attn_ready", "attn_turned", "attn_T_ready", "mixed", "mix_added"))
        ready, cleared, wv_hi_ready, wv_lo_ready = (m.sem(n) for n in ("ready", "cleared", "wv_hi_ready", "wv_lo_ready"))
        agg_turned, agg_added, norm_step, value_ready, std_ready, z_ready, squared, h_ready, h_turned, hi_ready, lo_ready, v_done, v_kept = (
            m.sem(n) for n in ("agg_turned", "agg_added", "norm_step", "value_ready", "std_ready", "z_ready", "squared", "h_ready", "h_turned", "hi_ready",
                               "lo_ready", "v_done", "v_kept"))
        late_squared, late_value_ready, late_std_ready, late_step, late_h_ready, late_turned, late_hi_ready, late_lo_ready = (
            m.sem(n) for n in ("late_squared", "late_value_ready", "late_std_ready", "late_step", "late_h_ready", "late_turned", "late_hi_ready", "late_lo_ready"))
        late_stored, logits_done, peak_taken, exps_ready, gates_ready, gates_turned, gates_kept, gates_stored = (
            m.sem(n) for n in ("late_stored", "logits_done", "peak_taken", "exps_ready", "gates_ready", "gates_turned", "gates_kept", "gates_stored"))
        w_hi_ready, w_lo_ready, projected, rotated_ready, doubled, part_hi, part_lo = (
            m.sem(n) for n in ("w_hi_ready", "w_lo_ready", "projected", "rotated_ready", "doubled", "part_hi", "part_lo"))
        max_done, max_free, max_step, turned, maxima_ready = (m.sem(n) for n in ("max_done", "max_free", "max_step", "turned", "maxima_ready"))
        score_done, score_free, probs_free, y_ready, out_done, out_step, out_free = (
            m.sem(n) for n in ("score_done", "score_free", "probs_free", "y_ready", "out_done", "out_step", "out_free"))
        block = ctx.enter_context(nc.Block())

        PER_KV = NH // NKV
        PROJECTIONS = NKV + NH
        COMBINE = 4
        ORDER = span_order()

        def steps_before(m):
            j, turn = divmod(m, NH)
            return NH * SPAN * j * (j + 1) // 2 + (turn * span_steps(j) if turn else 0)

        def number_of(m):
            return m // NH * PROJECTIONS + NKV + m % NH

        def place_of(m):
            return m % NKV * (1 + PER_KV) + 1 + m % NH // NKV

        def over_spans(eng, mix, sum_, do):
            with eng.Fori(0, MIX_ROUNDS) as i:
                for s in range(RING):
                    mix(i, s)
            with eng.Fori(MIX_ROUNDS, LOOPED // RING) as i:
                for s in range(RING):
                    sum_(i, s)
            for what, *at in ORDER:
                if what in do:
                    do[what](*at)

        @block.sync
        def _(sp):
            def fill(s, group):
                sp.dma_start(slots[s][:, :], row_numbers[:, bass.ds(group * GROUP, GROUP)]).then_inc(slot_filled[s], 16)

            for s in range(RING):
                fill(s, s)
            with sp.Fori(1, GROUPS // RING) as i:
                for s in range(RING):
                    sp.wait_ge(gathered[s], i * (16 * GROUP))
                    fill(s, i * RING + s)

        @block.gpsimd
        def _(pool):
            last_row = pool.to_reg(PADDED * RELS - 1)

            def gather(s):
                for e in range(GROUP):
                    pool.indirect_dma_start(out=rows[:, s, e, :], out_offset=None, in_=keep["h_table"],
                                            in_offset=bass.IndirectOffsetOnAxis(ap=slots[s][:, e:e + 1], axis=0),
                                            bounds_check=last_row, oob_is_err=True).then_inc(gathered[s], 16)

            for s in range(RING):
                pool.wait_ge(slot_filled[s], 16)
                gather(s)
            with pool.Fori(1, GROUPS // RING) as i:
                for s in range(RING):
                    pool.wait_ge(slot_filled[s], i * 16 + 16)
                    pool.wait_ge(summed, i * RING + (s - RING + 1))
                    pool.sem_inc(gather_turns, 1)
                    gather(s)

        @block.scalar
        def _(act):
            act.sem_inc(score_free, 2)
            act.dma_start(proj[:, :, :], t["proj_T"].rearrange("(k p) o -> p k o", p=P)).then_inc(proj_loaded, 16)
            act.dma_start(biases[:, :, :], t["biases"].partition_broadcast(P)).then_inc(proj_loaded, 16)
            act.dma_start(raw_w[:, 0, :, :], t["wv_T"].rearrange("(k p) o -> p k o", p=P)).then_inc(v_weights_loaded, 16)
            for tensor, name in ((norm_w, "ln1_w"), (norm2_w, "ln2_w")):
                act.dma_start(tensor[:, :], t[name]).then_inc(v_weights_loaded, 16)
            act.dma_start(router[:, :, :], t["router_T"].rearrange("(k p) o -> p k o", p=P)).then_inc(v_weights_loaded, 16)
            act.wait_ge(cleared, 3)
            act.dma_start(wo[0:HD, :, 0:C], t["wo_T"].rearrange("g d c -> d g c")).then_inc(wo_loaded, 16)
            nc.scalar.activation(mask[:, :], const[:, MASK:MASK + P], ACT.Copy)
            nc.scalar.activation(mask_T[:, :], const[:, MASK_T:MASK_T + P], ACT.Copy)
            nc.scalar.activation(ident_r[:, :], const[:, IDENT:IDENT + P], ACT.Copy).then_inc(ready, 1)
            act.wait_ge(v_weights_loaded, 64)
            nc.scalar.activation(router_hi[:, :, :], router[:, :, :], ACT.Copy)
            nc.scalar.activation(wv_hi[:, :, :], raw_w[:, 0, :, :], ACT.Copy).then_inc(wv_hi_ready, 1)
            act.wait_ge(wv_lo_ready, 1)
            for n in range(PROJECTIONS):
                act.dma_start(raw_w[:, n, :, :], t["wqk_T"][n].rearrange("(k p) n -> p k n", p=P)).then_inc(weights_loaded, 16)
            act.wait_ge(weights_loaded, 16 * PROJECTIONS)

            def mix(i, s):
                n = i * RING + s
                act.wait_ge(q_turned, n)
                nc.scalar.activation(q_row, row_of(q_all, n), ACT.Copy).then_inc(q_copied, 1)
                act.wait_ge(q_turned, n + 1)
                nc.scalar.activation(q_T, pq[:, 0:C].rearrange("p (k c) -> p k c", k=K2), ACT.Copy).then_inc(q_T_ready, 1)
                act.wait_ge(attn_turned, n + 1)
                nc.scalar.activation(attn_T, pq[:, C:2 * C].rearrange("p (k c) -> p k c", k=K2), ACT.Copy).then_inc(attn_T_ready, 1)

            def split_hi(number, place):
                if number >= 2:
                    act.wait_ge(projected, number - 1)
                nc.scalar.activation(w_hi[number % 2][:, :, :], raw_w[:, place, :, :], ACT.Copy).then_inc(w_hi_ready, 1)

            def parts(number, scale, outputs):
                act.wait_ge(doubled, number + 1)
                for out in outputs:
                    ins = nc.scalar.activation(out, p_b[0:out.shape[0], :], ACT.Copy, scale=scale)
                ins.then_inc(part_hi, 1)

            def load_rope(j):
                act.wait_ge(rotated_ready, j * PROJECTIONS)
                act.dma_start(rope[:, :], t["rope"][:, j * BANK:(j + 1) * BANK]).then_inc(rope_loaded, 16)

            def root(j, which):
                act.wait_ge(value_ready, 2 * j + which + 1)
                nc.scalar.activation(std[:, which, :], value[:, which, :], ACT.Sqrt).then_inc(std_ready, 1)

            def squares(j):
                for n in range(SPAN):
                    act.wait_ge(z_ready, j * SPAN + n + 1)
                    nc.scalar.activation(h[:, n, :], z[:, j * SPAN + n, :], ACT.Square, accum_out=mean_sq[:, 0, n:n + 1]).then_inc(squared, 1)

            def take_hi(out, weight, done, ready, j):
                for s in range(2):
                    act.wait_ge(done, j * 2 + s + 1)
                    for k in range(K2):
                        ins = nc.scalar.activation(out[:, k, s * C:(s + 1) * C].rearrange("p (t c) -> p t c", t=2),
                                                   p_max[s][:, :].rearrange("p (t k c) -> p t k c", t=2, k=K2)[:, :, k, :], ACT.Copy, scale=weight[:, k:k + 1])
                    ins.then_inc(ready, 1)

            def keep_values(j):
                act.wait_ge(v_done, j + 1)
                for kv in range(NKV):
                    ins = nc.scalar.activation(v[:, kv, j * SPAN:(j + 1) * SPAN, 0:HD],
                                               p_max[0][:, :].rearrange("p (t a c) -> p t a c", t=SPAN, a=NKV)[:, :, kv, :], ACT.Copy)
                ins.then_inc(v_kept, 1)

            def exponentials(m, i):
                start = max(0, i - SPAN * (m // NH)) * P
                b = steps_before(m) + i
                act.wait_ge(score_done, b + 1)
                act.wait_ge(probs_free, b + 1)
                nc.scalar.activation(probs[:, i % 2, start:BANK], p_score[i % 2][:, start:BANK], ACT.Exp).then_inc(score_free, 1)

            def take_maxima(m):
                act.wait_ge(turned, m + 1)
                nc.scalar.activation(q_max[m % NKV][HD:HD + 2, :], p_b[HD:HD + 2, :], ACT.Copy).then_inc(maxima_ready, 1)

            def keep_sum(m):
                act.wait_ge(probs_free, steps_before(m + 1) + 2)
                act.wait_ge(out_done, m * SPAN)
                nc.scalar.activation(y_T[:, :], p_y[0:HD + 1, :], ACT.Copy).then_inc(y_ready, 1)

            def late_squares(j):
                act.wait_ge(out_free, SPAN * NH * (j + 1) + 2)
                if j:
                    act.wait_ge(gates_stored, 16 * j)
                for n in range(SPAN):
                    nc.scalar.activation(late_h[:, n, :], z[:, j * SPAN + n, :], ACT.Square, accum_out=mean_sq[:, 1, n:n + 1]).then_inc(late_squared, 1)

            def late_root(j):
                act.wait_ge(late_value_ready, j + 1)
                nc.scalar.activation(std[:, 2, :], value[:, 2, :], ACT.Sqrt).then_inc(late_std_ready, 1)

            def late_hi_part(j):
                if j:
                    act.wait_ge(late_stored, 32 * j)
                take_hi(late_hi, norm2_w, late_turned, late_hi_ready, j)

            def late_exp(j):
                act.wait_ge(late_lo_ready, 2 * j + 2)
                cols = slice(j * BANK, (j + 1) * BANK)
                act.dma_start(keep["tokens_hi"][:, :, cols], late_hi[:, :, :].bitcast(F32)).then_inc(late_stored, 16)
                act.dma_start(keep["tokens_lo"][:, :, cols], late_lo[:, :, :].bitcast(F32)).then_inc(late_stored, 16)
                act.wait_ge(peak_taken, j + 1)
                nc.scalar.activation(probs_e[:, :, :], logits[:, :, :], ACT.Exp).then_inc(exps_ready, 1)

            def late_gates(j):
                act.wait_ge(gates_turned, j + 1)
                nc.scalar.activation(gates_T, p_max[1][0:NE, :], ACT.Copy).then_inc(gates_kept, 1)
                act.wait_ge(gates_kept, j + 1)
                act.dma_start(keep["gate_rows"][:, j * BANK:(j + 1) * BANK], gates_T).then_inc(gates_stored, 16)

            over_spans(act, mix, lambda i, s: None, {
                "rope": load_rope, "key_weights": lambda j, kv: split_hi(j * PROJECTIONS + kv, kv * (1 + PER_KV)),
                "root_1": lambda j: root(j, 0), "squares": squares, "root_2": lambda j: root(j, 1),
                "h_hi": lambda j: take_hi(h_hi, norm_w, h_turned, hi_ready, j), "v_keep": keep_values,
                "key_double": lambda j, kv: parts(j * PROJECTIONS + kv, 1.0, [k_hi[kv][:, j * BANK:(j + 1) * BANK]]),
                "weights": lambda m: split_hi(number_of(m), place_of(m)),
                "double": lambda m: parts(number_of(m), HD ** -0.5, [q_both[m % NKV][:, :], q_max[m % NKV][0:HD, :]]),
                "scores": exponentials, "turn": take_maxima, "keep": keep_sum, "late_squares": late_squares, "late_root": late_root,
                "late_hi": late_hi_part, "late_exp": late_exp, "late_gates": late_gates})
            act.wait_ge(late_stored, 32 * SPANS)
            act.wait_ge(gates_stored, 16 * SPANS)

        @block.tensor
        def _(pe):
            pe.sem_inc(probs_free, 2)
            pe.wait_ge(proj_loaded, 32)

            pe.wait_ge(ready, 1)
            pe.wait_ge(cleared, 3)
            pe.wait_ge(wv_lo_ready, 1)
            pe.wait_ge(wo_loaded, 16)

            def sum_(i, s):
                pe.wait_ge(gathered[s], i * (16 * GROUP) + 16 * GROUP)
                pe.wait_ge(hot_ready, i * RING + (s + 1))
                pe.wait_ge(added, i * RING + s)
                for k in range(K2):
                    for e in range(GROUP):
                        ins = nc.tensor.matmul(p_sum[:, k * WINDOW:(k + 1) * WINDOW], rows[:, s, e, k * P:(k + 1) * P], hot[:, e, :],
                                               start=e == 0, stop=e == GROUP - 1)
                ins.then_inc(summed, 1)

            def mix(i, s):
                n = i * RING + s
                pe.wait_ge(q_copied, n + 1)
                for k in range(K2):
                    ins = nc.tensor.transpose(pq[:, k * P:(k + 1) * P], q_row[:, k * P:(k + 1) * P], ident)
                ins.then_inc(q_turned, 1)
                pe.wait_ge(q_T_ready, n + 1)
                for k in range(K2):
                    ins = nc.tensor.matmul(pa[:, k * (P + 4):(k + 1) * (P + 4)], q_T[:, k, :], context[:, k, :], start=True, stop=True)
                ins.then_inc(attended, 1)
                sum_(i, s)
                pe.wait_ge(attn_ready, n + 1)
                for k in range(K2):
                    ins = nc.tensor.transpose(pq[:, C + k * P:C + (k + 1) * P], attn[:, k * P:(k + 1) * P], ident)
                ins.then_inc(attn_turned, 1)
                pe.wait_ge(mix_added, n)
                for one in range(2):
                    nc.tensor.matmul(pm[:, 0:C], const[:, ROW0:ROW0 + P], biases[:, one, :], start=one == 0, stop=False)
                pe.wait_ge(attn_T_ready, n + 1)
                for k in range(K2):
                    ins = nc.tensor.matmul(pm[:, 0:C], attn_T[:, k, :], proj[:, k, :], start=False, stop=k == K2 - 1)
                ins.then_inc(mixed, 1)

            issued = {"maxima": 0, "late": 0}

            def project(number, heads_out):
                s = number % 2
                pe.wait_ge(w_lo_ready, number + 1)
                pe.wait_ge(rotated_ready, number)
                pe.wait_ge(out_free, heads_out * SPAN + 2)
                split_product(nc, p_a[:, :], [w_hi[s][:, k, :] for k in range(K2)], [w_lo[s][:, k, :] for k in range(K2)],
                              [h_hi[:, k, :] for k in range(K2)], [h_lo[:, k, :] for k in range(K2)], True, True).then_inc(projected, 1)

            def double(number):
                pe.wait_ge(rotated_ready, number + 1)
                pe.wait_ge(part_lo, number)
                nc.tensor.matmul(p_b[:, :], const[:, DUP:DUP + P], rotated[:, number % 2, :], start=True, stop=True).then_inc(doubled, 1)

            def maxima_banks_free():
                pe.wait_ge(max_free, issued["maxima"] + 2)
                if issued["late"]:
                    pe.wait_ge(gates_kept, issued["late"])

            def transposes(row, s, done):
                for n in range(2):
                    for k in range(K2):
                        ins = nc.tensor.transpose(p_max[s][:, (n * K2 + k) * P:(n * K2 + k + 1) * P], row(2 * s + n, k), ident)
                ins.then_inc(done, 1)

            def turn_sums(j):
                pe.wait_ge(added, GROUPS_BEFORE[j])
                maxima_banks_free()
                for s in range(2):
                    transposes(lambda n, k: agg_T[:, k, (SPAN * j + n) * P:(SPAN * j + n + 1) * P], s, agg_turned)

            def turn_h(j):
                for s in range(2):
                    pe.wait_ge(h_ready, j * 2 + s + 1)
                    transposes(lambda n, k: h[:, n, k * P:(k + 1) * P], s, h_turned)

            def value_products(j):
                pe.wait_ge(lo_ready, j * 2 + 2)
                for n in range(SPAN):
                    tile = slice(n * P, (n + 1) * P)
                    ins = split_product(nc, p_max[0][:, tile], [h_hi[:, k, tile] for k in range(K2)], [h_lo[:, k, tile] for k in range(K2)],
                                        [wv_hi[:, k, :] for k in range(K2)], [wv_lo[:, k, :] for k in range(K2)], True, True)
                ins.then_inc(v_done, 1)

            def maxima(m, n, c):
                j, kv = m // NH, m % NKV
                if n == 0 and c == 0:
                    pe.wait_ge(part_lo, number_of(m) + 1)
                    pe.wait_ge(v_kept, j + 1)
                    if issued["late"]:
                        pe.wait_ge(gates_kept, issued["late"])
                a = n * (j + 1) + c
                width = BANK if c < j else (n + 1) * P
                pe.wait_ge(max_free, steps_before(m) + (a + 1))
                bank = p_max[a % 2]
                ins = nc.tensor.matmul(bank[:, 0:width], q_both[kv][:, n * P:(n + 1) * P], k_hi[kv][:, c * BANK:c * BANK + width], start=True, stop=c < j,
                                       skip_group_check=True)
                if c == j:
                    ins = nc.tensor.matmul(bank[:, width - P:width], ident_r[:, :], mask[:, :], start=False, stop=True, skip_group_check=True)
                ins.then_inc(max_done, 1)
                issued["maxima"] += 1

            def turn_maxima(m):
                pe.wait_ge(max_step, m * COMBINE + COMBINE)
                for n in range(SPAN):
                    ins = nc.tensor.transpose(p_b[:, n * P:(n + 1) * P], columns[:, n, :], ident)
                ins.then_inc(turned, 1)

            def scores(m, i):
                j, kv = m // NH, m % NKV
                start = max(0, i - SPAN * j) * P
                if i == 0:
                    pe.wait_ge(maxima_ready, m + 1)
                pe.wait_ge(score_free, steps_before(m) + (i + 1))
                out, keys = p_score[i % 2][:, start:BANK], slice(i * P, (i + 1) * P)
                diagonal = i >= SPAN * j
                nc.tensor.matmul(out, k_hi[kv][:, keys], q_both[kv][:, start:BANK], start=True, stop=False, skip_group_check=True)
                ins = nc.tensor.matmul(out, k_lo[kv][:, keys], q_max[kv][:, start:BANK], start=False, stop=not diagonal, skip_group_check=True)
                if diagonal:
                    ins = nc.tensor.matmul(p_score[i % 2][:, start:start + P], ident_r[:, :], mask_T[:, :], start=False, stop=True, skip_group_check=True)
                ins.then_inc(score_done, 1)

            def values(m, i):
                j = m // NH
                start = max(0, i - SPAN * j) * P
                pe.wait_ge(score_free, steps_before(m) + (i + 3))
                if i == 0:
                    pe.wait_ge(y_ready, m)
                nc.tensor.matmul(p_y[0:HD + 1, start:BANK], v[:, m % NKV, i, :], probs[:, i % 2, start:BANK], start=i == 0,
                                 stop=i == span_steps(j) - 1).then_inc(probs_free, 1)

            def out(m):
                pe.wait_ge(y_ready, m + 1)
                for n in range(SPAN):
                    pe.wait_ge(out_free, m * SPAN + (n + 1))
                    nc.tensor.matmul(outs[n % 2][:, 0:C + 1], y_T[:, n * P:(n + 1) * P], wo[:, m % NKV * PER_KV + m % NH // NKV, :],
                                     start=True, stop=True).then_inc(out_done, 1)

            def late_turn(j):
                maxima_banks_free()
                for s in range(2):
                    pe.wait_ge(late_h_ready, j * 2 + s + 1)
                    transposes(lambda n, k: late_h[:, n, k * P:(k + 1) * P], s, late_turned)

            def late_logits(j):
                pe.wait_ge(late_lo_ready, j * 2 + 2)
                for n in range(SPAN):
                    tile = slice(n * P, (n + 1) * P)
                    ins = split_product(nc, p_max[0][:, n * NE:(n + 1) * NE], [late_hi[:, k, tile] for k in range(K2)], [late_lo[:, k, tile] for k in range(K2)],
                                        [router_hi[:, k, :] for k in range(K2)], [router_lo[:, k, :] for k in range(K2)], True, True)
                ins.then_inc(logits_done, 1)

            def late_gates(j):
                pe.wait_ge(gates_ready, j + 1)
                for n in range(SPAN):
                    ins = nc.tensor.transpose(p_max[1][0:NE, n * P:(n + 1) * P], gates[:, n, :], ident)
                ins.then_inc(gates_turned, 1)
                issued["late"] += 1

            over_spans(pe, mix, sum_, {
                "sum": lambda g: sum_(g // RING, g % RING), "sums": turn_sums, "h_turn": turn_h, "v": value_products,
                "key_project": lambda j, kv: project(j * PROJECTIONS + kv, max(0, NH * j - 1)), "key_double": lambda j, kv: double(j * PROJECTIONS + kv),
                "project": lambda m: project(number_of(m), max(0, m - 1)), "double": lambda m: double(number_of(m)), "maxima": maxima, "turn": turn_maxima,
                "scores": scores, "values": values, "out": out, "late_turn": late_turn, "late_logits": late_logits, "late_gates": late_gates})

        @block.vector
        def _(dve):
            dve.sem_inc(max_free, 2)
            dve.sem_inc(out_free, 2)
            nc.vector.memset(wo[:, :, :], 0.0).then_inc(cleared, 1)
            dve.wait_ge(cleared, 1)
            nc.vector.memset(wo[HD:HD + 1, :, C:C + 1], 1.0)
            nc.vector.memset(v[:, :, :, HD:HD + 1], 1.0).then_inc(cleared, 1)
            for s in range(NKV):
                nc.vector.memset(k_lo[s][HD:HD + 2, :].bitcast(F32), 1.0)
            nc.vector.memset(columns[:, :, :], 0.0).then_inc(cleared, 1)
            dve.wait_ge(wv_hi_ready, 1)
            nc.vector.tensor_tensor(router_lo[:, :, :], router[:, :, :], router_hi[:, :, :].bitcast(F32), ALU.subtract)
            nc.vector.tensor_tensor(wv_lo[:, :, :], raw_w[:, 0, :, :], wv_hi[:, :, :].bitcast(F32), ALU.subtract).then_inc(wv_lo_ready, 1)
            dve.wait_ge(weights_loaded, 16 * PROJECTIONS)

            def make_hot(i, s):
                nc.vector.tensor_tensor(hot[:, :, :], window_iota[:, :].unsqueeze(1).to_broadcast([P, GROUP, WINDOW]),
                                        in_window[:, bass.ds((i * RING + s) * GROUP, GROUP)].unsqueeze(2).to_broadcast([P, GROUP, WINDOW]),
                                        ALU.is_equal).then_inc(hot_ready, 1)

            def add_sum(i, s):
                g = i * RING + s
                at = dve.value_load(base[0:1, bass.ds(g, 1)], min_val=0, max_val=PADDED)
                dve.wait_ge(summed, g + 1)
                dve.wait_ge(added, g)
                place = agg_T[:, :, bass.ds(at, WINDOW)]
                nc.vector.tensor_tensor(place, place, p_sum[:, 0:K2 * WINDOW].rearrange("p (k w) -> p k w", k=K2), ALU.add).then_inc(added, 1)

            def sum_(i, s):
                make_hot(i, s)
                add_sum(i, s)

            def mix(i, s):
                n = i * RING + s
                make_hot(i, s)
                dve.wait_ge(attended, n + 1)
                both = pa[:, 0:2 * (P + 4)].rearrange("p (k c) -> p k c", k=K2)
                nc.vector.tensor_scalar(den[:, 0, :].rearrange("p (k c) -> p k c", k=K2), both[:, :, P:P + 4], 1e-6, None, ALU.max).then_inc(den_step, 1)
                dve.wait_ge(den_step, n * 2 + 1)
                nc.vector.reciprocal(den[:, 1, :], den[:, 0, :]).then_inc(den_step, 1)
                dve.wait_ge(den_step, n * 2 + 2)
                for k in range(K2):
                    ins = nc.vector.tensor_tensor(attn[:, k * P:(k + 1) * P].rearrange("p (h e) -> p h e", h=4), both[:, k, 0:P].rearrange("p (h e) -> p h e", h=4),
                                                  den[:, 1, 4 * k:4 * k + 4].unsqueeze(2).to_broadcast([P, 4, 32]), ALU.mult)
                ins.then_inc(attn_ready, 1)
                add_sum(i, s)
                dve.wait_ge(mixed, n + 1)
                row = row_of(residual, n)
                nc.vector.tensor_tensor(row, row, pm[:, 0:C], ALU.add).then_inc(mix_added, 1)

            def split_lo(number, place):
                dve.wait_ge(w_hi_ready, number + 1)
                nc.vector.tensor_tensor(w_lo[number % 2][:, :, :], raw_w[:, place, :, :], w_hi[number % 2][:, :, :].bitcast(F32), ALU.subtract).then_inc(w_lo_ready, 1)

            def rotate(number):
                dve.wait_ge(projected, number + 1)
                if number >= 2:
                    dve.wait_ge(doubled, number - 1)
                nc.vector.tensor_tensor(rotated[:, number % 2, :], p_a[:, :], rope[:, :], ALU.mult).then_inc(rotated_ready, 1)

            chain = [0]

            def then(ins):
                chain[0] += 1
                ins.then_inc(norm_step, 1)
                dve.wait_ge(norm_step, chain[0])

            def root(which, ready, n):
                x, r, w = value[:, which, :], inv[:, which, :], work[:, which, :]
                dve.wait_ge(ready, n)
                then(nc.vector.reciprocal(r, std[:, which, :]))
                then(nc.vector.tensor_tensor(w, x, r, ALU.mult))
                then(nc.vector.tensor_tensor(w, w, r, ALU.mult))
                then(nc.vector.tensor_scalar(w, w, -0.5, 1.5, ALU.mult, ALU.add))
                then(nc.vector.tensor_tensor(r, r, w, ALU.mult))

            def add_sums(j):
                for s in range(2):
                    dve.wait_ge(agg_turned, j * 2 + s + 1)
                    two = residual[:, SPAN * j + 2 * s:SPAN * j + 2 * s + 2, :]
                    nc.vector.tensor_tensor(two, two, p_max[s][:, :].rearrange("p (t c) -> p t c", t=2), ALU.add).then_inc(agg_added, 1)
                for n in range(SPAN):
                    dve.wait_ge(agg_added, j * 2 + n // 2 + 1)
                    ins = nc.vector.bn_stats(stats[:, n, :], residual[:, SPAN * j + n, :])
                then(ins)
                for n in range(SPAN):
                    ins = nc.vector.bn_aggr(mv[:, n, :], stats[:, n, :])
                then(ins)
                nc.vector.tensor_scalar(value[:, 0, :], mv[:, :, 1], EPS_LN, None, ALU.add).then_inc(value_ready, 1)
                dve.wait_ge(value_ready, 2 * j + 1)

            def normal(j):
                root(0, std_ready, 2 * j + 1)
                for n in range(SPAN):
                    tile = SPAN * j + n
                    nc.vector.tensor_scalar(z[:, tile, :], residual[:, tile, :], mv[:, n, 0:1], inv[:, 0, n:n + 1], ALU.subtract, ALU.mult).then_inc(z_ready, 1)

            def second_value(j):
                dve.wait_ge(squared, SPAN * (j + 1))
                nc.vector.tensor_scalar(value[:, 1, :], mean_sq[:, 0, :], 1.0 / C, EPS_RMS, ALU.mult, ALU.add).then_inc(value_ready, 1)
                dve.wait_ge(value_ready, 2 * j + 2)

            def scaled_rows(j, which, out, ready):
                for n in range(SPAN):
                    ins = nc.vector.tensor_scalar(out[:, n, :], z[:, SPAN * j + n, :], inv[:, which, n:n + 1], None, ALU.mult)
                    if n % 2:
                        ins.then_inc(ready, 1)

            def h_rows(j):
                root(1, std_ready, 2 * j + 2)
                scaled_rows(j, 1, h, h_ready)

            def take_lo(out, hi, weight, done, ready, j):
                for s in range(2):
                    dve.wait_ge(done, j * 2 + s + 1)
                    cols = slice(s * C, (s + 1) * C)
                    for k in range(K2):
                        ins = nc.vector.scalar_tensor_tensor(out[:, k, cols].rearrange("p (t c) -> p t c", t=2),
                                                             p_max[s][:, :].rearrange("p (t k c) -> p t k c", t=2, k=K2)[:, :, k, :], weight[:, k:k + 1],
                                                             hi[:, k, cols].bitcast(F32).rearrange("p (t c) -> p t c", t=2), ALU.mult, ALU.subtract)
                    ins.then_inc(ready, 1)

            def key_project(j, kv):
                dve.wait_ge(rope_loaded, 16 * (j + 1))
                rotate(j * PROJECTIONS + kv)

            def key_low(j, kv):
                dve.wait_ge(part_hi, j * PROJECTIONS + kv + 1)
                x = slice(j * BANK, (j + 1) * BANK)
                nc.vector.tensor_tensor(k_lo[kv][0:HD, x], p_b[0:HD, :], k_hi[kv][0:HD, x].bitcast(F32), ALU.subtract).then_inc(part_lo, 1)

            def query_low(m):
                dve.wait_ge(part_hi, number_of(m) + 1)
                q = q_both[m % NKV]
                nc.vector.scalar_tensor_tensor(q[HD:P, :], p_b[HD:P, :], HD ** -0.5, q[HD:P, :].bitcast(F32), ALU.mult, ALU.subtract).then_inc(part_lo, 1)

            def maxima(m, n, c):
                j = m // NH
                a = n * (j + 1) + c
                width = BANK if c < j else (n + 1) * P
                dve.wait_ge(max_done, steps_before(m) + (a + 1))
                nc.vector.tensor_reduce(neg[:, m % NKV, n, c:c + 1], p_max[a % 2][:, 0:width], AX.X, ALU.max, negate=True).then_inc(max_free, 1)

            def combine_maxima(m):
                done = m * COMBINE
                dve.wait_ge(max_free, steps_before(m + 1) + 2)
                nc.vector.tensor_reduce(neg_max[:, :], neg[:, m % NKV, :, 0:m // NH + 1], AX.X, ALU.min).then_inc(max_step, 1)
                dve.wait_ge(max_step, done + 1)
                nc.vector.tensor_copy(neg_hi[:, :], neg_max[:, :]).then_inc(max_step, 1)
                dve.wait_ge(max_step, done + 2)
                dve.wait_ge(turned, m)
                nc.vector.tensor_copy(columns[:, :, HD], neg_hi[:, :].bitcast(F32)).then_inc(max_step, 1)
                nc.vector.tensor_tensor(columns[:, :, HD + 1], neg_max[:, :], neg_hi[:, :].bitcast(F32), ALU.subtract).then_inc(max_step, 1)

            def add_output(m):
                for n in range(SPAN):
                    done = m * SPAN + (n + 1)
                    one = inverse[:, n % 2:n % 2 + 1]
                    dve.wait_ge(out_done, done)
                    nc.vector.reciprocal(one, outs[n % 2][:, C:C + 1]).then_inc(out_step, 1)
                    dve.wait_ge(out_step, done)
                    row = z[:, SPAN * (m // NH) + n, :]
                    nc.vector.scalar_tensor_tensor(row, outs[n % 2][:, 0:C], one, row, ALU.mult, ALU.add).then_inc(out_free, 1)

            def late_value(j):
                dve.wait_ge(late_squared, SPAN * (j + 1))
                nc.vector.tensor_scalar(value[:, 2, :], mean_sq[:, 1, :], 1.0 / C, EPS_RMS, ALU.mult, ALU.add).then_inc(late_value_ready, 1)
                dve.wait_ge(late_value_ready, j + 1)
                dve.wait_ge(out_free, SPAN * NH * (j + 1) + 2)
                span = slice(SPAN * j, SPAN * (j + 1))
                nc.vector.tensor_tensor(residual[:, span, :], residual[:, span, :], z[:, span, :], ALU.add)

            def late_rows(j):
                root(2, late_std_ready, j + 1)
                scaled_rows(j, 2, late_h, late_h_ready)

            def spread(rows):
                return rows.unsqueeze(2).to_broadcast([P, SPAN, NE])

            def late_peak(j):
                dve.wait_ge(logits_done, j + 1)
                logit = p_max[0][:, 0:SPAN * NE].rearrange("p (t e) -> p t e", e=NE)
                then(nc.vector.tensor_reduce(peak[:, :], logit, AX.X, ALU.max))
                nc.vector.tensor_tensor(logits[:, :, :], logit, spread(peak[:, :]), ALU.subtract).then_inc(peak_taken, 1)

            def late_pick(j):
                dve.wait_ge(exps_ready, j + 1)
                then(nc.vector.tensor_reduce(total[:, :], probs_e[:, :, :], AX.X, ALU.add))
                then(nc.vector.reciprocal(scale[:, :], total[:, :]))
                then(nc.vector.tensor_tensor(probs_e[:, :, :], probs_e[:, :, :], spread(scale[:, :]), ALU.mult))
                for n in range(SPAN):
                    ins = nc.vector.max(top[:, n, :], probs_e[:, n, :])
                then(ins)
                for n in range(SPAN):
                    ins = nc.vector.max_index(index_u[:, n, :], top[:, n, :], probs_e[:, n, :])
                then(ins)
                nc.vector.tensor_copy(index[:, :, :], index_u[:, :, :])
                then(nc.vector.tensor_tensor(total[:, :], top[:, :, 0], top[:, :, 1], ALU.add))
                then(nc.vector.tensor_scalar(total[:, :], total[:, :], 1e-9, None, ALU.add))
                then(nc.vector.reciprocal(scale[:, :], total[:, :]))
                then(nc.vector.tensor_tensor(pair[:, :, :], top[:, :, 0:2], scale[:, :].unsqueeze(2).to_broadcast([P, SPAN, 2]), ALU.mult))
                for one in range(2):
                    ins = nc.vector.tensor_tensor(hit[:, one, :, :], spread(index[:, :, one]), window_iota[:, 0:NE].unsqueeze(1).to_broadcast([P, SPAN, NE]), ALU.is_equal)
                then(ins)
                for one in range(2):
                    ins = nc.vector.tensor_tensor(hit[:, one, :, :], hit[:, one, :, :], spread(pair[:, :, one]), ALU.mult)
                then(ins)
                nc.vector.tensor_tensor(gates[:, :, :], hit[:, 0, :, :], hit[:, 1, :, :], ALU.add).then_inc(gates_ready, 1)

            over_spans(dve, mix, sum_, {
                "hot": lambda g: make_hot(g // RING, g % RING), "sum": lambda g: add_sum(g // RING, g % RING),
                "key_weights": lambda j, kv: split_lo(j * PROJECTIONS + kv, kv * (1 + PER_KV)), "sums": add_sums, "normal": normal,
                "value_2": second_value, "h": h_rows, "h_lo": lambda j: take_lo(h_lo, h_hi, norm_w, hi_ready, lo_ready, j),
                "key_project": key_project, "key_double": key_low,
                "weights": lambda m: split_lo(number_of(m), place_of(m)), "project": lambda m: rotate(number_of(m)),
                "double": query_low, "maxima": maxima, "turn": combine_maxima, "out": add_output,
                "late_value": late_value, "late_rows": late_rows, "late_lo": lambda j: take_lo(late_lo, late_hi, norm2_w, late_hi_ready, late_lo_ready, j),
                "late_logits": late_peak, "late_pick": late_pick})


CHUNKS = HID // P
REST = HID - CHUNKS * P
REST_SHARE = P // REST
REST_GROUPS = math.ceil(NE / REST_SHARE)
TOKENS = 500
ROUNDS = NODES // TOKENS
GROUP_STEPS = ROUNDS * CHUNKS


def stage_experts(nc, t, keep):
    with ExitStack() as ctx:
        m = Memory(nc, ctx, "experts")
        h_hi, h_lo, acc_T = keep["h_hi"], keep["h_lo"], keep["acc_T"]
        raw_up, raw_down = m.sb("raw_up", [P, 2, K2, CHUNKS * P]), m.sb("raw_down", [P, CHUNKS, C])
        up_hi, up_lo = ([m.sb(f"up_{x}{s}", [P, 2, K2, CHUNKS * P], F32R) for s in range(2)] for x in ("hi", "lo"))
        down_hi, down_lo = ([m.sb(f"down_{x}{s}", [P, CHUNKS, C], F32R) for s in range(2)] for x in ("hi", "lo"))
        gate = m.sb("gate", [P, 2, NODES])
        hidden = m.sb("hidden", [P, 3, TOKENS])
        hid_hi, hid_lo = m.sb("hid_hi", [P, CHUNKS, TOKENS], F32R), m.sb("hid_lo", [P, CHUNKS, TOKENS], F32R)
        psum_1, psum_3 = [m.ps(f"one{s}") for s in range(3)], [m.ps(f"three{s}") for s in range(3)]
        psum_o = [m.ps(f"out{k}") for k in range(K2)]
        tokens_loaded = [m.sem(f"tokens_loaded{s}") for s in range(2)]
        raw_loaded, split_turns, split_hi, weights_ready, acc_zero = (m.sem(n) for n in ("raw_loaded", "split_turns", "split_hi", "weights_ready", "acc_zero"))
        gates_loaded = [m.sem(f"gates_loaded{s}") for s in range(2)]
        one_done, three_done, silu_done, multiplied, gated, hi_done, lo_done, down_done, round_done, acc_added = (
            m.sem(n) for n in ("one_done", "three_done", "silu_done", "multiplied", "gated", "hi_done", "lo_done", "down_done", "round_done", "acc_added"))
        block = ctx.enter_context(nc.Block())
        TAIL = REST_GROUPS * ROUNDS
        MAIN = NE * GROUP_STEPS

        def over_groups(eng, group, tail):
            group(0, 0, 0)
            with eng.Fori(0, (NE - 2) // 2) as i:
                group(i * 2 + 1, 1, i)
                group(i * 2 + 2, 0, i + 1)
            group(NE - 1, 1, NE // 2 - 1)
            tail()

        def over_rounds(eng, g, round_):
            round_(g, g * GROUP_STEPS, 0, 0)
            with eng.Fori(1, ROUNDS) as r:
                round_(g, g * GROUP_STEPS + r * CHUNKS, r * TOKENS, r)

        def steps_of_tail():
            for n in range(TAIL):
                yield n, MAIN + n, n % CHUNKS, (n // ROUNDS) % 2, n % ROUNDS * TOKENS

        @block.sync
        def _(sp):
            def load(g, s, uses):
                if not (isinstance(g, int) and g == 0):
                    sp.wait_ge(weights_ready, g)
                for w in range(2):
                    sp.dma_start(raw_up[:, w, :, :], t["up_T"][bass.ds(g, 1), w].rearrange("g (k p) n -> p (g k) n", p=P)).then_inc(raw_loaded, 16)
                sp.dma_start(raw_down[:, :, :], t["down_T"][bass.ds(g, 1)].rearrange("g (k p) n -> p (g k) n", p=P)).then_inc(raw_loaded, 16)
                if isinstance(g, int) and g == 0:
                    load_tokens(TOKENS, NODES, tokens_loaded[1])
                if not (isinstance(g, int) and g <= 1):
                    sp.wait_ge(gated, (g - 1) * GROUP_STEPS)
                sp.dma_start(gate[:, s, :], keep["gate_rows"][bass.ds(g, 1), 0:NODES].rearrange("a n -> (a n)").partition_broadcast(P)).then_inc(gates_loaded[s], 16)

            def tail():
                for j in range(REST_GROUPS):
                    g, s = NE + j, j % 2
                    sp.wait_ge(weights_ready, g)
                    for w in range(2):
                        sp.dma_start(raw_up[:, w, :, 0:P], t["rest_up_T"][j, w].rearrange("(k p) n -> p k n", p=P)).then_inc(raw_loaded, 16)
                    sp.dma_start(raw_down[:, 0, :], t["rest_down_T"][j]).then_inc(raw_loaded, 16)
                    sp.wait_ge(gated, (NE - 1) * GROUP_STEPS if j == 0 else MAIN + (j - 1) * ROUNDS)
                    for e in range(REST_SHARE):
                        top = P if e == REST_SHARE - 1 else (e + 1) * REST
                        expert = min(j * REST_SHARE + e, NE - 1)
                        sp.dma_start(gate[e * REST:top, s, :], keep["gate_rows"][expert, 0:NODES].partition_broadcast(top - e * REST)).then_inc(gates_loaded[s], 16)

            def load_tokens(start, end, loaded):
                for tensor, name in ((h_hi, "tokens_hi"), (h_lo, "tokens_lo")):
                    sp.dma_start(tensor[:, :, start:end].bitcast(F32), keep[name][:, :, start:end]).then_inc(loaded, 16)

            load_tokens(0, TOKENS, tokens_loaded[0])
            over_groups(sp, load, tail)

        @block.gpsimd
        def _(pool):
            def split(g, s, chunks):
                pool.wait_ge(raw_loaded, g * 48 + 48)
                if not (isinstance(g, int) and g <= 1):
                    pool.wait_ge(down_done, (g - 1) * GROUP_STEPS if not isinstance(g, int) or g <= NE else MAIN + (g - NE - 1) * ROUNDS)
                pool.sem_inc(split_turns, 1)
                cols = slice(0, chunks * P)
                nc.gpsimd.tensor_copy(up_hi[s][:, :, :, cols], raw_up[:, :, :, cols])
                nc.gpsimd.tensor_copy(down_hi[s][:, 0:chunks, :], raw_down[:, 0:chunks, :]).then_inc(split_hi, 1)
                pool.wait_ge(split_hi, g + 1)
                for w in range(2):
                    nc.gpsimd.tensor_tensor(up_lo[s][:, w, :, cols], raw_up[:, w, :, cols], up_hi[s][:, w, :, cols].bitcast(F32), ALU.subtract)
                nc.gpsimd.tensor_tensor(down_lo[s][:, 0:chunks, :], raw_down[:, 0:chunks, :], down_hi[s][:, 0:chunks, :].bitcast(F32),
                                        ALU.subtract).then_inc(weights_ready, 1)

            def tail():
                for j in range(REST_GROUPS):
                    split(NE + j, j % 2, 1)

            over_groups(pool, lambda g, s, uses: split(g, s, CHUNKS), tail)

        @block.scalar
        def _(act):
            def silu(n, q):
                act.wait_ge(one_done, n + 1)
                if not (isinstance(n, int) and n < 2):
                    act.wait_ge(lo_done, n - 1)
                nc.scalar.activation(hidden[:, q % 3, :], psum_1[q % 3][:, 0:TOKENS], ACT.Silu).then_inc(silu_done, 1)

            def hi(n, q):
                act.wait_ge(gated, n + 1)
                if not (isinstance(n, int) and n < CHUNKS):
                    act.wait_ge(down_done, n - (CHUNKS - 1))
                nc.scalar.activation(hid_hi[:, q, :], hidden[:, q % 3, :], ACT.Copy).then_inc(hi_done, 1)

            def step(n, q):
                silu(n, q)
                if not (isinstance(n, int) and n == 0):
                    hi(n - 1, (q - 1) % CHUNKS)

            def tail():
                for _, n, q, _, _ in steps_of_tail():
                    step(n, q)
                hi(MAIN + TAIL - 1, CHUNKS - 1)

            def group(g, s, uses):
                over_rounds(act, g, lambda g, n, col, r: [step(n + c, c) for c in range(CHUNKS)])

            over_groups(act, group, tail)

        @block.tensor
        def _(pe):
            def up(n, q, s, c, col):
                if not (isinstance(n, int) and n < 2):
                    pe.wait_ge(multiplied, n - 1)
                cols, x = slice(c * P, (c + 1) * P), bass.ds(col, TOKENS)
                for w, (bank, done) in enumerate(((psum_1, one_done), (psum_3, three_done))):
                    split_product(nc, bank[q % 3][:, 0:TOKENS], [up_hi[s][:, w, k, cols] for k in range(K2)], [up_lo[s][:, w, k, cols] for k in range(K2)],
                                  [h_hi[:, k, x] for k in range(K2)], [h_lo[:, k, x] for k in range(K2)], True, True).then_inc(done, 1)

            def down(n, q, s, c, first, last, rounds):
                pe.wait_ge(lo_done, n + 1)
                if first and not (isinstance(rounds, int) and rounds == 0):
                    pe.wait_ge(acc_added, rounds)
                for k in range(K2):
                    rows = slice(k * P, (k + 1) * P)
                    ins = split_product(nc, psum_o[k][:, 0:TOKENS], [down_hi[s][:, c, rows]], [down_lo[s][:, c, rows]],
                                        [hid_hi[:, q, :]], [hid_lo[:, q, :]], first, last)
                ins.then_inc(down_done, 1)
                if last:
                    pe.wait_ge(down_done, n + 1)
                    pe.sem_inc(round_done, 1)

            def group(g, s, uses):
                pe.wait_ge(weights_ready, g + 1)

                def round_(g, n, col, r):
                    if isinstance(g, int) and g == 0:
                        pe.wait_ge(tokens_loaded[0 if isinstance(r, int) else 1], 32)
                    for c in range(CHUNKS):
                        up(n + c, c, s, c, col)
                        if c >= 2:
                            down(n + (c - 2), c - 2, s, c - 2, c == 2, False, g * ROUNDS + r)
                        elif not (isinstance(n, int) and n == 0):
                            before = (1 - s) if isinstance(r, int) else s
                            down(n + (c - 2), CHUNKS - 2 + c, before, CHUNKS - 2 + c, False, c == 1, None)

                over_rounds(pe, g, round_)

            def tail():
                def tail_down(n):
                    if n < 0:
                        down(MAIN + n, CHUNKS + n, 1, CHUNKS + n, False, n == -1, None)
                    else:
                        down(MAIN + n, n % CHUNKS, (n // ROUNDS) % 2, 0, True, True, NE * ROUNDS + n)

                for i, n, q, s, col in steps_of_tail():
                    if i % ROUNDS == 0:
                        pe.wait_ge(weights_ready, NE + i // ROUNDS + 1)
                    up(n, q, s, 0, col)
                    tail_down(i - 2)
                tail_down(TAIL - 2)
                tail_down(TAIL - 1)

            over_groups(pe, group, tail)

        @block.vector
        def _(dve):
            def add(rounds, col):
                dve.wait_ge(round_done, rounds + 1)
                for k in range(K2):
                    place = acc_T[:, k, bass.ds(col, TOKENS)]
                    ins = nc.vector.tensor_tensor(place, place, psum_o[k][:, 0:TOKENS], ALU.add)
                ins.then_inc(acc_added, 1)

            def lo(n, q):
                dve.wait_ge(hi_done, n + 1)
                nc.vector.tensor_tensor(hid_lo[:, q, :], hidden[:, q % 3, :], hid_hi[:, q, :].bitcast(F32), ALU.subtract).then_inc(lo_done, 1)

            def step(n, q, s, col):
                here = hidden[:, q % 3, :]
                dve.wait_ge(silu_done, n + 1)
                dve.wait_ge(three_done, n + 1)
                nc.vector.tensor_tensor(here, here, psum_3[q % 3][:, 0:TOKENS], ALU.mult).then_inc(multiplied, 1)
                dve.wait_ge(multiplied, n + 1)
                nc.vector.tensor_tensor(here, here, gate[:, s, bass.ds(col, TOKENS)], ALU.mult).then_inc(gated, 1)
                if not (isinstance(n, int) and n == 0):
                    lo(n - 1, (q - 1) % CHUNKS)

            def group(g, s, uses):
                dve.wait_ge(gates_loaded[s], uses * 16 + 16)

                def round_(g, n, col, r):
                    for c in range(CHUNKS):
                        if c == 2 and not (isinstance(n, int) and n == 0):
                            if isinstance(r, int):
                                add(g * ROUNDS - 1, NODES - TOKENS)
                            else:
                                add(g * ROUNDS + r - 1, col - TOKENS)
                        step(n + c, c, s, col)

                over_rounds(dve, g, round_)

            def tail():
                for i, n, q, s, col in steps_of_tail():
                    if i % ROUNDS == 0:
                        dve.wait_ge(gates_loaded[s], 16 * (NE // 2) + 16 * REST_SHARE * (i // ROUNDS // 2 + 1))
                    if i == 2:
                        add(NE * ROUNDS - 1, NODES - TOKENS)
                    if i >= 3:
                        add(NE * ROUNDS + i - 3, (i - 3) % ROUNDS * TOKENS)
                    step(n, q, s, col)
                lo(MAIN + TAIL - 1, CHUNKS - 1)
                for i in range(TAIL - 3, TAIL):
                    add(NE * ROUNDS + i, i % ROUNDS * TOKENS)

            nc.vector.memset(acc_T[:, :, :], 0.0).then_inc(acc_zero, 1)
            dve.wait_ge(acc_zero, 1)
            over_groups(dve, group, tail)


def stage_output(nc, t, keep, out):
    with ExitStack() as ctx:
        m = Memory(nc, ctx, "output")
        residual, const, acc_T = keep["residual"], keep["const"], keep["acc_T"]
        part = [m.sb(f"part{s}", [P, K2, P]) for s in range(2)]
        rows = m.sb("rows", [P, 2, C])
        psum = [m.ps(f"turned{s}") for s in range(2)]
        part_ready, turned, rows_ready = m.sem("part_ready"), m.sem("turned"), m.sem("rows_ready")
        stored = [m.sem(f"stored{s}") for s in range(2)]
        block = ctx.enter_context(nc.Block())
        PAIRS = TILES // 2 - 1

        def over(eng, tile):
            tile(0, 0, 0, P)
            tile(1, 1, 0, P)
            with eng.Fori(1, PAIRS) as i:
                tile(i * 2, 0, i, P)
                tile(i * 2 + 1, 1, i, P)
            tile(TILES - 2, 0, PAIRS, P)
            tile(TILES - 1, 1, PAIRS, LAST)

        def opens(n):
            return isinstance(n, int) and n < 2

        @block.scalar
        def _(act):
            def tile(n, s, use, tall):
                if not opens(n):
                    act.wait_ge(turned, n - 1)
                nc.scalar.activation(part[s][:, :, 0:tall], acc_T[:, :, bass.ds(n * P, tall)], ACT.Copy).then_inc(part_ready, 1)

            over(act, tile)

        @block.tensor
        def _(pe):
            def tile(n, s, use, tall):
                pe.wait_ge(part_ready, n + 1)
                if not opens(n):
                    pe.wait_ge(rows_ready, n - 1)
                for k in range(K2):
                    ins = nc.tensor.transpose(psum[s][0:tall, k * P:(k + 1) * P], part[s][:, k, 0:tall], const[:, IDENT:IDENT + P])
                ins.then_inc(turned, 1)

            over(pe, tile)

        @block.vector
        def _(dve):
            def tile(n, s, use, tall):
                dve.wait_ge(turned, n + 1)
                if not opens(n):
                    dve.wait_ge(stored[s], use * 16)
                nc.vector.tensor_tensor(rows[0:tall, s, :], residual[0:tall, bass.ds(n, 1), :].rearrange("p a c -> p (a c)"), psum[s][0:tall, 0:C],
                                        ALU.add).then_inc(rows_ready, 1)

            over(dve, tile)

        @block.sync
        def _(sp):
            def tile(n, s, use, tall):
                sp.wait_ge(rows_ready, n + 1)
                sp.dma_start(out[bass.ds(n * P, tall), :], rows[0:tall, s, :]).then_inc(stored[s], 16)

            over(sp, tile)
            for s in range(2):
                sp.wait_ge(stored[s], 16 * (TILES // 2))


def program(nc, t, out):
    with ExitStack() as ctx:
        m = Memory(nc, ctx, "kept")
        keep = {"residual": m.sb("residual", [P, TILES, C]), "const": m.sb("const", [P, CONSTANTS]),
                "q_all": m.sb("q_all", [P, TILES, C]),
                "h_rows": nc.dram_tensor("h_rows", (PADDED, H_COLS), F32, kind="Internal").ap(),
                "tokens_hi": nc.dram_tensor("tokens_hi", (P, K2, PADDED), F32, kind="Internal").ap(),
                "tokens_lo": nc.dram_tensor("tokens_lo", (P, K2, PADDED), F32, kind="Internal").ap(),
                "row_numbers": nc.dram_tensor("row_numbers", (P, COLUMNS), I32, kind="Internal").ap(),
                "gate_rows": nc.dram_tensor("gate_rows", (NE, PADDED), F32, kind="Internal").ap()}
        keep["h_table"] = keep["h_rows"].rearrange("n (r c) -> (n r) c", r=RELS)
        keep["z"] = keep["q_all"]
        with ExitStack() as nodes:
            m = Memory(nc, nodes, "nodes")
            keep.update(context=m.sb("context", [P, K2, P + 4]))
            stage_projections(nc, t, keep)
            keep.update(agg_T=m.sb("agg_T", [P, K2, PADDED + WINDOW]), in_window=m.sb("in_window", [P, COLUMNS]),
                        base=m.sb("base", [P, GROUPS], I32), window_iota=m.sb("window_iota", [P, WINDOW]),
                        rows=m.sb("rows", [P, RING, GROUP, C]), slots=[m.sb(f"slot{s}", [P, GROUP], I32) for s in range(RING)])
            stage_edges(nc, t, keep)
            stage_spans(nc, t, keep)
        with ExitStack() as inner:
            m = Memory(nc, inner, "tokens")
            keep.update(h_hi=m.sb("h_hi", [P, K2, NODES], F32R), h_lo=m.sb("h_lo", [P, K2, NODES], F32R))
            keep["acc_T"] = keep["z"][:, :, :].rearrange("p t c -> p (t c)")[:, 0:K2 * NODES].rearrange("p (k n) -> p k n", k=K2)
            stage_experts(nc, t, keep)
            stage_output(nc, t, keep, out)


def attention_arrays(a):
    half = HD // 2
    wq, wk = a["L0_ffn_wq"].reshape(NH, HD, C), a["L0_ffn_wk"].reshape(NKV, HD, C)

    def with_rotated(w):
        return np.concatenate([w, w[:, half:], w[:, :half]], axis=1).transpose(0, 2, 1)

    w1, w3, w2 = (w.transpose(0, 2, 1) for w in (a["L0_ffn_w1"], a["L0_ffn_w3"], a["L0_ffn_w2"]))
    up = np.stack([w1, w3], axis=1)
    whole = CHUNKS * P
    rest_up = np.zeros((REST_GROUPS, 2, C, P), up.dtype)
    rest_down = np.zeros((REST_GROUPS, P, C), w2.dtype)
    for e in range(NE):
        j, at = e // REST_SHARE, e % REST_SHARE * REST
        rest_up[j, :, :, at:at + REST] = up[e, :, :, whole:]
        rest_down[j, at:at + REST] = w2[e, whole:]
    return {
        "up_T": up[..., :whole],
        "down_T": w2[:, :whole],
        "rest_up_T": rest_up,
        "rest_down_T": rest_down,
        "wv_T": a["L0_ffn_wv"].T,
        "wqk_T": np.concatenate([np.concatenate([with_rotated(wk[g:g + 1]), with_rotated(wq[g * NH // NKV:(g + 1) * NH // NKV])]) for g in range(NKV)]),
        "wo_T": a["L0_ffn_wo"].T.reshape(NH, HD, C),
        "router_T": a["L0_ffn_router_w"].T,
        "ln1_w": a["L0_ffn_ln1_w"].reshape(K2, P).T,
        "ln2_w": a["L0_ffn_ln2_w"].reshape(K2, P).T,
        "rope": rope_table(),
    }


def kernel(**inputs):
    import concourse.bacc as bacc
    from concourse.bass_utils import run_bass_kernel_spmd as run

    a = {name: np.asarray(v) for name, v in inputs.items()}
    arrays = {
        "x": a["x"],
        "src_T": a["src"].reshape(COLUMNS, P).T,
        "dst_T": a["dst"].reshape(COLUMNS, P).T,
        "type_T": a["edge_type_8"].reshape(COLUMNS, P).T,
        "basis": a["L0_gnn_basis"],
        "comp": a["L0_gnn_comp"],
        "dense_T": np.concatenate([a["L0_mix_Wkv"].T, a["L0_mix_Wq"].T, a["L0_gnn_loop_weight"]], axis=1),
        "biases": np.stack([a["L0_gnn_bias_param"], a["L0_mix_bproj"]]),
        "proj_T": a["L0_mix_Wproj"].T,
        "constants": constants(),
    }
    arrays.update(attention_arrays(a))
    arrays = {name: np.ascontiguousarray(v) for name, v in arrays.items()}
    nc = bacc.Bacc("TRN2", target_bir_lowering=False, num_devices=1)
    t = {name: nc.dram_tensor(name, v.shape, mybir.dt.from_np(v.dtype), kind="ExternalInput").ap() for name, v in arrays.items()}
    out = nc.dram_tensor("out", (NODES, C), F32, kind="ExternalOutput").ap()
    program(nc, t, out)
    return run(nc, [arrays], core_ids=[0]).results[0]["out"]
```

```python
import math

import concourse.bass as bass
import numpy as np
from concourse import mybir
from contextlib import ExitStack

F32, F32R, I32, U32 = mybir.dt.float32, mybir.dt.float32r, mybir.dt.int32, mybir.dt.uint32
ALU, ACT, AX = mybir.AluOpType, mybir.ActivationFunctionType, mybir.AxisListType

P = 128
NODES, C, EDGES = 2500, 256, 80000
K2 = C // P
TILES = math.ceil(NODES / P)
LAST = NODES - (TILES - 1) * P
PADDED = TILES * P
RELS, BASES = 8, 4
H_COLS = RELS * C
BANK = 512
EPS_LN, EPS_RMS = 1e-5, 1e-6

COLUMNS = EDGES // P
GROUP = 5
GROUPS = COLUMNS // GROUP
RING = 5
WINDOW = 32
GENERAL_WINDOWS = PADDED // BANK

NH, NKV, HD = 4, 2, 64
NE, HID = 8, 682
"""Columns of the table of constants."""
IDENT, BLOCKS, HEADS, ROW0, DUP, MASK, MASK_T = 0, 128, 256, 260, 388, 516, 644
CONSTANTS = 772


def constants():
    t = np.zeros((P, CONSTANTS), np.float32)
    i = np.arange(P)
    t[:, IDENT:IDENT + P] = np.eye(P)
    t[:, BLOCKS:BLOCKS + P] = i[:, None] // 32 == i[None] // 32
    t[:, HEADS:HEADS + 4] = i[:, None] // 32 == np.arange(4)[None]
    t[0, ROW0:ROW0 + P] = 1
    t[:, DUP:DUP + P] = i[:, None] % HD == i[None] % HD
    t[:, MASK:MASK + P] = np.where(i[None] > i[:, None], -1e30, 0)
    t[:, MASK_T:MASK_T + P] = np.where(i[:, None] > i[None], -1e30, 0)
    return t


def rope_table():
    inv = 1.0 / 10000.0 ** (np.arange(0, HD, 2, dtype=np.float32) / HD)
    f = np.outer(np.arange(PADDED, dtype=np.float32), inv)
    emb = np.concatenate([f, f], axis=-1).T
    sign = np.where(np.arange(HD) < HD // 2, -1, 1)[:, None]
    return np.concatenate([np.cos(emb), np.sin(emb) * sign]).astype(np.float32)


class Memory:

    def __init__(self, nc, ctx, stage):
        self.nc, self.ctx, self.stage = nc, ctx, stage

    def sb(self, name, shape, dt=F32):
        return self.ctx.enter_context(self.nc.sbuf_tensor(f"{self.stage}_{name}", shape, dt))

    def ps(self, name, shape=(P, BANK)):
        return self.ctx.enter_context(self.nc.psum_tensor(f"{self.stage}_psum_{name}", list(shape), F32))

    def sem(self, name):
        return self.ctx.enter_context(self.nc.semaphore(f"{self.stage}_{name}"))


def split_product(nc, out, w_hi, w_lo, x_hi, x_lo, first, last):
    n = len(w_hi)
    for k in range(n):
        for j, (w, x) in enumerate(((w_hi[k], x_hi[k]), (w_hi[k], x_lo[k]), (w_lo[k], x_hi[k]))):
            ins = nc.tensor.matmul(out, w, x, start=first and k == 0 and j == 0, stop=last and k == n - 1 and j == 2)
    return ins


def inverse_root(nc, dve, done, count, value, root, inverse, work):
    for out, op in ((inverse, lambda o: nc.vector.reciprocal(o, root)),
                    (work, lambda o: nc.vector.tensor_tensor(o, value, inverse, ALU.mult)),
                    (work, lambda o: nc.vector.tensor_tensor(o, work, inverse, ALU.mult)),
                    (work, lambda o: nc.vector.tensor_scalar(o, work, -0.5, 1.5, ALU.mult, ALU.add)),
                    (inverse, lambda o: nc.vector.tensor_tensor(o, inverse, work, ALU.mult))):
        op(out).then_inc(done, 1)
        count += 1
        dve.wait_ge(done, count)
    return count


SPAN = BANK // P
SPANS = TILES // SPAN
GROUPS_BEFORE = [min(GROUPS, math.ceil(GROUPS * BANK * (j + 1) / NODES + 2)) for j in range(SPANS)]
CONDITIONS = 1 + SPANS


def row_of(tensor, n):
    return tensor[:, bass.ds(n, 1), :].rearrange("p a c -> p (a c)")


def stage_projections(nc, t, keep):
    with ExitStack() as ctx:
        m = Memory(nc, ctx, "proj")
        residual, q_all, context, const, agg_T, in_window, base, window_iota, flag = (
            keep[n] for n in ("residual", "q_all", "context", "const", "agg_T", "in_window", "base", "window_iota", "flag"))
        WIDE = H_COLS + 4 * C
        KV, QL = H_COLS // BANK, H_COLS // BANK + 1
        w_hi, w_lo = m.sb("w_hi", [P, K2, WIDE], F32R), m.sb("w_lo", [P, K2, WIDE], F32R)
        dense = m.sb("dense", [P, K2, 4 * C])
        basis = m.sb("basis", [P, K2, BASES, C])
        comp = m.sb("comp", [P, RELS * BASES])
        rel = m.sb("rel", [P, K2, C])
        stats, mv = m.sb("stats", [P, TILES, 6]), m.sb("mv", [P, TILES, 2])
        std, rstd = m.sb("std", [P, TILES]), m.sb("rstd", [P, TILES])
        var_eps, work = m.sb("var_eps", [P, TILES]), m.sb("work", [P, TILES])
        xn, loop_all = m.sb("xn", [P, 2, C]), m.sb("loop_all", [P, TILES, C])
        x_hi = [m.sb(f"x_hi{s}", [P, K2, P], F32R) for s in range(2)]
        x_lo = [m.sb(f"x_lo{s}", [P, K2, P], F32R) for s in range(2)]
        h_out = m.sb("h_out", [P, 2, 4, BANK])
        k_exp, q_exp = m.sb("k_exp", [P, 2, C]), m.sb("q_exp", [P, 2, C])
        k_row, v_row = m.sb("k_row", [P, 2, C]), m.sb("v_row", [P, 2, K2, P + 1])
        src, dst, typ = m.sb("src", [P, COLUMNS], I32), m.sb("dst", [P, COLUMNS], I32), m.sb("typ", [P, COLUMNS], I32)
        first, base_f = m.sb("first", [P, GROUPS], I32), m.sb("base_f", [P, GROUPS])
        window_iota_i = m.sb("window_iota_i", [P, WINDOW], I32)
        extremes, worst = m.sb("extremes", [P, 2]), m.sb("worst", [P, 2])
        earliest, outside = m.sb("earliest", [P, SPANS - 1]), m.sb("outside", [P, CONDITIONS])
        count, push = m.sb("count", [P, 1]), m.sb("push", [P, 2])
        psum_t = [m.ps(f"t{s}") for s in range(2)]
        banks = [m.ps(f"bank{s}") for s in range(4)]
        psum_c = [m.ps(f"context{k}") for k in range(K2)]

        const_loaded, pad_zero, x_loaded = m.sem("const_loaded"), m.sem("pad_zero"), m.sem("x_loaded")
        basis_loaded, dense_loaded, edges_loaded = m.sem("basis_loaded"), m.sem("dense_loaded"), m.sem("edges_loaded")
        stats_step, std_ready = m.sem("stats_step"), m.sem("std_ready")
        mix_step, dense_hi, dense_lo, rel_hi, rel_lo = (m.sem(n) for n in ("mix_step", "dense_hi", "dense_lo", "rel_hi", "rel_lo"))
        pool_ready = m.sem("pool_ready")
        xn_ready, transposed, hi_ready, lo_ready = (m.sem(n) for n in ("xn_ready", "transposed", "hi_ready", "lo_ready"))
        kv_done, ql_done, chunk_done, h_by_act, h_by_dve = (m.sem(n) for n in ("kv_done", "ql_done", "chunk_done", "h_by_act", "h_by_dve"))
        h_stored = [m.sem(f"h_stored{s}") for s in range(2)]
        relu_done, k_exp_ready, q_exp_ready = m.sem("relu_done"), m.sem("k_exp_ready"), m.sem("q_exp_ready")
        kv_ready, ql_ready, context_done, context_kept = (m.sem(n) for n in ("kv_ready", "ql_ready", "context_done", "context_kept"))
        prep, index_ready, extremes_ready, worst_found, numbers_stored = (
            m.sem(n) for n in ("prep", "index_ready", "extremes_ready", "worst_found", "numbers_stored"))
        block = ctx.enter_context(nc.Block())
        CHUNKS = H_COLS // BANK

        def over_tiles(eng, tile):
            tile(0, 0, 0, True, False)
            with eng.Fori(0, RELS) as i:
                tile(i * 2 + 1, 1, i, False, False)
                tile(i * 2 + 2, 0, i + 1, False, False)
            for n in range(2 * RELS + 1, TILES):
                tile(n, n % 2, n // 2, False, n == TILES - 1)

        @block.sync
        def _(sp):
            sp.dma_start(residual[:, 0:TILES - 1, :], t["x"][0:(TILES - 1) * P, :].rearrange("(t p) c -> p t c", p=P)).then_inc(x_loaded, 16)
            sp.wait_ge(pad_zero, 1)
            sp.dma_start(residual[0:LAST, TILES - 1, :], t["x"][(TILES - 1) * P:NODES, :]).then_inc(x_loaded, 16)
            sp.dma_start(const[:, :], t["constants"]).then_inc(const_loaded, 16)
            for tensor, name in ((src, "src_T"), (typ, "type_T"), (dst, "dst_T")):
                sp.dma_start(tensor[:, :], t[name]).then_inc(edges_loaded, 16)
            sp.dma_start(first[:, :], t["first_targets"].partition_broadcast(P)).then_inc(edges_loaded, 16)
            sp.wait_ge(index_ready, 1)
            sp.dma_start(keep["row_numbers"], src[:, :]).then_inc(numbers_stored, 16)

            def store(n, s, pair, first, last):
                sp.wait_ge(h_by_act, n * 2 + 2)
                sp.wait_ge(h_by_dve, n * 2 + 2)
                sp.dma_start(keep["h_rows"][bass.ds(n * P, P), :], h_out[:, s, :, :].rearrange("p a b -> p (a b)")).then_inc(h_stored[s], 16)

            over_tiles(sp, store)
            for s in range(2):
                sp.wait_ge(h_stored[s], 16 * (TILES // 2))
            sp.wait_ge(numbers_stored, 16)

        @block.gpsimd
        def _(pool):
            nc.gpsimd.memset(v_row[:, :, :, P:P + 1], 1.0)
            nc.gpsimd.iota(window_iota_i[:, :], pattern=[[1, WINDOW]], base=0, channel_multiplier=0).then_inc(pool_ready, 1)
            nc.gpsimd.memset(agg_T[:, :, :], 0.0).then_inc(pool_ready, 1)
            pool.wait_ge(extremes_ready, 1)
            nc.gpsimd.partition_all_reduce(worst[:, :], extremes[:, :], P, bass.bass_isa.ReduceOp.max).then_inc(worst_found, 1)

        @block.scalar
        def _(act):
            act.dma_start(dense[:, :, :], t["dense_T"].rearrange("(k p) o -> p k o", p=P)).then_inc(dense_loaded, 16)
            for b in range(BASES):
                act.dma_start(basis[:, :, b, :], t["basis"][b].rearrange("(k p) o -> p k o", p=P)).then_inc(basis_loaded, 16)
            act.dma_start(comp[:, :], t["comp"].rearrange("r b -> (r b)").partition_broadcast(P)).then_inc(basis_loaded, 16)
            act.wait_ge(dense_loaded, 16)
            nc.scalar.activation(w_hi[:, :, H_COLS:WIDE], dense[:, :, :], ACT.Copy).then_inc(dense_hi, 1)
            act.wait_ge(stats_step, 2 * TILES + 1)
            nc.scalar.activation(std[:, :], var_eps[:, :], ACT.Sqrt).then_inc(std_ready, 1)

            def hi(q, s):
                act.wait_ge(transposed, q + 1)
                nc.scalar.activation(x_hi[s][:, :, :], psum_t[s][:, 0:C].rearrange("p (k c) -> p k c", k=K2), ACT.Copy).then_inc(hi_ready, 1)

            def elu_exp(bank, out, n, which, ready):
                nc.scalar.activation(out, bank, ACT.Relu, scale=-1.0).then_inc(relu_done, 1)
                act.wait_ge(relu_done, n * 2 + which)
                nc.scalar.activation(out, out, ACT.Exp, scale=-1.0).then_inc(ready, 1)

            def attention_tile(n, s, pair, first, last):
                hi(n + 1, 1 - s)
                if s == 0 and not isinstance(n, int):
                    act.wait_ge(mix_step, pair * BASES)
                    nc.scalar.activation(w_hi[:, :, bass.ds((pair - 1) * C, C)], rel[:, :, :], ACT.Copy).then_inc(rel_hi, 1)
                act.wait_ge(kv_done, n + 1)
                if not first:
                    act.wait_ge(kv_ready, n - 1)
                elu_exp(banks[2 * s][:, 0:C], k_exp[:, s, :], n, 1, k_exp_ready)
                act.wait_ge(ql_done, n + 1)
                if not first:
                    act.wait_ge(ql_ready, n - 1)
                elu_exp(banks[2 * s + 1][:, 0:C], q_exp[:, s, :], n, 2, q_exp_ready)

            def relation_tile(n, s, pair, first, last):
                for c in (0, 2):
                    act.wait_ge(chunk_done, n * CHUNKS + c + 1)
                    if c == 0 and not first:
                        act.wait_ge(h_stored[s], pair * 16)
                    nc.scalar.activation(h_out[:, s, c, :], banks[c][:, :], ACT.Copy).then_inc(h_by_act, 1)
                    if c == 0 and not last:
                        hi(n + (TILES + 1), 1 - s)

            hi(0, 0)
            over_tiles(act, attention_tile)
            over_tiles(act, relation_tile)

        @block.tensor
        def _(pe):
            pe.wait_ge(const_loaded, 16)
            ident = const[:, IDENT:IDENT + P]

            def transposes(q, s):
                pe.wait_ge(xn_ready, q + 1)
                if not (isinstance(q, int) and q < 2):
                    pe.wait_ge(lo_ready, q - 1)
                for k in range(K2):
                    ins = nc.tensor.transpose(psum_t[s][:, k * P:(k + 1) * P], xn[:, s, k * P:(k + 1) * P], ident)
                ins.then_inc(transposed, 1)

            def context_products(n, s, first, last):
                pe.wait_ge(kv_ready, n + 1)
                rows = LAST if last else P
                for k in range(K2):
                    ins = nc.tensor.matmul(psum_c[k][:, 0:P + 1], k_row[0:rows, s, k * P:(k + 1) * P], v_row[0:rows, s, k, :], start=first, stop=last)
                ins.then_inc(context_done, 1)

            def chunk(s, c, bank, done):
                cols = slice(c * BANK, (c + 1) * BANK)
                split_product(nc, banks[bank][:, :], [x_hi[s][:, k, :] for k in range(K2)], [x_lo[s][:, k, :] for k in range(K2)],
                              [w_hi[:, k, cols] for k in range(K2)], [w_lo[:, k, cols] for k in range(K2)], True, True).then_inc(done, 1)

            def attention_tile(n, s, pair, first, last):
                pe.wait_ge(lo_ready, n + 1)
                if not first:
                    pe.wait_ge(kv_ready, n - 1)
                chunk(s, KV, 2 * s, kv_done)
                transposes(n + 1, 1 - s)
                if not first:
                    pe.wait_ge(ql_ready, n - 1)
                chunk(s, QL, 2 * s + 1, ql_done)
                if not first:
                    context_products(n - 1, 1 - s, isinstance(n, int) and n == 1, False)

            def relation_tile(n, s, pair, first, last):
                pe.wait_ge(lo_ready, n + (TILES + 1))
                for c in range(CHUNKS):
                    if first:
                        pe.wait_ge(kv_ready if c % 2 == 0 else ql_ready, TILES - 1 + c // 2)
                    else:
                        pe.wait_ge((h_by_act, h_by_dve)[c % 2], n * 2 - (c < 2))
                    chunk(s, c, c, chunk_done)
                    if c == 1 and not last:
                        transposes(n + (TILES + 1), 1 - s)

            transposes(0, 0)
            pe.wait_ge(dense_lo, 1)
            attention_tile(0, 0, 0, True, False)
            attention_tile(1, 1, 0, False, False)
            with pe.Fori(1, TILES // 2) as i:
                attention_tile(i * 2, 0, i, False, False)
                attention_tile(i * 2 + 1, 1, i, False, False)
            context_products(TILES - 1, (TILES - 1) % 2, False, True)
            pe.wait_ge(rel_lo, RELS)
            over_tiles(pe, relation_tile)

        @block.vector
        def _(dve):
            nc.vector.memset(residual[:, TILES - 1, :], 0.0).then_inc(pad_zero, 1)
            dve.wait_ge(dense_hi, 1)
            nc.vector.tensor_tensor(w_lo[:, :, H_COLS:WIDE], dense[:, :, :], w_hi[:, :, H_COLS:WIDE].bitcast(F32), ALU.subtract).then_inc(dense_lo, 1)
            dve.wait_ge(x_loaded, 32)
            for n in range(TILES):
                nc.vector.bn_stats(stats[:, n, :], residual[:, n, :]).then_inc(stats_step, 1)
            dve.wait_ge(stats_step, TILES)
            for n in range(TILES):
                nc.vector.bn_aggr(mv[:, n, :], stats[:, n, :]).then_inc(stats_step, 1)
            dve.wait_ge(stats_step, 2 * TILES)
            nc.vector.tensor_scalar(var_eps[:, :], mv[:, :, 1], EPS_LN, None, ALU.add).then_inc(stats_step, 1)
            dve.wait_ge(std_ready, 1)
            inverse_root(nc, dve, stats_step, 2 * TILES + 1, var_eps[:, :], std[:, :], rstd[:, :], work[:, :])

            def normalise(n, s):
                nc.vector.tensor_scalar(xn[:, s, :], row_of(residual, n), mv[:, bass.ds(n, 1), 0], rstd[:, bass.ds(n, 1)],
                                        ALU.subtract, ALU.mult).then_inc(xn_ready, 1)

            def lo(q, s):
                dve.wait_ge(hi_ready, q + 1)
                nc.vector.tensor_tensor(x_lo[s][:, :, :], psum_t[s][:, 0:C].rearrange("p (k c) -> p k c", k=K2), x_hi[s][:, :, :].bitcast(F32),
                                        ALU.subtract).then_inc(lo_ready, 1)

            def attention_tile(n, s, pair, first, last):
                lo(n + 1, 1 - s)
                kv, ql = banks[2 * s], banks[2 * s + 1]
                dve.wait_ge(k_exp_ready, n + 1)
                if not first:
                    dve.wait_ge(context_done, n - 1)
                nc.vector.scalar_tensor_tensor(k_row[:, s, :], kv[:, 0:C], 0.0, k_exp[:, s, :], ALU.max, ALU.add)
                nc.vector.tensor_copy(v_row[:, s, :, 0:P], kv[:, C:2 * C].rearrange("p (k c) -> p k c", k=K2)).then_inc(kv_ready, 1)
                dve.wait_ge(q_exp_ready, n + 1)
                nc.vector.scalar_tensor_tensor(row_of(q_all, n), ql[:, 0:C], 0.0, q_exp[:, s, :], ALU.max, ALU.add)
                nc.vector.tensor_copy(row_of(loop_all, n), ql[:, C:2 * C]).then_inc(ql_ready, 1)
                dve.wait_ge(transposed, n + 1)
                normalise(n + 2 - TILES if isinstance(n, int) and n + 2 >= TILES else n + 2, s)
                if s == 1 and not isinstance(n, int):
                    dve.wait_ge(rel_lo, pair)
                    nc.vector.tensor_scalar(rel[:, :, :], basis[:, :, 0, :], comp[:, bass.ds(pair * BASES, 1)], None, ALU.mult).then_inc(mix_step, 1)
                    for b in range(1, BASES):
                        dve.wait_ge(mix_step, pair * BASES + b)
                        nc.vector.scalar_tensor_tensor(rel[:, :, :], basis[:, :, b, :], comp[:, bass.ds(pair * BASES + b, 1)], rel[:, :, :],
                                                       ALU.mult, ALU.add).then_inc(mix_step, 1)
                elif not isinstance(n, int):
                    dve.wait_ge(rel_hi, pair)
                    cols = bass.ds((pair - 1) * C, C)
                    nc.vector.tensor_tensor(w_lo[:, :, cols], rel[:, :, :], w_hi[:, :, cols].bitcast(F32), ALU.subtract).then_inc(rel_lo, 1)

            def index_work():
                dve.wait_ge(edges_loaded, 64)
                nc.vector.scalar_tensor_tensor(src[:, :], src[:, :], float(RELS), typ[:, :], ALU.mult, ALU.add).then_inc(index_ready, 1)
                nc.vector.tensor_copy(base_f[:, :], first[:, :])
                nc.vector.tensor_copy(window_iota[:, :], window_iota_i[:, :]).then_inc(prep, 1)
                dve.wait_ge(prep, 1)
                nc.vector.tensor_tensor(in_window[:, :].rearrange("p (g e) -> p g e", e=GROUP), dst[:, :].rearrange("p (g e) -> p g e", e=GROUP),
                                        base_f[:, :].unsqueeze(2).to_broadcast([P, GROUPS, GROUP]), ALU.subtract).then_inc(prep, 1)
                for j in range(SPANS - 1):
                    nc.vector.tensor_reduce(earliest[:, j:j + 1], base_f[:, GROUPS_BEFORE[j]:GROUPS], AX.X, ALU.min)
                dve.wait_ge(prep, 2)
                nc.vector.tensor_reduce(extremes[:, 0:1], in_window[:, :], AX.X, ALU.max)
                nc.vector.tensor_reduce(extremes[:, 1:2], in_window[:, :], AX.X, ALU.min, negate=True).then_inc(extremes_ready, 1)

            def flag_work():
                dve.wait_ge(worst_found, 1)
                dve.wait_ge(extremes_ready, 1)
                nc.vector.tensor_scalar(outside[:, 0:1], worst[:, 0:1], float(WINDOW), None, ALU.is_ge)
                nc.vector.tensor_scalar(outside[:, 1:2], worst[:, 1:2], 0.0, None, ALU.is_gt)
                for j in range(SPANS - 1):
                    ins = nc.vector.tensor_scalar(outside[:, 2 + j:3 + j], earliest[:, j:j + 1], float((j + 1) * BANK), None, ALU.is_lt)
                ins.then_inc(prep, 1)
                dve.wait_ge(prep, 3)
                nc.vector.tensor_reduce(count[:, :], outside[:, :], AX.X, ALU.add).then_inc(prep, 1)
                dve.wait_ge(prep, 4)
                nc.vector.tensor_copy(flag[:, :], count[:, :])
                nc.vector.tensor_scalar(push[:, 0:1], count[:, :], -4.0 * PADDED, None, ALU.mult)
                nc.vector.tensor_scalar(push[:, 1:2], count[:, :], float(PADDED), None, ALU.mult).then_inc(prep, 1)
                dve.wait_ge(prep, 5)
                nc.vector.tensor_scalar(in_window[:, :], in_window[:, :], push[:, 0:1], None, ALU.add)
                nc.vector.tensor_scalar(base[:, :], base_f[:, :], push[:, 1:2], float(PADDED), ALU.add, ALU.min).then_inc(prep, 1)

            def relation_tile(n, s, pair, first, last):
                if not (isinstance(n, int) and n + 2 >= TILES):
                    dve.wait_ge(transposed, n + (TILES + 1))
                    normalise(n + 2, s)
                row = row_of(residual, n)
                if first:
                    dve.wait_ge(xn_ready, TILES + 1)
                nc.vector.tensor_tensor(row, row, row_of(loop_all, n), ALU.add)
                for c in (1, 3):
                    dve.wait_ge(chunk_done, n * CHUNKS + c + 1)
                    if c == 1 and not first:
                        dve.wait_ge(h_stored[s], pair * 16)
                    nc.vector.tensor_copy(h_out[:, s, c, :], banks[c][:, :]).then_inc(h_by_dve, 1)
                    if c == 1 and not last:
                        lo(n + (TILES + 1), 1 - s)
                if first:
                    index_work()
                if last:
                    flag_work()

            for n in range(2):
                normalise(n, n)
            dve.wait_ge(pool_ready, 1)
            dve.wait_ge(basis_loaded, 16 * (BASES + 1))
            lo(0, 0)
            over_tiles(dve, attention_tile)
            dve.wait_ge(context_done, TILES)
            for k in range(K2):
                nc.vector.tensor_tensor(context[:, k, 0:P], psum_c[k][:, 0:P], const[:, BLOCKS:BLOCKS + P], ALU.mult)
                nc.vector.tensor_scalar(context[:, k, P:P + 4], const[:, HEADS:HEADS + 4], psum_c[k][:, P:P + 1], None, ALU.mult).then_inc(context_kept, 1)
            over_tiles(dve, relation_tile)
            dve.wait_ge(pool_ready, 2)


def stage_scattered(nc, t, keep):
    with ExitStack() as ctx:
        m = Memory(nc, ctx, "scattered")
        agg_T, row_numbers, rows, slots, flag = (keep[n] for n in ("agg_T", "row_numbers", "rows", "slots", "flag"))
        dst, dst_f = m.sb("dst", [P, COLUMNS], I32), m.sb("dst_f", [P, COLUMNS])
        iota_i, iota = m.sb("iota_i", [P, PADDED], I32), m.sb("iota", [P, PADDED])
        wide_hot = m.sb("wide_hot", [P, BANK])
        psum = [m.ps(f"sum{k}") for k in range(K2)]
        targets_loaded, iota_made, ready, slot_filled, gathered, group_used, gather_turns = (
            m.sem(n) for n in ("targets_loaded", "iota_made", "ready", "slot_filled", "gathered", "group_used", "gather_turns"))
        wide_ready, wide_used, wide_added = m.sem("wide_ready"), m.sem("wide_used"), m.sem("wide_added")
        block = ctx.enter_context(nc.Block())

        def failed(eng):
            return eng.value_load(flag[0:1, 0:1], min_val=0, max_val=CONDITIONS)

        @block.sync
        def _(sp):
            with sp.If(failed(sp) > 0):
                sp.dma_start(dst[:, :], t["dst_T"]).then_inc(targets_loaded, 16)
                with sp.Fori(0, GROUPS) as g:
                    sp.wait_ge(gathered, g * (16 * GROUP))
                    sp.dma_start(slots[0][:, :], row_numbers[:, bass.ds(g * GROUP, GROUP)]).then_inc(slot_filled, 16)

        @block.gpsimd
        def _(pool):
            last_row = pool.to_reg(PADDED * RELS - 1)
            with pool.If(failed(pool) > 0):
                nc.gpsimd.iota(iota_i[:, :], pattern=[[1, PADDED]], base=0, channel_multiplier=0).then_inc(iota_made, 1)
                with pool.Fori(0, GROUPS) as g:
                    pool.wait_ge(slot_filled, g * 16 + 16)
                    pool.wait_ge(group_used, g)
                    pool.sem_inc(gather_turns, 1)
                    for e in range(GROUP):
                        pool.indirect_dma_start(out=rows[:, 0, e, :], out_offset=None, in_=keep["h_table"],
                                                in_offset=bass.IndirectOffsetOnAxis(ap=slots[0][:, e:e + 1], axis=0),
                                                bounds_check=last_row, oob_is_err=True).then_inc(gathered, 16)

        @block.tensor
        def _(pe):
            with pe.If(failed(pe) > 0):
                with pe.Fori(0, GROUPS) as g:
                    with pe.Fori(0, GENERAL_WINDOWS) as w:
                        for e in range(GROUP):
                            pe.wait_ge(wide_ready, g * (GENERAL_WINDOWS * GROUP) + w * GROUP + (e + 1))
                            if e == 0:
                                pe.wait_ge(gathered, g * (16 * GROUP) + 16 * GROUP)
                                pe.wait_ge(wide_added, g * GENERAL_WINDOWS + w)
                            for k in range(K2):
                                ins = nc.tensor.matmul(psum[k][:, :], rows[:, 0, e, k * P:(k + 1) * P], wide_hot[:, :], start=e == 0, stop=e == GROUP - 1)
                            ins.then_inc(wide_used, 1)
                    pe.wait_ge(wide_used, g * (GENERAL_WINDOWS * GROUP) + GENERAL_WINDOWS * GROUP)
                    pe.sem_inc(group_used, 1)

        @block.vector
        def _(dve):
            with dve.If(failed(dve) > 0):
                dve.wait_ge(targets_loaded, 16)
                nc.vector.tensor_copy(dst_f[:, :], dst[:, :])
                dve.wait_ge(iota_made, 1)
                nc.vector.tensor_copy(iota[:, :], iota_i[:, :]).then_inc(ready, 1)
                dve.wait_ge(ready, 1)
                with dve.Fori(0, GROUPS) as g:
                    with dve.Fori(0, GENERAL_WINDOWS) as w:
                        for e in range(GROUP):
                            dve.wait_ge(wide_used, g * (GENERAL_WINDOWS * GROUP) + w * GROUP + e)
                            nc.vector.tensor_scalar(wide_hot[:, :], iota[:, bass.ds(w * BANK, BANK)], dst_f[:, bass.ds(g * GROUP + e, 1)], None,
                                                    ALU.is_equal).then_inc(wide_ready, 1)
                        dve.wait_ge(wide_used, g * (GENERAL_WINDOWS * GROUP) + w * GROUP + GROUP)
                        dve.wait_ge(wide_added, g * GENERAL_WINDOWS + w)
                        for k in range(K2):
                            place = agg_T[:, k, bass.ds(w * BANK, BANK)]
                            ins = nc.vector.tensor_tensor(place, place, psum[k][:, :], ALU.add)
                        ins.then_inc(wide_added, 1)


SPAN_HEADS = NH * SPANS
MIX_ROUNDS = TILES // RING
LOOPED = GROUPS_BEFORE[0] // RING * RING


COST = {"scores": 0.33, "values": 0.67, "keep": 0, "gap": 0, "combine": 0.4, "turn": 0.4, "weights": 0, "key_weights": 0, "rope": 0,
        "out": 0.7, "maxima": 0.25, "project": 1, "key_project": 1, "double": 0.7, "key_double": 0.7, "v": 2, "sum": 0.8}
ARRIVAL = 2.5


def span_steps(j):
    return SPAN * (j + 1)


def rows_items(j):
    chain = ("sums", "normal", "squares", "value_2", "h", "h_turn", "h_hi", "h_lo", "v", "v_keep")
    return ([("rope", j)] + [("key_weights", j, kv) for kv in range(NKV)] + [(name, j) for name in chain] +
            [(name, j, kv) for kv in range(NKV) for name in ("key_project", "key_double")])


def prepare_items(m):
    return ([("weights", m), ("project", m), ("double", m), ("gap",)] + [("maxima", m, n, c) for n in range(SPAN) for c in range(m // NH + 1)] +
            [("combine", m), ("turn", m), ("gap",)])


def late_items(j):
    return [(name, j) for name in ("late_squares", "late_value", "late_rows")], [
        (name, j) for name in ("late_turn", "late_hi", "late_lo", "late_logits", "late_exp", "late_pick", "late_gates")]


def shares(items, places):
    cost = [0.4 if what[0] == "maxima" else 0.1 if what[0].endswith("weights") else 1 for what in items]
    out, spent = [[] for _ in range(places)], 0
    for what, c in zip(items, cost):
        out[min(places - 1, int(spent * places / (sum(cost) + 1e-9)))].append(what)
        spent += c
    return out


def span_order():
    order = [("hot", LOOPED)]
    clock, ended, arrival = 0, [0] * LOOPED, [0] * (LOOPED + 1)

    def do(items):
        nonlocal clock
        for what in items:
            order.append(what)
            clock += COST.get(what[0], 0.8)
            if len(ended) < GROUPS and arrival[-1] <= clock:
                add_group()

    def add_group():
        nonlocal clock
        g = len(ended)
        clock = max(clock, arrival[g]) + COST["sum"]
        order.append(("sum", g))
        ended.append(clock)
        if g + 1 < GROUPS:
            order.append(("hot", g + 1))
            arrival.append(max(arrival[g], ended[g + 1 - RING]) + ARRIVAL)

    while len(ended) < GROUPS_BEFORE[0]:
        add_group()
    do(rows_items(0))
    do(prepare_items(0))
    before = None
    for m in range(SPAN_HEADS):
        j, turn = divmod(m, NH)
        ahead = [("out", m - 1, 0), ("out", m - 1, 1)] if m else []
        if turn == NH - 1 and j + 1 < SPANS:
            ahead += rows_items(j + 1)
        if m + 1 < SPAN_HEADS:
            ahead += prepare_items(m + 1)
        if j and turn < 2:
            ahead += late_items(j - 1)[turn]
        if turn == NH - 1 and j + 1 < SPANS:
            while len(ended) < GROUPS_BEFORE[j + 1]:
                add_group()
        steps = span_steps(j)
        ahead = shares(ahead, 2 * (steps - 1))
        for i in range(steps):
            do([("scores", m, i)])
            if i:
                do(ahead[2 * i - 2])
            if before:
                do([("values",) + before])
            if i:
                do(ahead[2 * i - 1])
            elif m:
                do([("keep", m - 1)])
            before = (m, i)
    first, second = late_items(SPANS - 1)
    return order + [("values",) + before, ("keep", SPAN_HEADS - 1), ("out", SPAN_HEADS - 1, 0), ("out", SPAN_HEADS - 1, 1)] + first + second


def stage_spans(nc, t, keep):
    with ExitStack() as ctx:
        m = Memory(nc, ctx, "spans")
        residual, const, agg_T, context, z = keep["residual"], keep["const"], keep["agg_T"], keep["context"], keep["q_all"]
        q_all = z
        row_numbers, in_window, base, rows, slots, window_iota = (keep[n] for n in ("row_numbers", "in_window", "base", "rows", "slots", "window_iota"))
        hot = m.sb("hot", [P, GROUP, WINDOW])
        late_h = m.sb("late_h", [P, SPAN, C])
        proj, biases = late_h[:, 0:2, :], late_h[:, 2:4, :]
        late_hi, late_lo = m.sb("late_hi", [P, K2, BANK], F32R), m.sb("late_lo", [P, K2, BANK], F32R)
        gates_T = late_h[:, :, :].rearrange("p a c -> p (a c)")[0:NE, 0:BANK]
        den = m.sb("den", [P, 2, 8])
        rope = m.sb("rope", [P, BANK])
        raw_w = m.sb("raw_w", [P, NKV + NH, K2, P])
        w_hi, w_lo = ([m.sb(f"w_{x}{s}", [P, K2, P], F32R) for s in range(2)] for x in ("hi", "lo"))
        wv_hi, wv_lo = m.sb("wv_hi", [P, K2, P], F32R), m.sb("wv_lo", [P, K2, P], F32R)
        norm_w, norm2_w = m.sb("norm_w", [P, K2]), m.sb("norm2_w", [P, K2])
        router = m.sb("router", [P, K2, NE])
        router_hi, router_lo = m.sb("router_hi", [P, K2, NE], F32R), m.sb("router_lo", [P, K2, NE], F32R)
        logits, top, probs_e, index_u = m.sb("logits", [P, SPAN, NE]), m.sb("top", [P, SPAN, NE]), m.sb("probs_e", [P, SPAN, NE]), m.sb("index_u", [P, SPAN, NE], U32)
        index, gates = logits, top
        hit = m.sb("hit", [P, 2, SPAN, NE])
        peak, total, scale, pair = m.sb("peak", [P, SPAN]), m.sb("total", [P, SPAN]), m.sb("scale", [P, SPAN]), m.sb("pair", [P, SPAN, 2])
        h_hi, h_lo = m.sb("h_hi", [P, K2, BANK], F32R), m.sb("h_lo", [P, K2, BANK], F32R)
        rotated = m.sb("rotated", [P, 2, BANK])
        q_both = [m.sb(f"q_both{s}", [P, BANK], F32R) for s in range(NKV)]
        q_max = [m.sb(f"q_max{s}", [HD + 2, BANK], F32R) for s in range(NKV)]
        k_hi = [m.sb(f"k_hi{s}", [P, PADDED], F32R) for s in range(NKV)]
        k_lo = [m.sb(f"k_lo{s}", [HD + 2, PADDED], F32R) for s in range(NKV)]
        v = m.sb("v", [P, NKV, TILES, HD + 1])
        wo = m.sb("wo", [HD + 1, NH, C + 1])
        probs = m.sb("probs", [P, 2, BANK])
        y_T = m.sb("y_T", [HD + 1, BANK])
        neg = m.sb("neg", [P, NKV, SPAN, SPANS])
        neg_max, neg_hi = m.sb("neg_max", [P, SPAN]), m.sb("neg_hi", [P, SPAN], F32R)
        columns = m.sb("columns", [P, SPAN, P])
        inverse = m.sb("inverse", [P, 2])
        stats, mv = m.sb("stats", [P, SPAN, 6]), m.sb("mv", [P, SPAN, 2])
        value, inv, work = (m.sb(n, [P, 3, SPAN]) for n in ("value", "inv", "work"))
        mean_sq = m.sb("mean_sq", [P, 2, SPAN])
        ident_r, mask, mask_T = m.sb("ident_r", [P, P], F32R), m.sb("mask", [P, P], F32R), m.sb("mask_T", [P, P], F32R)
        h = rotated[:, :, :].rearrange("p a (b c) -> p (a b) c", c=C)
        q_row, attn = h[:, 0, :], h[:, 2, :]
        q_T, attn_T = (probs[:, s, 0:C].rearrange("p (k c) -> p k c", k=K2) for s in range(2))
        ident = const[:, IDENT:IDENT + P]

        p_sum = m.ps("sum")
        p_max = [m.ps(f"max{s}") for s in range(2)]
        p_score = [m.ps(f"score{s}") for s in range(2)]
        p_y, p_a, p_b = m.ps("y"), m.ps("a"), m.ps("b")
        outs = (p_a, p_b)
        pq, pa, pm = p_score[0], p_a, p_b

        slot_filled = [m.sem(f"slot_filled{s}") for s in range(RING)]
        gathered = [m.sem(f"gathered{s}") for s in range(RING)]
        gather_turns, hot_ready, summed, added = (m.sem(n) for n in ("gather_turns", "hot_ready", "summed", "added"))
        proj_loaded, v_weights_loaded, weights_loaded, wo_loaded = (
            m.sem(n) for n in ("proj_loaded", "v_weights_loaded", "weights_loaded", "wo_loaded"))
        rope_loaded = m.sem("rope_loaded")
        q_copied, q_turned, q_T_ready, attended, den_step, attn_ready, attn_turned, attn_T_ready, mixed, mix_added = (
            m.sem(n) for n in ("q_copied", "q_turned", "q_T_ready", "attended", "den_step", "attn_ready", "attn_turned", "attn_T_ready", "mixed", "mix_added"))
        ready, cleared, wv_hi_ready, wv_lo_ready = (m.sem(n) for n in ("ready", "cleared", "wv_hi_ready", "wv_lo_ready"))
        agg_turned, agg_added, norm_step, z_ready, squared, h_ready, h_turned, hi_ready, lo_ready, v_done, v_kept = (
            m.sem(n) for n in ("agg_turned", "agg_added", "norm_step", "z_ready", "squared", "h_ready", "h_turned", "hi_ready",
                               "lo_ready", "v_done", "v_kept"))
        late_squared, late_h_ready, late_turned, late_hi_ready, late_lo_ready = (
            m.sem(n) for n in ("late_squared", "late_h_ready", "late_turned", "late_hi_ready", "late_lo_ready"))
        late_stored, logits_done, peak_taken, exps_ready, gates_ready, gates_turned, gates_kept, gates_stored = (
            m.sem(n) for n in ("late_stored", "logits_done", "peak_taken", "exps_ready", "gates_ready", "gates_turned", "gates_kept", "gates_stored"))
        w_hi_ready, w_lo_ready, projected, rotated_ready, doubled, part_hi, part_lo = (
            m.sem(n) for n in ("w_hi_ready", "w_lo_ready", "projected", "rotated_ready", "doubled", "part_hi", "part_lo"))
        max_done, max_free, max_step, turned, maxima_ready = (m.sem(n) for n in ("max_done", "max_free", "max_step", "turned", "maxima_ready"))
        score_done, score_free, probs_free, y_ready, out_done, out_step, out_free = (
            m.sem(n) for n in ("score_done", "score_free", "probs_free", "y_ready", "out_done", "out_step", "out_free"))
        block = ctx.enter_context(nc.Block())

        PER_KV = NH // NKV
        PROJECTIONS = NKV + NH
        COMBINE = 4
        ORDER = span_order()

        def steps_before(m):
            j, turn = divmod(m, NH)
            return NH * SPAN * j * (j + 1) // 2 + (turn * span_steps(j) if turn else 0)

        def number_of(m):
            return m // NH * PROJECTIONS + NKV + m % NH

        def place_of(m):
            return m % NKV * (1 + PER_KV) + 1 + m % NH // NKV

        def over_spans(eng, mix, sum_, setup, do):
            with eng.Fori(0, MIX_ROUNDS) as i:
                for s in range(RING):
                    mix(i, s)
            setup()
            with eng.Fori(MIX_ROUNDS, LOOPED // RING) as i:
                for s in range(RING):
                    sum_(i, s)
            for what, *at in ORDER:
                if what in do:
                    do[what](*at)

        @block.sync
        def _(sp):
            def fill(s, group):
                sp.dma_start(slots[s][:, :], row_numbers[:, bass.ds(group * GROUP, GROUP)]).then_inc(slot_filled[s], 16)

            for s in range(RING):
                fill(s, s)
            with sp.Fori(1, GROUPS // RING) as i:
                for s in range(RING):
                    sp.wait_ge(gathered[s], i * (16 * GROUP))
                    fill(s, i * RING + s)

        @block.gpsimd
        def _(pool):
            last_row = pool.to_reg(PADDED * RELS - 1)

            def gather(s):
                for e in range(GROUP):
                    pool.indirect_dma_start(out=rows[:, s, e, :], out_offset=None, in_=keep["h_table"],
                                            in_offset=bass.IndirectOffsetOnAxis(ap=slots[s][:, e:e + 1], axis=0),
                                            bounds_check=last_row, oob_is_err=True).then_inc(gathered[s], 16)

            for s in range(RING):
                pool.wait_ge(slot_filled[s], 16)
                gather(s)
            with pool.Fori(1, GROUPS // RING) as i:
                for s in range(RING):
                    pool.wait_ge(slot_filled[s], i * 16 + 16)
                    pool.wait_ge(summed, i * RING + (s - RING + 1))
                    pool.sem_inc(gather_turns, 1)
                    gather(s)

        @block.scalar
        def _(act):
            act.sem_inc(score_free, 2)
            act.dma_start(proj[:, :, :], t["proj_T"].rearrange("(k p) o -> p k o", p=P)).then_inc(proj_loaded, 16)
            act.dma_start(biases[:, :, :], t["biases"].partition_broadcast(P)).then_inc(proj_loaded, 16)

            for tensor, name in ((norm_w, "ln1_w"), (norm2_w, "ln2_w")):
                act.dma_start(tensor[:, :], t[name]).then_inc(v_weights_loaded, 16)
            act.dma_start(router[:, :, :], t["router_T"].rearrange("(k p) o -> p k o", p=P)).then_inc(v_weights_loaded, 16)
            act.dma_start(raw_w[:, 0, :, :], t["wv_T"].rearrange("(k p) o -> p k o", p=P)).then_inc(v_weights_loaded, 16)
            act.dma_start(wo[0:HD, :, 0:C], t["wo_T"].rearrange("g d c -> d g c")).then_inc(wo_loaded, 16)

            def mix(i, s):
                n = i * RING + s
                act.wait_ge(q_turned, n)
                nc.scalar.activation(q_row, row_of(q_all, n), ACT.Copy).then_inc(q_copied, 1)
                act.wait_ge(q_turned, n + 1)
                nc.scalar.activation(q_T, pq[:, 0:C].rearrange("p (k c) -> p k c", k=K2), ACT.Copy).then_inc(q_T_ready, 1)
                act.wait_ge(attn_turned, n + 1)
                nc.scalar.activation(attn_T, pq[:, C:2 * C].rearrange("p (k c) -> p k c", k=K2), ACT.Copy).then_inc(attn_T_ready, 1)

            def split_hi(number, place):
                if number >= 2:
                    act.wait_ge(projected, number - 1)
                nc.scalar.activation(w_hi[number % 2][:, :, :], raw_w[:, place, :, :], ACT.Copy).then_inc(w_hi_ready, 1)

            def parts(number, scale, outputs):
                act.wait_ge(doubled, number + 1)
                for out in outputs:
                    ins = nc.scalar.activation(out, p_b[0:out.shape[0], :], ACT.Copy, scale=scale)
                ins.then_inc(part_hi, 1)

            def load_rope(j):
                act.wait_ge(rotated_ready, j * PROJECTIONS)
                act.dma_start(rope[:, :], t["rope"][:, j * BANK:(j + 1) * BANK]).then_inc(rope_loaded, 16)

            def squares(j):
                for n in range(SPAN):
                    act.wait_ge(z_ready, j * SPAN + n + 1)
                    nc.scalar.activation(h[:, n, :], z[:, j * SPAN + n, :], ACT.Square, accum_out=mean_sq[:, 0, n:n + 1]).then_inc(squared, 1)

            def take_hi(out, weight, done, ready, j):
                for s in range(2):
                    act.wait_ge(done, j * 2 + s + 1)
                    for k in range(K2):
                        ins = nc.scalar.activation(out[:, k, s * C:(s + 1) * C].rearrange("p (t c) -> p t c", t=2),
                                                   p_max[s][:, :].rearrange("p (t k c) -> p t k c", t=2, k=K2)[:, :, k, :], ACT.Copy, scale=weight[:, k:k + 1])
                    ins.then_inc(ready, 1)

            def keep_values(j):
                act.wait_ge(v_done, j + 1)
                for kv in range(NKV):
                    ins = nc.scalar.activation(v[:, kv, j * SPAN:(j + 1) * SPAN, 0:HD],
                                               p_max[0][:, :].rearrange("p (t a c) -> p t a c", t=SPAN, a=NKV)[:, :, kv, :], ACT.Copy)
                ins.then_inc(v_kept, 1)

            def exponentials(m, i):
                start = max(0, i - SPAN * (m // NH)) * P
                b = steps_before(m) + i
                act.wait_ge(score_done, b + 1)
                act.wait_ge(probs_free, b + 1)
                nc.scalar.activation(probs[:, i % 2, start:BANK], p_score[i % 2][:, start:BANK], ACT.Exp).then_inc(score_free, 1)

            def take_maxima(m):
                act.wait_ge(turned, m + 1)
                nc.scalar.activation(q_max[m % NKV][HD:HD + 2, :], p_b[HD:HD + 2, :], ACT.Copy).then_inc(maxima_ready, 1)

            def keep_sum(m):
                act.wait_ge(probs_free, steps_before(m + 1) + 2)
                act.wait_ge(out_done, m * SPAN)
                nc.scalar.activation(y_T[:, :], p_y[0:HD + 1, :], ACT.Copy).then_inc(y_ready, 1)

            def late_squares(j):
                act.wait_ge(out_free, SPAN * NH * (j + 1) + 2)
                if j:
                    act.wait_ge(gates_stored, 16 * j)
                for n in range(SPAN):
                    nc.scalar.activation(late_h[:, n, :], z[:, j * SPAN + n, :], ACT.Square, accum_out=mean_sq[:, 1, n:n + 1]).then_inc(late_squared, 1)

            def late_hi_part(j):
                if j:
                    act.wait_ge(late_stored, 32 * j)
                take_hi(late_hi, norm2_w, late_turned, late_hi_ready, j)

            def late_exp(j):
                act.wait_ge(late_lo_ready, 2 * j + 2)
                cols = slice(j * BANK, (j + 1) * BANK)
                act.dma_start(keep["tokens_hi"][:, :, cols], late_hi[:, :, :].bitcast(F32)).then_inc(late_stored, 16)
                act.dma_start(keep["tokens_lo"][:, :, cols], late_lo[:, :, :].bitcast(F32)).then_inc(late_stored, 16)
                act.wait_ge(peak_taken, j + 1)
                nc.scalar.activation(probs_e[:, :, :], logits[:, :, :], ACT.Exp).then_inc(exps_ready, 1)

            def late_gates(j):
                act.wait_ge(gates_turned, j + 1)
                nc.scalar.activation(gates_T, p_max[1][0:NE, :], ACT.Copy).then_inc(gates_kept, 1)
                act.wait_ge(gates_kept, j + 1)
                act.dma_start(keep["gate_rows"][:, j * BANK:(j + 1) * BANK], gates_T).then_inc(gates_stored, 16)

            def setup():
                nc.scalar.activation(mask[:, :], const[:, MASK:MASK + P], ACT.Copy)
                nc.scalar.activation(mask_T[:, :], const[:, MASK_T:MASK_T + P], ACT.Copy)
                nc.scalar.activation(ident_r[:, :], const[:, IDENT:IDENT + P], ACT.Copy).then_inc(ready, 1)
                act.wait_ge(v_weights_loaded, 64)
                nc.scalar.activation(router_hi[:, :, :], router[:, :, :], ACT.Copy)
                nc.scalar.activation(wv_hi[:, :, :], raw_w[:, 0, :, :], ACT.Copy).then_inc(wv_hi_ready, 1)
                act.wait_ge(wv_lo_ready, 1)
                for n in range(PROJECTIONS):
                    act.dma_start(raw_w[:, n, :, :], t["wqk_T"][n].rearrange("(k p) n -> p k n", p=P)).then_inc(weights_loaded, 16)
                act.wait_ge(weights_loaded, 16 * PROJECTIONS)

            over_spans(act, mix, lambda i, s: None, setup, {
                "rope": load_rope, "key_weights": lambda j, kv: split_hi(j * PROJECTIONS + kv, kv * (1 + PER_KV)),
                "squares": squares, 
                "h_hi": lambda j: take_hi(h_hi, norm_w, h_turned, hi_ready, j), "v_keep": keep_values,
                "key_double": lambda j, kv: parts(j * PROJECTIONS + kv, 1.0, [k_hi[kv][:, j * BANK:(j + 1) * BANK]]),
                "weights": lambda m: split_hi(number_of(m), place_of(m)),
                "double": lambda m: parts(number_of(m), HD ** -0.5, [q_both[m % NKV][:, :], q_max[m % NKV][0:HD, :]]),
                "scores": exponentials, "turn": take_maxima, "keep": keep_sum, "late_squares": late_squares, 
                "late_hi": late_hi_part, "late_exp": late_exp, "late_gates": late_gates})
            act.wait_ge(late_stored, 32 * SPANS)
            act.wait_ge(gates_stored, 16 * SPANS)

        @block.tensor
        def _(pe):
            pe.sem_inc(probs_free, 2)
            pe.wait_ge(proj_loaded, 32)


            def sum_(i, s):
                pe.wait_ge(gathered[s], i * (16 * GROUP) + 16 * GROUP)
                pe.wait_ge(hot_ready, i * RING + (s + 1))
                pe.wait_ge(added, i * RING + s)
                for k in range(K2):
                    for e in range(GROUP):
                        ins = nc.tensor.matmul(p_sum[:, k * WINDOW:(k + 1) * WINDOW], rows[:, s, e, k * P:(k + 1) * P], hot[:, e, :],
                                               start=e == 0, stop=e == GROUP - 1)
                ins.then_inc(summed, 1)

            def mix(i, s):
                n = i * RING + s
                pe.wait_ge(q_copied, n + 1)
                for k in range(K2):
                    ins = nc.tensor.transpose(pq[:, k * P:(k + 1) * P], q_row[:, k * P:(k + 1) * P], ident)
                ins.then_inc(q_turned, 1)
                pe.wait_ge(q_T_ready, n + 1)
                for k in range(K2):
                    ins = nc.tensor.matmul(pa[:, k * (P + 4):(k + 1) * (P + 4)], q_T[:, k, :], context[:, k, :], start=True, stop=True)
                ins.then_inc(attended, 1)
                sum_(i, s)
                pe.wait_ge(attn_ready, n + 1)
                for k in range(K2):
                    ins = nc.tensor.transpose(pq[:, C + k * P:C + (k + 1) * P], attn[:, k * P:(k + 1) * P], ident)
                ins.then_inc(attn_turned, 1)
                pe.wait_ge(mix_added, n)
                for one in range(2):
                    nc.tensor.matmul(pm[:, 0:C], const[:, ROW0:ROW0 + P], biases[:, one, :], start=one == 0, stop=False)
                pe.wait_ge(attn_T_ready, n + 1)
                for k in range(K2):
                    ins = nc.tensor.matmul(pm[:, 0:C], attn_T[:, k, :], proj[:, k, :], start=False, stop=k == K2 - 1)
                ins.then_inc(mixed, 1)

            issued = {"maxima": 0, "late": 0}

            def project(number, heads_out):
                s = number % 2
                pe.wait_ge(w_lo_ready, number + 1)
                pe.wait_ge(rotated_ready, number)
                pe.wait_ge(out_free, heads_out * SPAN + 2)
                split_product(nc, p_a[:, :], [w_hi[s][:, k, :] for k in range(K2)], [w_lo[s][:, k, :] for k in range(K2)],
                              [h_hi[:, k, :] for k in range(K2)], [h_lo[:, k, :] for k in range(K2)], True, True).then_inc(projected, 1)

            def double(number):
                pe.wait_ge(rotated_ready, number + 1)
                pe.wait_ge(part_lo, number)
                nc.tensor.matmul(p_b[:, :], const[:, DUP:DUP + P], rotated[:, number % 2, :], start=True, stop=True).then_inc(doubled, 1)

            def maxima_banks_free():
                pe.wait_ge(max_free, issued["maxima"] + 2)
                if issued["late"]:
                    pe.wait_ge(gates_kept, issued["late"])

            def transposes(row, s, done):
                for n in range(2):
                    for k in range(K2):
                        ins = nc.tensor.transpose(p_max[s][:, (n * K2 + k) * P:(n * K2 + k + 1) * P], row(2 * s + n, k), ident)
                ins.then_inc(done, 1)

            def turn_sums(j):
                if j == 0:
                    pe.wait_ge(ready, 1)
                    pe.wait_ge(cleared, 3)
                    pe.wait_ge(wv_lo_ready, 1)
                    pe.wait_ge(wo_loaded, 16)
                pe.wait_ge(added, GROUPS_BEFORE[j])
                maxima_banks_free()
                for s in range(2):
                    transposes(lambda n, k: agg_T[:, k, (SPAN * j + n) * P:(SPAN * j + n + 1) * P], s, agg_turned)

            def turn_h(j):
                for s in range(2):
                    pe.wait_ge(h_ready, j * 2 + s + 1)
                    transposes(lambda n, k: h[:, n, k * P:(k + 1) * P], s, h_turned)

            def value_products(j):
                pe.wait_ge(lo_ready, j * 2 + 2)
                for n in range(SPAN):
                    tile = slice(n * P, (n + 1) * P)
                    ins = split_product(nc, p_max[0][:, tile], [h_hi[:, k, tile] for k in range(K2)], [h_lo[:, k, tile] for k in range(K2)],
                                        [wv_hi[:, k, :] for k in range(K2)], [wv_lo[:, k, :] for k in range(K2)], True, True)
                ins.then_inc(v_done, 1)

            def maxima(m, n, c):
                j, kv = m // NH, m % NKV
                if n == 0 and c == 0:
                    pe.wait_ge(part_lo, number_of(m) + 1)
                    pe.wait_ge(v_kept, j + 1)
                    if issued["late"]:
                        pe.wait_ge(gates_kept, issued["late"])
                a = n * (j + 1) + c
                width = BANK if c < j else (n + 1) * P
                pe.wait_ge(max_free, steps_before(m) + (a + 1))
                bank = p_max[a % 2]
                ins = nc.tensor.matmul(bank[:, 0:width], q_both[kv][:, n * P:(n + 1) * P], k_hi[kv][:, c * BANK:c * BANK + width], start=True, stop=c < j,
                                       skip_group_check=True)
                if c == j:
                    ins = nc.tensor.matmul(bank[:, width - P:width], ident_r[:, :], mask[:, :], start=False, stop=True, skip_group_check=True)
                ins.then_inc(max_done, 1)
                issued["maxima"] += 1

            def turn_maxima(m):
                pe.wait_ge(max_step, m * COMBINE + COMBINE)
                for n in range(SPAN):
                    ins = nc.tensor.transpose(p_b[:, n * P:(n + 1) * P], columns[:, n, :], ident)
                ins.then_inc(turned, 1)

            def scores(m, i):
                j, kv = m // NH, m % NKV
                start = max(0, i - SPAN * j) * P
                if i == 0:
                    pe.wait_ge(maxima_ready, m + 1)
                pe.wait_ge(score_free, steps_before(m) + (i + 1))
                out, keys = p_score[i % 2][:, start:BANK], slice(i * P, (i + 1) * P)
                diagonal = i >= SPAN * j
                nc.tensor.matmul(out, k_hi[kv][:, keys], q_both[kv][:, start:BANK], start=True, stop=False, skip_group_check=True)
                ins = nc.tensor.matmul(out, k_lo[kv][:, keys], q_max[kv][:, start:BANK], start=False, stop=not diagonal, skip_group_check=True)
                if diagonal:
                    ins = nc.tensor.matmul(p_score[i % 2][:, start:start + P], ident_r[:, :], mask_T[:, :], start=False, stop=True, skip_group_check=True)
                ins.then_inc(score_done, 1)

            def values(m, i):
                j = m // NH
                start = max(0, i - SPAN * j) * P
                pe.wait_ge(score_free, steps_before(m) + (i + 3))
                if i == 0:
                    pe.wait_ge(y_ready, m)
                nc.tensor.matmul(p_y[0:HD + 1, start:BANK], v[:, m % NKV, i, :], probs[:, i % 2, start:BANK], start=i == 0,
                                 stop=i == span_steps(j) - 1).then_inc(probs_free, 1)

            def out(m, half):
                pe.wait_ge(y_ready, m + 1)
                for n in range(2 * half, 2 * half + 2):
                    pe.wait_ge(out_free, m * SPAN + (n + 1))
                    nc.tensor.matmul(outs[n % 2][:, 0:C + 1], y_T[:, n * P:(n + 1) * P], wo[:, m % NKV * PER_KV + m % NH // NKV, :],
                                     start=True, stop=True).then_inc(out_done, 1)

            def late_turn(j):
                maxima_banks_free()
                for s in range(2):
                    pe.wait_ge(late_h_ready, j * 2 + s + 1)
                    transposes(lambda n, k: late_h[:, n, k * P:(k + 1) * P], s, late_turned)

            def late_logits(j):
                pe.wait_ge(late_lo_ready, j * 2 + 2)
                for n in range(SPAN):
                    tile = slice(n * P, (n + 1) * P)
                    ins = split_product(nc, p_max[0][:, n * NE:(n + 1) * NE], [late_hi[:, k, tile] for k in range(K2)], [late_lo[:, k, tile] for k in range(K2)],
                                        [router_hi[:, k, :] for k in range(K2)], [router_lo[:, k, :] for k in range(K2)], True, True)
                ins.then_inc(logits_done, 1)

            def late_gates(j):
                pe.wait_ge(gates_ready, j + 1)
                for n in range(SPAN):
                    ins = nc.tensor.transpose(p_max[1][0:NE, n * P:(n + 1) * P], gates[:, n, :], ident)
                ins.then_inc(gates_turned, 1)
                issued["late"] += 1

            over_spans(pe, mix, sum_, lambda: None, {
                "sum": lambda g: sum_(g // RING, g % RING), "sums": turn_sums, "h_turn": turn_h, "v": value_products,
                "key_project": lambda j, kv: project(j * PROJECTIONS + kv, max(0, NH * j - 1)), "key_double": lambda j, kv: double(j * PROJECTIONS + kv),
                "project": lambda m: project(number_of(m), max(0, m - 1)), "double": lambda m: double(number_of(m)), "maxima": maxima, "turn": turn_maxima,
                "scores": scores, "values": values, "out": out, "late_turn": late_turn, "late_logits": late_logits, "late_gates": late_gates})

        @block.vector
        def _(dve):
            dve.sem_inc(max_free, 2)
            dve.sem_inc(out_free, 2)
            nc.vector.memset(wo[0:HD, :, C:C + 1], 0.0)
            nc.vector.memset(wo[HD:HD + 1, :, 0:C], 0.0)
            nc.vector.memset(wo[HD:HD + 1, :, C:C + 1], 1.0).then_inc(cleared, 1)
            nc.vector.memset(v[:, :, :, HD:HD + 1], 1.0).then_inc(cleared, 1)
            for s in range(NKV):
                nc.vector.memset(k_lo[s][HD:HD + 2, :].bitcast(F32), 1.0)
            nc.vector.memset(columns[:, :, :], 0.0).then_inc(cleared, 1)
            def setup():
                dve.wait_ge(wv_hi_ready, 1)
                nc.vector.tensor_tensor(router_lo[:, :, :], router[:, :, :], router_hi[:, :, :].bitcast(F32), ALU.subtract)
                nc.vector.tensor_tensor(wv_lo[:, :, :], raw_w[:, 0, :, :], wv_hi[:, :, :].bitcast(F32), ALU.subtract).then_inc(wv_lo_ready, 1)

            def make_hot(i, s):
                nc.vector.tensor_tensor(hot[:, :, :], window_iota[:, :].unsqueeze(1).to_broadcast([P, GROUP, WINDOW]),
                                        in_window[:, bass.ds((i * RING + s) * GROUP, GROUP)].unsqueeze(2).to_broadcast([P, GROUP, WINDOW]),
                                        ALU.is_equal).then_inc(hot_ready, 1)

            def add_sum(i, s):
                g = i * RING + s
                at = dve.value_load(base[0:1, bass.ds(g, 1)], min_val=0, max_val=PADDED)
                dve.wait_ge(summed, g + 1)
                dve.wait_ge(added, g)
                place = agg_T[:, :, bass.ds(at, WINDOW)]
                nc.vector.tensor_tensor(place, place, p_sum[:, 0:K2 * WINDOW].rearrange("p (k w) -> p k w", k=K2), ALU.add).then_inc(added, 1)

            def sum_(i, s):
                make_hot(i, s)
                add_sum(i, s)

            def mix(i, s):
                n = i * RING + s
                make_hot(i, s)
                dve.wait_ge(attended, n + 1)
                both = pa[:, 0:2 * (P + 4)].rearrange("p (k c) -> p k c", k=K2)
                nc.vector.tensor_scalar(den[:, 0, :].rearrange("p (k c) -> p k c", k=K2), both[:, :, P:P + 4], 1e-6, None, ALU.max).then_inc(den_step, 1)
                dve.wait_ge(den_step, n * 2 + 1)
                nc.vector.reciprocal(den[:, 1, :], den[:, 0, :]).then_inc(den_step, 1)
                dve.wait_ge(den_step, n * 2 + 2)
                for k in range(K2):
                    ins = nc.vector.tensor_tensor(attn[:, k * P:(k + 1) * P].rearrange("p (h e) -> p h e", h=4), both[:, k, 0:P].rearrange("p (h e) -> p h e", h=4),
                                                  den[:, 1, 4 * k:4 * k + 4].unsqueeze(2).to_broadcast([P, 4, 32]), ALU.mult)
                ins.then_inc(attn_ready, 1)
                add_sum(i, s)
                dve.wait_ge(mixed, n + 1)
                row = row_of(residual, n)
                nc.vector.tensor_tensor(row, row, pm[:, 0:C], ALU.add).then_inc(mix_added, 1)

            def split_lo(number, place):
                dve.wait_ge(w_hi_ready, number + 1)
                nc.vector.tensor_tensor(w_lo[number % 2][:, :, :], raw_w[:, place, :, :], w_hi[number % 2][:, :, :].bitcast(F32), ALU.subtract).then_inc(w_lo_ready, 1)

            def rotate(number):
                dve.wait_ge(projected, number + 1)
                if number >= 2:
                    dve.wait_ge(doubled, number - 1)
                nc.vector.tensor_tensor(rotated[:, number % 2, :], p_a[:, :], rope[:, :], ALU.mult).then_inc(rotated_ready, 1)

            chain = [0]

            def then(ins):
                chain[0] += 1
                ins.then_inc(norm_step, 1)
                dve.wait_ge(norm_step, chain[0])

            def root(which):
                x, r, w = value[:, which, :], inv[:, which, :], work[:, which, :]
                then(nc.vector.tensor_scalar(w.bitcast(I32), x.bitcast(I32), 1, None, ALU.logical_shift_right))
                then(nc.vector.tensor_scalar(r.bitcast(I32), w.bitcast(I32), -1.0, float(0x5f3759df), ALU.mult, ALU.add))
                for _ in range(3):
                    then(nc.vector.tensor_tensor(w, r, r, ALU.mult))
                    then(nc.vector.scalar_tensor_tensor(w, w, -0.5, x, ALU.mult, ALU.mult))
                    then(nc.vector.scalar_tensor_tensor(r, w, 1.5, r, ALU.add, ALU.mult))

            def add_sums(j):
                for s in range(2):
                    dve.wait_ge(agg_turned, j * 2 + s + 1)
                    two = residual[:, SPAN * j + 2 * s:SPAN * j + 2 * s + 2, :]
                    nc.vector.tensor_tensor(two, two, p_max[s][:, :].rearrange("p (t c) -> p t c", t=2), ALU.add).then_inc(agg_added, 1)
                for n in range(SPAN):
                    dve.wait_ge(agg_added, j * 2 + n // 2 + 1)
                    ins = nc.vector.bn_stats(stats[:, n, :], residual[:, SPAN * j + n, :])
                then(ins)
                for n in range(SPAN):
                    ins = nc.vector.bn_aggr(mv[:, n, :], stats[:, n, :])
                then(ins)

            def normal(j):
                then(nc.vector.tensor_scalar(value[:, 0, :], mv[:, :, 1], EPS_LN, None, ALU.add))
                root(0)
                for n in range(SPAN):
                    tile = SPAN * j + n
                    nc.vector.tensor_scalar(z[:, tile, :], residual[:, tile, :], mv[:, n, 0:1], inv[:, 0, n:n + 1], ALU.subtract, ALU.mult).then_inc(z_ready, 1)

            def second_value(j):
                dve.wait_ge(squared, SPAN * (j + 1))
                then(nc.vector.tensor_scalar(value[:, 1, :], mean_sq[:, 0, :], 1.0 / C, EPS_RMS, ALU.mult, ALU.add))

            def scaled_rows(j, which, out, ready):
                for n in range(SPAN):
                    ins = nc.vector.tensor_scalar(out[:, n, :], z[:, SPAN * j + n, :], inv[:, which, n:n + 1], None, ALU.mult)
                    if n % 2:
                        ins.then_inc(ready, 1)

            def h_rows(j):
                root(1)
                scaled_rows(j, 1, h, h_ready)

            def take_lo(out, hi, weight, done, ready, j):
                for s in range(2):
                    dve.wait_ge(done, j * 2 + s + 1)
                    cols = slice(s * C, (s + 1) * C)
                    for k in range(K2):
                        ins = nc.vector.scalar_tensor_tensor(out[:, k, cols].rearrange("p (t c) -> p t c", t=2),
                                                             p_max[s][:, :].rearrange("p (t k c) -> p t k c", t=2, k=K2)[:, :, k, :], weight[:, k:k + 1],
                                                             hi[:, k, cols].bitcast(F32).rearrange("p (t c) -> p t c", t=2), ALU.mult, ALU.subtract)
                    ins.then_inc(ready, 1)

            def key_project(j, kv):
                dve.wait_ge(rope_loaded, 16 * (j + 1))
                rotate(j * PROJECTIONS + kv)

            def key_low(j, kv):
                dve.wait_ge(part_hi, j * PROJECTIONS + kv + 1)
                x = slice(j * BANK, (j + 1) * BANK)
                nc.vector.tensor_tensor(k_lo[kv][0:HD, x], p_b[0:HD, :], k_hi[kv][0:HD, x].bitcast(F32), ALU.subtract).then_inc(part_lo, 1)

            def query_low(m):
                dve.wait_ge(part_hi, number_of(m) + 1)
                q = q_both[m % NKV]
                nc.vector.scalar_tensor_tensor(q[HD:P, :], p_b[HD:P, :], HD ** -0.5, q[HD:P, :].bitcast(F32), ALU.mult, ALU.subtract).then_inc(part_lo, 1)

            def maxima(m, n, c):
                j = m // NH
                a = n * (j + 1) + c
                width = BANK if c < j else (n + 1) * P
                dve.wait_ge(max_done, steps_before(m) + (a + 1))
                nc.vector.tensor_reduce(neg[:, m % NKV, n, c:c + 1], p_max[a % 2][:, 0:width], AX.X, ALU.max, negate=True).then_inc(max_free, 1)

            def combine_maxima(m):
                done = m * COMBINE
                dve.wait_ge(max_free, steps_before(m + 1) + 2)
                nc.vector.tensor_reduce(neg_max[:, :], neg[:, m % NKV, :, 0:m // NH + 1], AX.X, ALU.min).then_inc(max_step, 1)
                dve.wait_ge(max_step, done + 1)
                nc.vector.tensor_copy(neg_hi[:, :], neg_max[:, :]).then_inc(max_step, 1)
                dve.wait_ge(max_step, done + 2)
                dve.wait_ge(turned, m)
                nc.vector.tensor_copy(columns[:, :, HD], neg_hi[:, :].bitcast(F32)).then_inc(max_step, 1)
                nc.vector.tensor_tensor(columns[:, :, HD + 1], neg_max[:, :], neg_hi[:, :].bitcast(F32), ALU.subtract).then_inc(max_step, 1)

            def add_output(m, half):
                for n in range(2 * half, 2 * half + 2):
                    done = m * SPAN + (n + 1)
                    one = inverse[:, n % 2:n % 2 + 1]
                    dve.wait_ge(out_done, done)
                    nc.vector.reciprocal(one, outs[n % 2][:, C:C + 1]).then_inc(out_step, 1)
                    dve.wait_ge(out_step, done)
                    row = z[:, SPAN * (m // NH) + n, :]
                    nc.vector.scalar_tensor_tensor(row, outs[n % 2][:, 0:C], one, row, ALU.mult, ALU.add).then_inc(out_free, 1)

            def late_value(j):
                dve.wait_ge(late_squared, SPAN * (j + 1))
                then(nc.vector.tensor_scalar(value[:, 2, :], mean_sq[:, 1, :], 1.0 / C, EPS_RMS, ALU.mult, ALU.add))
                dve.wait_ge(out_free, SPAN * NH * (j + 1) + 2)
                span = slice(SPAN * j, SPAN * (j + 1))
                nc.vector.tensor_tensor(residual[:, span, :], residual[:, span, :], z[:, span, :], ALU.add)

            def late_rows(j):
                root(2)
                scaled_rows(j, 2, late_h, late_h_ready)

            def spread(rows):
                return rows.unsqueeze(2).to_broadcast([P, SPAN, NE])

            def late_peak(j):
                dve.wait_ge(logits_done, j + 1)
                logit = p_max[0][:, 0:SPAN * NE].rearrange("p (t e) -> p t e", e=NE)
                then(nc.vector.tensor_reduce(peak[:, :], logit, AX.X, ALU.max))
                nc.vector.tensor_tensor(logits[:, :, :], logit, spread(peak[:, :]), ALU.subtract).then_inc(peak_taken, 1)

            def late_pick(j):
                dve.wait_ge(exps_ready, j + 1)
                then(nc.vector.tensor_reduce(total[:, :], probs_e[:, :, :], AX.X, ALU.add))
                then(nc.vector.reciprocal(scale[:, :], total[:, :]))
                then(nc.vector.tensor_tensor(probs_e[:, :, :], probs_e[:, :, :], spread(scale[:, :]), ALU.mult))
                for n in range(SPAN):
                    ins = nc.vector.max(top[:, n, :], probs_e[:, n, :])
                then(ins)
                for n in range(SPAN):
                    ins = nc.vector.max_index(index_u[:, n, :], top[:, n, :], probs_e[:, n, :])
                then(ins)
                nc.vector.tensor_copy(index[:, :, :], index_u[:, :, :])
                then(nc.vector.tensor_tensor(total[:, :], top[:, :, 0], top[:, :, 1], ALU.add))
                then(nc.vector.tensor_scalar(total[:, :], total[:, :], 1e-9, None, ALU.add))
                then(nc.vector.reciprocal(scale[:, :], total[:, :]))
                then(nc.vector.tensor_tensor(pair[:, :, :], top[:, :, 0:2], scale[:, :].unsqueeze(2).to_broadcast([P, SPAN, 2]), ALU.mult))
                for one in range(2):
                    ins = nc.vector.tensor_tensor(hit[:, one, :, :], spread(index[:, :, one]), window_iota[:, 0:NE].unsqueeze(1).to_broadcast([P, SPAN, NE]), ALU.is_equal)
                then(ins)
                for one in range(2):
                    ins = nc.vector.tensor_tensor(hit[:, one, :, :], hit[:, one, :, :], spread(pair[:, :, one]), ALU.mult)
                then(ins)
                nc.vector.tensor_tensor(gates[:, :, :], hit[:, 0, :, :], hit[:, 1, :, :], ALU.add).then_inc(gates_ready, 1)

            over_spans(dve, mix, sum_, setup, {
                "hot": lambda g: make_hot(g // RING, g % RING), "sum": lambda g: add_sum(g // RING, g % RING),
                "key_weights": lambda j, kv: split_lo(j * PROJECTIONS + kv, kv * (1 + PER_KV)), "sums": add_sums, "normal": normal,
                "value_2": second_value, "h": h_rows, "h_lo": lambda j: take_lo(h_lo, h_hi, norm_w, hi_ready, lo_ready, j),
                "key_project": key_project, "key_double": key_low,
                "weights": lambda m: split_lo(number_of(m), place_of(m)), "project": lambda m: rotate(number_of(m)),
                "double": query_low, "maxima": maxima, "combine": combine_maxima, "out": add_output,
                "late_value": late_value, "late_rows": late_rows, "late_lo": lambda j: take_lo(late_lo, late_hi, norm2_w, late_hi_ready, late_lo_ready, j),
                "late_logits": late_peak, "late_pick": late_pick})


CHUNKS = HID // P
REST = HID - CHUNKS * P
REST_SHARE = P // REST
REST_GROUPS = math.ceil(NE / REST_SHARE)
TOKENS = 500
ROUNDS = NODES // TOKENS
GROUP_STEPS = ROUNDS * CHUNKS


def stage_experts(nc, t, keep):
    with ExitStack() as ctx:
        m = Memory(nc, ctx, "experts")
        h_hi, h_lo, acc_T = keep["h_hi"], keep["h_lo"], keep["acc_T"]
        raw_up, raw_down = m.sb("raw_up", [P, 2, K2, CHUNKS * P]), m.sb("raw_down", [P, CHUNKS, C])
        up_hi, up_lo = ([m.sb(f"up_{x}{s}", [P, 2, K2, CHUNKS * P], F32R) for s in range(2)] for x in ("hi", "lo"))
        down_hi, down_lo = ([m.sb(f"down_{x}{s}", [P, CHUNKS, C], F32R) for s in range(2)] for x in ("hi", "lo"))
        gate = m.sb("gate", [P, 2, NODES])
        hidden = m.sb("hidden", [P, 3, TOKENS])
        hid_hi, hid_lo = m.sb("hid_hi", [P, CHUNKS, TOKENS], F32R), m.sb("hid_lo", [P, CHUNKS, TOKENS], F32R)
        psum_1, psum_3 = [m.ps(f"one{s}") for s in range(3)], [m.ps(f"three{s}") for s in range(3)]
        psum_o = [m.ps(f"out{k}") for k in range(K2)]
        first_hi_ready, first_ready = m.sem("first_hi_ready"), m.sem("first_ready")
        tokens_loaded = [m.sem(f"tokens_loaded{s}") for s in range(2)]
        raw_loaded, split_turns, split_hi, weights_ready, acc_zero = (m.sem(n) for n in ("raw_loaded", "split_turns", "split_hi", "weights_ready", "acc_zero"))
        gates_loaded = [m.sem(f"gates_loaded{s}") for s in range(2)]
        one_done, three_done, silu_done, multiplied, gated, hi_done, lo_done, down_done, round_done, acc_added = (
            m.sem(n) for n in ("one_done", "three_done", "silu_done", "multiplied", "gated", "hi_done", "lo_done", "down_done", "round_done", "acc_added"))
        block = ctx.enter_context(nc.Block())
        TAIL = REST_GROUPS * ROUNDS
        MAIN = NE * GROUP_STEPS

        def over_groups(eng, group, tail):
            group(0, 0, 0)
            with eng.Fori(0, (NE - 2) // 2) as i:
                group(i * 2 + 1, 1, i)
                group(i * 2 + 2, 0, i + 1)
            group(NE - 1, 1, NE // 2 - 1)
            tail()

        def over_rounds(eng, g, round_):
            round_(g, g * GROUP_STEPS, 0, 0)
            with eng.Fori(1, ROUNDS) as r:
                round_(g, g * GROUP_STEPS + r * CHUNKS, r * TOKENS, r)

        def steps_of_tail():
            for n in range(TAIL):
                yield n, MAIN + n, n % CHUNKS, (n // ROUNDS) % 2, n % ROUNDS * TOKENS

        @block.sync
        def _(sp):
            def load(g, s, uses):
                if not (isinstance(g, int) and g == 0):
                    sp.wait_ge(first_ready, 2)
                    sp.wait_ge(weights_ready, g - 1)
                for w in range(2):
                    sp.dma_start(raw_up[:, w, :, :], t["up_T"][bass.ds(g, 1), w].rearrange("g (k p) n -> p (g k) n", p=P)).then_inc(raw_loaded, 16)
                sp.dma_start(raw_down[:, :, :], t["down_T"][bass.ds(g, 1)].rearrange("g (k p) n -> p (g k) n", p=P)).then_inc(raw_loaded, 16)
                if isinstance(g, int) and g == 0:
                    load_tokens(TOKENS, NODES, tokens_loaded[1])
                if not (isinstance(g, int) and g <= 1):
                    sp.wait_ge(gated, (g - 1) * GROUP_STEPS)
                sp.dma_start(gate[:, s, :], keep["gate_rows"][bass.ds(g, 1), 0:NODES].rearrange("a n -> (a n)").partition_broadcast(P)).then_inc(gates_loaded[s], 16)

            def tail():
                for j in range(REST_GROUPS):
                    g, s = NE + j, j % 2
                    sp.wait_ge(weights_ready, g - 1)
                    for w in range(2):
                        sp.dma_start(raw_up[:, w, :, 0:P], t["rest_up_T"][j, w].rearrange("(k p) n -> p k n", p=P)).then_inc(raw_loaded, 16)
                    sp.dma_start(raw_down[:, 0, :], t["rest_down_T"][j]).then_inc(raw_loaded, 16)
                    sp.wait_ge(gated, (NE - 1) * GROUP_STEPS if j == 0 else MAIN + (j - 1) * ROUNDS)
                    for e in range(REST_SHARE):
                        top = P if e == REST_SHARE - 1 else (e + 1) * REST
                        expert = min(j * REST_SHARE + e, NE - 1)
                        sp.dma_start(gate[e * REST:top, s, :], keep["gate_rows"][expert, 0:NODES].partition_broadcast(top - e * REST)).then_inc(gates_loaded[s], 16)

            def load_tokens(start, end, loaded):
                for tensor, name in ((h_hi, "tokens_hi"), (h_lo, "tokens_lo")):
                    sp.dma_start(tensor[:, :, start:end].bitcast(F32), keep[name][:, :, start:end]).then_inc(loaded, 16)

            load_tokens(0, TOKENS, tokens_loaded[0])
            over_groups(sp, load, tail)

        @block.gpsimd
        def _(pool):
            def split(g, s, chunks):
                if isinstance(g, int) and g == 0:
                    return
                pool.wait_ge(raw_loaded, g * 48 + 48)
                if not (isinstance(g, int) and g <= 1):
                    pool.wait_ge(down_done, (g - 1) * GROUP_STEPS if not isinstance(g, int) or g <= NE else MAIN + (g - NE - 1) * ROUNDS)
                pool.sem_inc(split_turns, 1)
                cols = slice(0, chunks * P)
                nc.gpsimd.tensor_copy(up_hi[s][:, :, :, cols], raw_up[:, :, :, cols])
                nc.gpsimd.tensor_copy(down_hi[s][:, 0:chunks, :], raw_down[:, 0:chunks, :]).then_inc(split_hi, 1)
                pool.wait_ge(split_hi, g)
                for w in range(2):
                    nc.gpsimd.tensor_tensor(up_lo[s][:, w, :, cols], raw_up[:, w, :, cols], up_hi[s][:, w, :, cols].bitcast(F32), ALU.subtract)
                nc.gpsimd.tensor_tensor(down_lo[s][:, 0:chunks, :], raw_down[:, 0:chunks, :], down_hi[s][:, 0:chunks, :].bitcast(F32),
                                        ALU.subtract).then_inc(weights_ready, 1)

            def tail():
                for j in range(REST_GROUPS):
                    split(NE + j, j % 2, 1)

            over_groups(pool, lambda g, s, uses: split(g, s, CHUNKS), tail)

        @block.scalar
        def _(act):
            act.wait_ge(raw_loaded, 48)
            nc.scalar.activation(up_hi[0][:, :, :, :], raw_up[:, :, :, :], ACT.Copy).then_inc(first_hi_ready, 1)
            nc.scalar.activation(down_hi[0][:, :, :], raw_down[:, :, :], ACT.Copy).then_inc(first_hi_ready, 1)

            def silu(n, q):
                act.wait_ge(one_done, n + 1)
                if not (isinstance(n, int) and n < 2):
                    act.wait_ge(lo_done, n - 1)
                nc.scalar.activation(hidden[:, q % 3, :], psum_1[q % 3][:, 0:TOKENS], ACT.Silu).then_inc(silu_done, 1)

            def hi(n, q):
                act.wait_ge(gated, n + 1)
                if not (isinstance(n, int) and n < CHUNKS):
                    act.wait_ge(down_done, n - (CHUNKS - 1))
                nc.scalar.activation(hid_hi[:, q, :], hidden[:, q % 3, :], ACT.Copy).then_inc(hi_done, 1)

            def step(n, q):
                silu(n, q)
                if not (isinstance(n, int) and n == 0):
                    hi(n - 1, (q - 1) % CHUNKS)

            def tail():
                for _, n, q, _, _ in steps_of_tail():
                    step(n, q)
                hi(MAIN + TAIL - 1, CHUNKS - 1)

            def group(g, s, uses):
                over_rounds(act, g, lambda g, n, col, r: [step(n + c, c) for c in range(CHUNKS)])

            over_groups(act, group, tail)

        @block.tensor
        def _(pe):
            def up(n, q, s, c, col):
                if not (isinstance(n, int) and n < 2):
                    pe.wait_ge(multiplied, n - 1)
                cols, x = slice(c * P, (c + 1) * P), bass.ds(col, TOKENS)
                for w, (bank, done) in enumerate(((psum_1, one_done), (psum_3, three_done))):
                    split_product(nc, bank[q % 3][:, 0:TOKENS], [up_hi[s][:, w, k, cols] for k in range(K2)], [up_lo[s][:, w, k, cols] for k in range(K2)],
                                  [h_hi[:, k, x] for k in range(K2)], [h_lo[:, k, x] for k in range(K2)], True, True).then_inc(done, 1)

            def down(n, q, s, c, first, last, rounds):
                pe.wait_ge(lo_done, n + 1)
                if first and not (isinstance(rounds, int) and rounds == 0):
                    pe.wait_ge(acc_added, rounds)
                for k in range(K2):
                    rows = slice(k * P, (k + 1) * P)
                    ins = split_product(nc, psum_o[k][:, 0:TOKENS], [down_hi[s][:, c, rows]], [down_lo[s][:, c, rows]],
                                        [hid_hi[:, q, :]], [hid_lo[:, q, :]], first, last)
                ins.then_inc(down_done, 1)
                if last:
                    pe.wait_ge(down_done, n + 1)
                    pe.sem_inc(round_done, 1)

            def group(g, s, uses):
                if isinstance(g, int) and g == 0:
                    pe.wait_ge(first_ready, 2)
                else:
                    pe.wait_ge(weights_ready, g)

                def round_(g, n, col, r):
                    if isinstance(g, int) and g == 0:
                        pe.wait_ge(tokens_loaded[0 if isinstance(r, int) else 1], 32)
                    for c in range(CHUNKS):
                        up(n + c, c, s, c, col)
                        if c >= 2:
                            down(n + (c - 2), c - 2, s, c - 2, c == 2, False, g * ROUNDS + r)
                        elif not (isinstance(n, int) and n == 0):
                            before = (1 - s) if isinstance(r, int) else s
                            down(n + (c - 2), CHUNKS - 2 + c, before, CHUNKS - 2 + c, False, c == 1, None)

                over_rounds(pe, g, round_)

            def tail():
                def tail_down(n):
                    if n < 0:
                        down(MAIN + n, CHUNKS + n, 1, CHUNKS + n, False, n == -1, None)
                    else:
                        down(MAIN + n, n % CHUNKS, (n // ROUNDS) % 2, 0, True, True, NE * ROUNDS + n)

                for i, n, q, s, col in steps_of_tail():
                    if i % ROUNDS == 0:
                        pe.wait_ge(weights_ready, NE + i // ROUNDS)
                    up(n, q, s, 0, col)
                    tail_down(i - 2)
                tail_down(TAIL - 2)
                tail_down(TAIL - 1)

            over_groups(pe, group, tail)

        @block.vector
        def _(dve):
            def add(rounds, col):
                dve.wait_ge(round_done, rounds + 1)
                for k in range(K2):
                    place = acc_T[:, k, bass.ds(col, TOKENS)]
                    ins = nc.vector.tensor_tensor(place, place, psum_o[k][:, 0:TOKENS], ALU.add)
                ins.then_inc(acc_added, 1)

            def lo(n, q):
                dve.wait_ge(hi_done, n + 1)
                nc.vector.tensor_tensor(hid_lo[:, q, :], hidden[:, q % 3, :], hid_hi[:, q, :].bitcast(F32), ALU.subtract).then_inc(lo_done, 1)

            def step(n, q, s, col):
                here = hidden[:, q % 3, :]
                dve.wait_ge(silu_done, n + 1)
                dve.wait_ge(three_done, n + 1)
                nc.vector.tensor_tensor(here, here, psum_3[q % 3][:, 0:TOKENS], ALU.mult).then_inc(multiplied, 1)
                dve.wait_ge(multiplied, n + 1)
                nc.vector.tensor_tensor(here, here, gate[:, s, bass.ds(col, TOKENS)], ALU.mult).then_inc(gated, 1)
                if not (isinstance(n, int) and n == 0):
                    lo(n - 1, (q - 1) % CHUNKS)

            def group(g, s, uses):
                dve.wait_ge(gates_loaded[s], uses * 16 + 16)

                def round_(g, n, col, r):
                    for c in range(CHUNKS):
                        if c == 2 and not (isinstance(n, int) and n == 0):
                            if isinstance(r, int):
                                add(g * ROUNDS - 1, NODES - TOKENS)
                            else:
                                add(g * ROUNDS + r - 1, col - TOKENS)
                        step(n + c, c, s, col)

                over_rounds(dve, g, round_)

            def tail():
                for i, n, q, s, col in steps_of_tail():
                    if i % ROUNDS == 0:
                        dve.wait_ge(gates_loaded[s], 16 * (NE // 2) + 16 * REST_SHARE * (i // ROUNDS // 2 + 1))
                    if i == 2:
                        add(NE * ROUNDS - 1, NODES - TOKENS)
                    if i >= 3:
                        add(NE * ROUNDS + i - 3, (i - 3) % ROUNDS * TOKENS)
                    step(n, q, s, col)
                lo(MAIN + TAIL - 1, CHUNKS - 1)
                for i in range(TAIL - 3, TAIL):
                    add(NE * ROUNDS + i, i % ROUNDS * TOKENS)

            dve.wait_ge(first_hi_ready, 1)
            nc.vector.tensor_tensor(up_lo[0][:, :, :, :], raw_up[:, :, :, :], up_hi[0][:, :, :, :].bitcast(F32), ALU.subtract).then_inc(first_ready, 1)
            dve.wait_ge(first_hi_ready, 2)
            nc.vector.tensor_tensor(down_lo[0][:, :, :], raw_down[:, :, :], down_hi[0][:, :, :].bitcast(F32), ALU.subtract).then_inc(first_ready, 1)
            nc.vector.memset(acc_T[:, :, :], 0.0).then_inc(acc_zero, 1)
            dve.wait_ge(acc_zero, 1)
            over_groups(dve, group, tail)


def stage_output(nc, t, keep, out):
    with ExitStack() as ctx:
        m = Memory(nc, ctx, "output")
        residual, const, acc_T = keep["residual"], keep["const"], keep["acc_T"]
        part = [m.sb(f"part{s}", [P, K2, P]) for s in range(2)]
        rows = m.sb("rows", [P, 2, C])
        psum = [m.ps(f"turned{s}") for s in range(2)]
        part_ready, turned, rows_ready = m.sem("part_ready"), m.sem("turned"), m.sem("rows_ready")
        stored = [m.sem(f"stored{s}") for s in range(2)]
        block = ctx.enter_context(nc.Block())
        PAIRS = TILES // 2 - 1

        def over(eng, tile):
            tile(0, 0, 0, P)
            tile(1, 1, 0, P)
            with eng.Fori(1, PAIRS) as i:
                tile(i * 2, 0, i, P)
                tile(i * 2 + 1, 1, i, P)
            tile(TILES - 2, 0, PAIRS, P)
            tile(TILES - 1, 1, PAIRS, LAST)

        def opens(n):
            return isinstance(n, int) and n < 2

        @block.scalar
        def _(act):
            def tile(n, s, use, tall):
                if not opens(n):
                    act.wait_ge(turned, n - 1)
                nc.scalar.activation(part[s][:, :, 0:tall], acc_T[:, :, bass.ds(n * P, tall)], ACT.Copy).then_inc(part_ready, 1)

            over(act, tile)

        @block.tensor
        def _(pe):
            def tile(n, s, use, tall):
                pe.wait_ge(part_ready, n + 1)
                if not opens(n):
                    pe.wait_ge(rows_ready, n - 1)
                for k in range(K2):
                    ins = nc.tensor.transpose(psum[s][0:tall, k * P:(k + 1) * P], part[s][:, k, 0:tall], const[:, IDENT:IDENT + P])
                ins.then_inc(turned, 1)

            over(pe, tile)

        @block.vector
        def _(dve):
            def tile(n, s, use, tall):
                dve.wait_ge(turned, n + 1)
                if not opens(n):
                    dve.wait_ge(stored[s], use * 16)
                nc.vector.tensor_tensor(rows[0:tall, s, :], residual[0:tall, bass.ds(n, 1), :].rearrange("p a c -> p (a c)"), psum[s][0:tall, 0:C],
                                        ALU.add).then_inc(rows_ready, 1)

            over(dve, tile)

        @block.sync
        def _(sp):
            def tile(n, s, use, tall):
                sp.wait_ge(rows_ready, n + 1)
                sp.dma_start(out[bass.ds(n * P, tall), :], rows[0:tall, s, :]).then_inc(stored[s], 16)

            over(sp, tile)
            for s in range(2):
                sp.wait_ge(stored[s], 16 * (TILES // 2))


def program(nc, t, out):
    with ExitStack() as ctx:
        m = Memory(nc, ctx, "kept")
        keep = {"residual": m.sb("residual", [P, TILES, C]), "const": m.sb("const", [P, CONSTANTS]),
                "q_all": m.sb("q_all", [P, TILES, C]),
                "h_rows": nc.dram_tensor("h_rows", (PADDED, H_COLS), F32, kind="Internal").ap(),
                "tokens_hi": nc.dram_tensor("tokens_hi", (P, K2, PADDED), F32, kind="Internal").ap(),
                "tokens_lo": nc.dram_tensor("tokens_lo", (P, K2, PADDED), F32, kind="Internal").ap(),
                "row_numbers": nc.dram_tensor("row_numbers", (P, COLUMNS), I32, kind="Internal").ap(),
                "gate_rows": nc.dram_tensor("gate_rows", (NE, PADDED), F32, kind="Internal").ap()}
        keep["h_table"] = keep["h_rows"].rearrange("n (r c) -> (n r) c", r=RELS)
        keep["z"] = keep["q_all"]
        with ExitStack() as nodes:
            m = Memory(nc, nodes, "nodes")
            keep.update(context=m.sb("context", [P, K2, P + 4]), agg_T=m.sb("agg_T", [P, K2, PADDED + WINDOW]), in_window=m.sb("in_window", [P, COLUMNS]),
                        base=m.sb("base", [P, GROUPS], I32), window_iota=m.sb("window_iota", [P, WINDOW]), flag=m.sb("flag", [P, 1], I32))
            stage_projections(nc, t, keep)
            keep.update(rows=m.sb("rows", [P, RING, GROUP, C]), slots=[m.sb(f"slot{s}", [P, GROUP], I32) for s in range(RING)])
            stage_scattered(nc, t, keep)
            stage_spans(nc, t, keep)
        with ExitStack() as inner:
            m = Memory(nc, inner, "tokens")
            keep.update(h_hi=m.sb("h_hi", [P, K2, NODES], F32R), h_lo=m.sb("h_lo", [P, K2, NODES], F32R))
            keep["acc_T"] = keep["z"][:, :, :].rearrange("p t c -> p (t c)")[:, 0:K2 * NODES].rearrange("p (k n) -> p k n", k=K2)
            stage_experts(nc, t, keep)
            stage_output(nc, t, keep, out)


def attention_arrays(a):
    half = HD // 2
    wq, wk = a["L0_ffn_wq"].reshape(NH, HD, C), a["L0_ffn_wk"].reshape(NKV, HD, C)

    def with_rotated(w):
        return np.concatenate([w, w[:, half:], w[:, :half]], axis=1).transpose(0, 2, 1)

    w1, w3, w2 = (w.transpose(0, 2, 1) for w in (a["L0_ffn_w1"], a["L0_ffn_w3"], a["L0_ffn_w2"]))
    up = np.stack([w1, w3], axis=1)
    whole = CHUNKS * P
    rest_up = np.zeros((REST_GROUPS, 2, C, P), up.dtype)
    rest_down = np.zeros((REST_GROUPS, P, C), w2.dtype)
    for e in range(NE):
        j, at = e // REST_SHARE, e % REST_SHARE * REST
        rest_up[j, :, :, at:at + REST] = up[e, :, :, whole:]
        rest_down[j, at:at + REST] = w2[e, whole:]
    return {
        "up_T": up[..., :whole],
        "down_T": w2[:, :whole],
        "rest_up_T": rest_up,
        "rest_down_T": rest_down,
        "wv_T": a["L0_ffn_wv"].T,
        "wqk_T": np.concatenate([np.concatenate([with_rotated(wk[g:g + 1]), with_rotated(wq[g * NH // NKV:(g + 1) * NH // NKV])]) for g in range(NKV)]),
        "wo_T": a["L0_ffn_wo"].T.reshape(NH, HD, C),
        "router_T": a["L0_ffn_router_w"].T,
        "ln1_w": a["L0_ffn_ln1_w"].reshape(K2, P).T,
        "ln2_w": a["L0_ffn_ln2_w"].reshape(K2, P).T,
        "rope": rope_table(),
    }


def kernel(**inputs):
    import concourse.bacc as bacc
    from concourse.bass_utils import run_bass_kernel_spmd as run

    a = {name: np.asarray(v) for name, v in inputs.items()}
    arrays = {
        "x": a["x"],
        "src_T": a["src"].reshape(COLUMNS, P).T,
        "dst_T": a["dst"].reshape(COLUMNS, P).T,
        "first_targets": a["dst"].reshape(GROUPS, GROUP * P)[:, 0],
        "type_T": a["edge_type_8"].reshape(COLUMNS, P).T,
        "basis": a["L0_gnn_basis"],
        "comp": a["L0_gnn_comp"],
        "dense_T": np.concatenate([a["L0_mix_Wkv"].T, a["L0_mix_Wq"].T, a["L0_gnn_loop_weight"]], axis=1),
        "biases": np.stack([a["L0_gnn_bias_param"], a["L0_mix_bproj"]]),
        "proj_T": a["L0_mix_Wproj"].T,
        "constants": constants(),
    }
    arrays.update(attention_arrays(a))
    arrays = {name: np.ascontiguousarray(v) for name, v in arrays.items()}
    nc = bacc.Bacc("TRN2", target_bir_lowering=False, num_devices=1)
    t = {name: nc.dram_tensor(name, v.shape, mybir.dt.from_np(v.dtype), kind="ExternalInput").ap() for name, v in arrays.items()}
    out = nc.dram_tensor("out", (NODES, C), F32, kind="ExternalOutput").ap()
    program(nc, t, out)
    return run(nc, [arrays], core_ids=[0]).results[0]["out"]
```
